# Optimizing a Trainium2 kernel written in Bass

```python
import numpy as np
import jax
import jax.numpy as jnp

def _softmax(x, axis=-1):
    return jax.nn.softmax(x, axis=axis)

def _gelu(x):
    return jax.nn.gelu(x, approximate=True)

def _silu(x):
    return jax.nn.silu(x)

def _sigmoid(x):
    return jax.nn.sigmoid(x)

def _layernorm(x, axis=-1, eps=1e-05):
    m = jnp.mean(x, axis=axis, keepdims=True)
    v = jnp.var(x, axis=axis, keepdims=True)
    return (x - m) / jnp.sqrt(v + eps)

def _scatter_add(tgt, idx, src, axis=0):
    return tgt.at[idx].add(src)

def _segment_sum(src, seg, n):
    return jax.ops.segment_sum(src, seg, n)
kernel_name = 'mk_decoder_preln_d2_seqx_r4_d044cf'

def setup_inputs(seed: int=0):
    np.random.seed(seed)
    _w = jnp.asarray

    def _rec_inputs():
        import jax
        import jax.numpy as jnp
        _rk = jax.random.key(seed)
        x = 7.22e-05 + 1 * jax.random.normal(jax.random.fold_in(_rk, 1), (8, 112, 256), jnp.float32)
        _lenS = 112 - jax.random.randint(jax.random.fold_in(_rk, 7), (8,), 0, max(1, 112 // 4) + 1, jnp.int32)
        _lenS2 = 375 - jax.random.randint(jax.random.fold_in(_rk, 8), (8,), 0, max(1, 375 // 4) + 1, jnp.int32)
        _ctx_1024P = jax.random.normal(jax.random.fold_in(_rk, 11), (8, 16, 256), jnp.float32)
        _ctx_1024c = jax.random.dirichlet(jax.random.fold_in(_rk, 511), 0.3 * jnp.ones((16,), jnp.float32), (8, 375))
        _ctx_1024t = jnp.einsum('bsk,bkd->bsd', _ctx_1024c, _ctx_1024P)
        _ctx_1024t = _ctx_1024t * jax.lax.rsqrt(jnp.mean(jnp.square(_ctx_1024t)) + 1e-12) * 0.953939
        ctx_1024 = 4.13588e-05 + 0.999923 * (_ctx_1024t + 0.3 * jax.random.normal(jax.random.fold_in(_rk, 611), (8, 375, 256), jnp.float32))
        _validS = jnp.arange(112)[None, :] < _lenS[:, None]
        _validS2 = jnp.arange(375)[None, :] < _lenS2[:, None]
        _causal = jnp.tril(jnp.ones((112, 112), dtype=bool))
        mask_BxSxS2_ff0 = jnp.where(jnp.ones((8, 112, 375), dtype=bool), 0.0, -1000000000.0).astype(jnp.float32)
        return (x, ctx_1024, mask_BxSxS2_ff0)
    x, ctx_1024, mask_BxSxS2_ff0 = _rec_inputs()

    def _L0_attn_setup():
        import jax, jax.numpy as jnp
        import numpy as np
        B, S, DM = (2, 512, 256)
        H, D = (16, 64)

        def _rel_pos_enc(seq_len: int, dim: int) -> jnp.ndarray:
            positions = jnp.arange(seq_len, dtype=jnp.float32)[:, None]
            div_term = jnp.exp(jnp.arange(0, dim, 2, dtype=jnp.float32) * -(np.log(10000.0) / dim))
            pe = jnp.zeros((seq_len, dim), dtype=jnp.float32)
            pe = pe.at[:, 0::2].set(jnp.sin(positions * div_term))
            pe = pe.at[:, 1::2].set(jnp.cos(positions * div_term))
            return pe
        key = jax.random.key(seed)
        k1, k2, k3 = jax.random.split(key, 3)
        x = jax.random.normal(k1, (B, S, DM), dtype=jnp.float32)
        W_qkv = jax.random.normal(k2, (DM, 3 * H * D), dtype=jnp.float32) / np.sqrt(DM)
        b_qkv = jnp.zeros((3 * H * D,), dtype=jnp.float32)
        W_out = jax.random.normal(k3, (H * D, DM), dtype=jnp.float32) / np.sqrt(H * D)
        b_out = jnp.zeros((DM,), dtype=jnp.float32)
        return {'x': x, 'W_qkv': W_qkv, 'b_qkv': b_qkv, 'W_out': W_out, 'b_out': b_out}
    _L0_attn_all = _L0_attn_setup()
    _L0_attn_in = {k: v for k, v in _L0_attn_all.items() if k in ('W_qkv', 'b_qkv', 'W_out', 'b_out')}
    del _L0_attn_all

    def _L0_xattn_setup():
        import jax, jax.numpy as jnp
        import numpy as np
        DIM = 256
        HEADS = 16
        DIM_HEAD = 64
        INNER = HEADS * DIM_HEAD
        MLP = 1024
        EPS = 1e-05

        def _layernorm(x, g, b):
            mu = jnp.mean(x, axis=-1, keepdims=True)
            var = jnp.mean(jnp.square(x - mu), axis=-1, keepdims=True)
            return (x - mu) * jax.lax.rsqrt(var + EPS) * g + b

        def _l2norm(x):
            n = jnp.sqrt(jnp.sum(jnp.square(x), axis=-1, keepdims=True))
            return x / jnp.maximum(n, 1e-12)

        def _split_heads(x, B, N):
            return x.reshape(B, N, HEADS, DIM_HEAD).transpose(0, 2, 1, 3)
        key = jax.random.key(seed)
        ks = jax.random.split(key, 16)
        B, N = (4, 512)
        s = 0.02
        return {'Q': jax.random.normal(ks[0], (B, N, DIM), jnp.float32), 'K': jax.random.normal(ks[1], (B, N, DIM), jnp.float32), 'V': jax.random.normal(ks[2], (B, N, DIM), jnp.float32), 'wq': jax.random.normal(ks[3], (DIM, INNER), jnp.float32) * s, 'wk': jax.random.normal(ks[4], (DIM, INNER), jnp.float32) * s, 'wv': jax.random.normal(ks[5], (DIM, INNER), jnp.float32) * s, 'wo': jax.random.normal(ks[6], (INNER, DIM), jnp.float32) * s, 'bo': jnp.zeros((DIM,), jnp.float32), 'w1': jax.random.normal(ks[7], (DIM, MLP), jnp.float32) * s, 'b1': jnp.zeros((MLP,), jnp.float32), 'w2': jax.random.normal(ks[8], (MLP, DIM), jnp.float32) * s, 'b2': jnp.zeros((DIM,), jnp.float32), 'ln1_g': jnp.ones((DIM,), jnp.float32), 'ln1_b': jnp.zeros((DIM,), jnp.float32), 'ln2_g': jnp.ones((DIM,), jnp.float32), 'ln2_b': jnp.zeros((DIM,), jnp.float32)}
    _L0_xattn_all = _L0_xattn_setup()
    _L0_xattn_in = {k: v for k, v in _L0_xattn_all.items() if k in ('wq', 'wk', 'wv', 'wo', 'bo', 'w1', 'b1', 'w2', 'b2', 'ln1_g', 'ln1_b', 'ln2_g', 'ln2_b')}
    del _L0_xattn_all

    def _L0_ffn_setup():
        import jax, jax.numpy as jnp
        import numpy as np
        H = 256
        M = 128
        E = 16
        TOP_K = 4
        N_GROUP = 4
        TOPK_GROUP = 2
        SCALE = 2.5
        B, S = (2, 256)

        def _gate(x2d, gate_kernel, gate_bias):
            n = x2d.shape[0]
            logits = jnp.dot(x2d.astype(jnp.float32), gate_kernel.astype(jnp.float32))
            scores = jax.nn.sigmoid(logits)
            scores_for_choice = scores + gate_bias
            group_scores = scores_for_choice.reshape(n, N_GROUP, E // N_GROUP)
            top2 = jax.lax.top_k(group_scores, k=2)[0]
            group_sum = jnp.sum(top2, axis=-1)
            group_idx = jax.lax.top_k(group_sum, k=TOPK_GROUP)[1]
            group_mask = jnp.zeros_like(group_sum).at[jnp.arange(n)[:, None], group_idx].set(1.0)
            score_mask = jnp.repeat(group_mask[:, :, None], E // N_GROUP, axis=2).reshape(n, E)
            masked_scores = jnp.where(score_mask > 0, scores_for_choice, 0.0)
            topk_weight, topk_idx = jax.lax.top_k(masked_scores, k=TOP_K)
            topk_weight = topk_weight / (jnp.sum(topk_weight, axis=-1, keepdims=True) + 1e-20)
            topk_weight = topk_weight * SCALE
            return (topk_idx, topk_weight)
        key = jax.random.key(seed)
        ks = jax.random.split(key, 9)
        sc_h = 1.0 / np.sqrt(H)
        sc_m = 1.0 / np.sqrt(M)
        return {'hidden_states': jax.random.normal(ks[0], (B, S, H), jnp.float32), 'gate_kernel': jax.random.normal(ks[1], (H, E), jnp.float32) * sc_h, 'gate_bias': jax.random.normal(ks[2], (E,), jnp.float32) * 0.01, 'w_gate': jax.random.normal(ks[3], (E, H, M), jnp.float32) * sc_h, 'w_up': jax.random.normal(ks[4], (E, H, M), jnp.float32) * sc_h, 'w_down': jax.random.normal(ks[5], (E, M, H), jnp.float32) * sc_m, 'sw_gate': jax.random.normal(ks[6], (H, 2 * M), jnp.float32) * sc_h, 'sw_up': jax.random.normal(ks[7], (H, 2 * M), jnp.float32) * sc_h, 'sw_down': jax.random.normal(ks[8], (2 * M, H), jnp.float32) * (1.0 / np.sqrt(2 * M))}
    _L0_ffn_all = _L0_ffn_setup()
    _L0_ffn_in = {k: v for k, v in _L0_ffn_all.items() if k in ('gate_kernel', 'gate_bias', 'w_gate', 'w_up', 'w_down', 'sw_gate', 'sw_up', 'sw_down')}
    del _L0_ffn_all

    def _L1_attn_setup():
        import jax, jax.numpy as jnp
        import numpy as np
        EPS = 1e-08

        def rms_norm_multihead(x, weight):
            x32 = x.astype(jnp.float32)
            normed = x32 * jax.lax.rsqrt(jnp.mean(x32 * x32, axis=-1, keepdims=True) + EPS)
            return normed.astype(x.dtype) * weight
        key = jax.random.key(seed)
        k0, k1, k2 = jax.random.split(key, 3)
        B, L, D, H = (2, 256, 256, 16)
        d = D // H
        X = jax.random.normal(k0, (B, L, D), dtype=jnp.float32)
        Wq = jax.random.normal(k1, (D, D), dtype=jnp.float32) * 0.02
        Wv = jax.random.normal(k2, (D, D), dtype=jnp.float32) * 0.02
        q_norm_w = jnp.ones((H, d), dtype=jnp.float32)
        v_norm_w = jnp.ones((H, d), dtype=jnp.float32)
        return {'X': X, 'Wq': Wq, 'Wv': Wv, 'q_norm_w': q_norm_w, 'v_norm_w': v_norm_w}
    _L1_attn_all = _L1_attn_setup()
    _L1_attn_in = {k: v for k, v in _L1_attn_all.items() if k in ('Wq', 'Wv', 'q_norm_w', 'v_norm_w')}
    del _L1_attn_all

    def _L1_xattn_setup():
        import jax, jax.numpy as jnp
        import numpy as np
        DIM = 256
        CTX_DIM = 256
        HEADS = 16
        DIM_HEAD = 64
        INNER = HEADS * DIM_HEAD
        FF_INNER = 4 * DIM
        EPS = 1e-05

        def layer_norm(x, g, b):
            mu = jnp.mean(x, axis=-1, keepdims=True)
            var = jnp.var(x, axis=-1, keepdims=True)
            return (x - mu) * jax.lax.rsqrt(var + EPS) * g + b
        key = jax.random.key(seed)
        ks = jax.random.split(key, 10)
        b, n, j = (2, 512, 512)
        x = jax.random.normal(ks[0], (b, n, DIM), dtype=jnp.float32)
        context = jax.random.normal(ks[1], (b, j, CTX_DIM), dtype=jnp.float32)
        mask = jnp.zeros((b, n, j), dtype=jnp.float32)
        s = 0.02
        Wq = jax.random.normal(ks[2], (DIM, INNER), dtype=jnp.float32) * s
        Wkv = jax.random.normal(ks[3], (CTX_DIM, 2 * DIM_HEAD), dtype=jnp.float32) * s
        Wout = jax.random.normal(ks[4], (INNER, DIM), dtype=jnp.float32) * s
        W1 = jax.random.normal(ks[5], (DIM, 2 * FF_INNER), dtype=jnp.float32) * s
        W2 = jax.random.normal(ks[6], (FF_INNER, DIM), dtype=jnp.float32) * s
        ln_g = jnp.ones((DIM,), jnp.float32)
        ln_b = jnp.zeros((DIM,), jnp.float32)
        cln_g = jnp.ones((CTX_DIM,), jnp.float32)
        cln_b = jnp.zeros((CTX_DIM,), jnp.float32)
        return {'x': x, 'context': context, 'mask': mask, 'ln_g': ln_g, 'ln_b': ln_b, 'cln_g': cln_g, 'cln_b': cln_b, 'Wq': Wq, 'Wkv': Wkv, 'Wout': Wout, 'W1': W1, 'W2': W2}
    _L1_xattn_all = _L1_xattn_setup()
    _L1_xattn_in = {k: v for k, v in _L1_xattn_all.items() if k in ('ln_g', 'ln_b', 'cln_g', 'cln_b', 'Wq', 'Wkv', 'Wout', 'W1', 'W2')}
    del _L1_xattn_all

    def _L1_ffn_setup():
        import jax, jax.numpy as jnp
        import numpy as np
        TOP_K = 2
        key = jax.random.key(seed)
        ks = jax.random.split(key, 8)
        B, S, D, E = (4, 512, 256, 8)
        H = 4 * D
        x = jax.random.normal(ks[0], (B, S, D), dtype=jnp.float32)
        W1 = jax.random.normal(ks[1], (E, D, H), dtype=jnp.float32) * np.sqrt(2.0 / (D + H))
        b1 = jax.random.normal(ks[2], (E, H), dtype=jnp.float32) * 1e-06
        W2 = jax.random.normal(ks[3], (E, H, D), dtype=jnp.float32) * np.sqrt(2.0 / (H + D))
        b2 = jax.random.normal(ks[4], (E, D), dtype=jnp.float32) * 1e-06
        gate_w = jax.random.normal(ks[5], (D, E), dtype=jnp.float32) * np.sqrt(1.0 / D)
        gate_b = jnp.zeros((E,), dtype=jnp.float32)
        temperature = jnp.asarray(1.0, dtype=jnp.float32)
        return {'x': x, 'W1': W1, 'b1': b1, 'W2': W2, 'b2': b2, 'gate_w': gate_w, 'gate_b': gate_b, 'temperature': temperature}
    _L1_ffn_all = _L1_ffn_setup()
    _L1_ffn_in = {k: v for k, v in _L1_ffn_all.items() if k in ('W1', 'b1', 'W2', 'b2', 'gate_w', 'gate_b', 'temperature')}
    del _L1_ffn_all
    return {'x': x, 'ctx_1024': ctx_1024, 'mask_BxSxS2_ff0': mask_BxSxS2_ff0, 'L0_attn_W_qkv': _L0_attn_in['W_qkv'], 'L0_attn_b_qkv': _L0_attn_in['b_qkv'], 'L0_attn_W_out': _L0_attn_in['W_out'], 'L0_attn_b_out': _L0_attn_in['b_out'], 'L0_xattn_wq': _L0_xattn_in['wq'], 'L0_xattn_wk': _L0_xattn_in['wk'], 'L0_xattn_wv': _L0_xattn_in['wv'], 'L0_xattn_wo': _L0_xattn_in['wo'], 'L0_xattn_bo': _L0_xattn_in['bo'], 'L0_xattn_w1': _L0_xattn_in['w1'], 'L0_xattn_b1': _L0_xattn_in['b1'], 'L0_xattn_w2': _L0_xattn_in['w2'], 'L0_xattn_b2': _L0_xattn_in['b2'], 'L0_xattn_ln1_g': _L0_xattn_in['ln1_g'], 'L0_xattn_ln1_b': _L0_xattn_in['ln1_b'], 'L0_xattn_ln2_g': _L0_xattn_in['ln2_g'], 'L0_xattn_ln2_b': _L0_xattn_in['ln2_b'], 'L0_ffn_gate_kernel': _L0_ffn_in['gate_kernel'], 'L0_ffn_gate_bias': _L0_ffn_in['gate_bias'], 'L0_ffn_w_gate': _L0_ffn_in['w_gate'], 'L0_ffn_w_up': _L0_ffn_in['w_up'], 'L0_ffn_w_down': _L0_ffn_in['w_down'], 'L0_ffn_sw_gate': _L0_ffn_in['sw_gate'], 'L0_ffn_sw_up': _L0_ffn_in['sw_up'], 'L0_ffn_sw_down': _L0_ffn_in['sw_down'], 'L1_attn_Wq': _L1_attn_in['Wq'], 'L1_attn_Wv': _L1_attn_in['Wv'], 'L1_attn_q_norm_w': _L1_attn_in['q_norm_w'], 'L1_attn_v_norm_w': _L1_attn_in['v_norm_w'], 'L1_xattn_ln_g': _L1_xattn_in['ln_g'], 'L1_xattn_ln_b': _L1_xattn_in['ln_b'], 'L1_xattn_cln_g': _L1_xattn_in['cln_g'], 'L1_xattn_cln_b': _L1_xattn_in['cln_b'], 'L1_xattn_Wq': _L1_xattn_in['Wq'], 'L1_xattn_Wkv': _L1_xattn_in['Wkv'], 'L1_xattn_Wout': _L1_xattn_in['Wout'], 'L1_xattn_W1': _L1_xattn_in['W1'], 'L1_xattn_W2': _L1_xattn_in['W2'], 'L1_ffn_W1': _L1_ffn_in['W1'], 'L1_ffn_b1': _L1_ffn_in['b1'], 'L1_ffn_W2': _L1_ffn_in['W2'], 'L1_ffn_b2': _L1_ffn_in['b2'], 'L1_ffn_gate_w': _L1_ffn_in['gate_w'], 'L1_ffn_gate_b': _L1_ffn_in['gate_b'], 'L1_ffn_temperature': _L1_ffn_in['temperature']}

def reference(x, ctx_1024, mask_BxSxS2_ff0, L0_attn_W_qkv, L0_attn_b_qkv, L0_attn_W_out, L0_attn_b_out, L0_xattn_wq, L0_xattn_wk, L0_xattn_wv, L0_xattn_wo, L0_xattn_bo, L0_xattn_w1, L0_xattn_b1, L0_xattn_w2, L0_xattn_b2, L0_xattn_ln1_g, L0_xattn_ln1_b, L0_xattn_ln2_g, L0_xattn_ln2_b, L0_ffn_gate_kernel, L0_ffn_gate_bias, L0_ffn_w_gate, L0_ffn_w_up, L0_ffn_w_down, L0_ffn_sw_gate, L0_ffn_sw_up, L0_ffn_sw_down, L1_attn_Wq, L1_attn_Wv, L1_attn_q_norm_w, L1_attn_v_norm_w, L1_xattn_ln_g, L1_xattn_ln_b, L1_xattn_cln_g, L1_xattn_cln_b, L1_xattn_Wq, L1_xattn_Wkv, L1_xattn_Wout, L1_xattn_W1, L1_xattn_W2, L1_ffn_W1, L1_ffn_b1, L1_ffn_W2, L1_ffn_b2, L1_ffn_gate_w, L1_ffn_gate_b, L1_ffn_temperature):
    import jax
    import jax.numpy as jnp

    def _L0_attn_ref(x, W_qkv, b_qkv, W_out, b_out):
        import jax, jax.numpy as jnp
        import numpy as np
        B, S, DM = (2, 512, 256)
        H, D = (16, 64)

        def _rel_pos_enc(seq_len: int, dim: int) -> jnp.ndarray:
            positions = jnp.arange(seq_len, dtype=jnp.float32)[:, None]
            div_term = jnp.exp(jnp.arange(0, dim, 2, dtype=jnp.float32) * -(np.log(10000.0) / dim))
            pe = jnp.zeros((seq_len, dim), dtype=jnp.float32)
            pe = pe.at[:, 0::2].set(jnp.sin(positions * div_term))
            pe = pe.at[:, 1::2].set(jnp.cos(positions * div_term))
            return pe
        b, s, _ = x.shape
        qkv = x @ W_qkv + b_qkv
        qkv = qkv.reshape(b, s, 3, H, D)
        q, k, v = (qkv[:, :, 0], qkv[:, :, 1], qkv[:, :, 2])
        pos_enc = _rel_pos_enc(s, D)
        k = k + pos_enc[None, :, None, :]
        scale = jnp.sqrt(jnp.asarray(D, dtype=x.dtype))
        scores = jnp.einsum('bqhd,bkhd->bhqk', q, k) / scale
        attn = jax.nn.softmax(scores, axis=-1)
        out = jnp.einsum('bhqk,bkhd->bqhd', attn, v)
        out = out.reshape(b, s, H * D)
        return out @ W_out + b_out

    def _L0_xattn_ref(Q, K, V, wq, wk, wv, wo, bo, w1, b1, w2, b2, ln1_g, ln1_b, ln2_g, ln2_b):
        import jax, jax.numpy as jnp
        import numpy as np
        DIM = 256
        HEADS = 16
        DIM_HEAD = 64
        INNER = HEADS * DIM_HEAD
        MLP = 1024
        EPS = 1e-05

        def _layernorm(x, g, b):
            mu = jnp.mean(x, axis=-1, keepdims=True)
            var = jnp.mean(jnp.square(x - mu), axis=-1, keepdims=True)
            return (x - mu) * jax.lax.rsqrt(var + EPS) * g + b

        def _l2norm(x):
            n = jnp.sqrt(jnp.sum(jnp.square(x), axis=-1, keepdims=True))
            return x / jnp.maximum(n, 1e-12)

        def _split_heads(x, B, N):
            return x.reshape(B, N, HEADS, DIM_HEAD).transpose(0, 2, 1, 3)
        B, Nq, _ = Q.shape
        Nk = K.shape[1]
        Qn = _layernorm(Q, ln1_g, ln1_b)
        Kn = _layernorm(K, ln1_g, ln1_b)
        Vn = _layernorm(V, ln1_g, ln1_b)
        q = _split_heads(Qn @ wq, B, Nq)
        k = _split_heads(Kn @ wk, B, Nk)
        v = _split_heads(Vn @ wv, B, Nk)
        qn = _l2norm(q)
        kn = _l2norm(k)
        attn = jnp.einsum('bhqd,bhkd->bhqk', qn, kn)
        out = jnp.einsum('bhqk,bhkd->bhqd', attn, v)
        out = out.transpose(0, 2, 1, 3).reshape(B, Nq, INNER)
        x = Q + out @ wo + bo
        xn = _layernorm(x, ln2_g, ln2_b)
        h = jax.nn.gelu(xn @ w1 + b1, approximate=False)
        return x + h @ w2 + b2

    def _L0_ffn_ref(hidden_states, gate_kernel, gate_bias, w_gate, w_up, w_down, sw_gate, sw_up, sw_down):
        import jax, jax.numpy as jnp
        import numpy as np
        H = 256
        M = 128
        E = 16
        TOP_K = 4
        N_GROUP = 4
        TOPK_GROUP = 2
        SCALE = 2.5
        B, S = (2, 256)

        def _gate(x2d, gate_kernel, gate_bias):
            n = x2d.shape[0]
            logits = jnp.dot(x2d.astype(jnp.float32), gate_kernel.astype(jnp.float32))
            scores = jax.nn.sigmoid(logits)
            scores_for_choice = scores + gate_bias
            group_scores = scores_for_choice.reshape(n, N_GROUP, E // N_GROUP)
            top2 = jax.lax.top_k(group_scores, k=2)[0]
            group_sum = jnp.sum(top2, axis=-1)
            group_idx = jax.lax.top_k(group_sum, k=TOPK_GROUP)[1]
            group_mask = jnp.zeros_like(group_sum).at[jnp.arange(n)[:, None], group_idx].set(1.0)
            score_mask = jnp.repeat(group_mask[:, :, None], E // N_GROUP, axis=2).reshape(n, E)
            masked_scores = jnp.where(score_mask > 0, scores_for_choice, 0.0)
            topk_weight, topk_idx = jax.lax.top_k(masked_scores, k=TOP_K)
            topk_weight = topk_weight / (jnp.sum(topk_weight, axis=-1, keepdims=True) + 1e-20)
            topk_weight = topk_weight * SCALE
            return (topk_idx, topk_weight)
        orig_shape = hidden_states.shape
        x = hidden_states.reshape(-1, orig_shape[-1])
        topk_idx, topk_weight = _gate(x, gate_kernel, gate_bias)
        onehot = (topk_idx[:, :, None] == jnp.arange(E)[None, None, :]).astype(topk_weight.dtype)
        combine = jnp.einsum('nke,nk->ne', onehot, topk_weight)
        g = jnp.einsum('nh,ehm->enm', x, w_gate)
        u = jnp.einsum('nh,ehm->enm', x, w_up)
        inter = jax.nn.silu(g) * u
        y_e = jnp.einsum('enm,emh->enh', inter, w_down)
        y = jnp.einsum('ne,enh->nh', combine, y_e)
        shared = jnp.dot(jax.nn.silu(jnp.dot(x, sw_gate)) * jnp.dot(x, sw_up), sw_down)
        return (y + shared).reshape(orig_shape)

    def _L1_attn_ref(X, Wq, Wv, q_norm_w, v_norm_w):
        import jax, jax.numpy as jnp
        import numpy as np
        EPS = 1e-08

        def rms_norm_multihead(x, weight):
            x32 = x.astype(jnp.float32)
            normed = x32 * jax.lax.rsqrt(jnp.mean(x32 * x32, axis=-1, keepdims=True) + EPS)
            return normed.astype(x.dtype) * weight
        B, L, D = X.shape
        H, d = q_norm_w.shape
        K = X.reshape(B, L, H, d)
        Q = rms_norm_multihead((X @ Wq.T).reshape(B, L, H, d), q_norm_w)
        V = rms_norm_multihead((X @ Wv.T).reshape(B, L, H, d), v_norm_w)
        W = jnp.cumsum(jnp.einsum('blhd,blhe->blhde', K, V), axis=1)
        out = jnp.einsum('blhd,blhde->blhe', Q, W).reshape(B, L, D)
        return out

    def _L1_xattn_ref(x, context, mask, ln_g, ln_b, cln_g, cln_b, Wq, Wkv, Wout, W1, W2):
        import jax, jax.numpy as jnp
        import numpy as np
        DIM = 256
        CTX_DIM = 256
        HEADS = 16
        DIM_HEAD = 64
        INNER = HEADS * DIM_HEAD
        FF_INNER = 4 * DIM
        EPS = 1e-05

        def layer_norm(x, g, b):
            mu = jnp.mean(x, axis=-1, keepdims=True)
            var = jnp.var(x, axis=-1, keepdims=True)
            return (x - mu) * jax.lax.rsqrt(var + EPS) * g + b
        scale = DIM_HEAD ** (-0.5)
        xn = layer_norm(x, ln_g, ln_b)
        cn = layer_norm(context, cln_g, cln_b)
        b, n, _ = xn.shape
        q = (xn @ Wq).reshape(b, n, HEADS, DIM_HEAD).transpose(0, 2, 1, 3) * scale
        kv = cn @ Wkv
        k, v = jnp.split(kv, 2, axis=-1)
        sim = jnp.einsum('bhid,bjd->bhij', q, k) + mask[:, None, :, :]
        attn = jax.nn.softmax(sim, axis=-1)
        out = jnp.einsum('bhij,bjd->bhid', attn, v)
        out = out.transpose(0, 2, 1, 3).reshape(b, n, INNER) @ Wout
        h = xn @ W1
        val, gate = jnp.split(h, 2, axis=-1)
        out = out + jax.nn.silu(gate) * val @ W2
        return out

    def _L1_ffn_ref(x, W1, b1, W2, b2, gate_w, gate_b, temperature):
        import jax, jax.numpy as jnp
        import numpy as np
        TOP_K = 2
        gates = (jnp.einsum('bsd,de->bse', x, gate_w) + gate_b) / temperature
        weights, indices = jax.lax.top_k(gates, TOP_K)
        weights = jax.nn.softmax(weights, axis=-1)
        h = jnp.einsum('bsd,edf->bsef', x, W1) + b1
        h = jax.nn.gelu(h, approximate=False)
        all_out = jnp.einsum('bsef,efd->bsed', h, W2) + b2
        expert_out = jnp.take_along_axis(all_out, indices[..., None], axis=2)
        out = jnp.sum(expert_out * weights[..., None], axis=2)
        return out
    x = x + _L0_attn_ref(_layernorm(x, axis=-1), L0_attn_W_qkv, L0_attn_b_qkv, L0_attn_W_out, L0_attn_b_out)
    x = x + _L0_xattn_ref(_layernorm(x, axis=-1), ctx_1024, ctx_1024, L0_xattn_wq, L0_xattn_wk, L0_xattn_wv, L0_xattn_wo, L0_xattn_bo, L0_xattn_w1, L0_xattn_b1, L0_xattn_w2, L0_xattn_b2, L0_xattn_ln1_g, L0_xattn_ln1_b, L0_xattn_ln2_g, L0_xattn_ln2_b)
    x = x + _L0_ffn_ref(_layernorm(x, axis=-1), L0_ffn_gate_kernel, L0_ffn_gate_bias, L0_ffn_w_gate, L0_ffn_w_up, L0_ffn_w_down, L0_ffn_sw_gate, L0_ffn_sw_up, L0_ffn_sw_down)
    x = x + _L1_attn_ref(_layernorm(x, axis=-1), L1_attn_Wq, L1_attn_Wv, L1_attn_q_norm_w, L1_attn_v_norm_w)
    x = x + _L1_xattn_ref(_layernorm(x, axis=-1), ctx_1024, mask_BxSxS2_ff0, L1_xattn_ln_g, L1_xattn_ln_b, L1_xattn_cln_g, L1_xattn_cln_b, L1_xattn_Wq, L1_xattn_Wkv, L1_xattn_Wout, L1_xattn_W1, L1_xattn_W2)
    x = x + _L1_ffn_ref(_layernorm(x, axis=-1), L1_ffn_W1, L1_ffn_b1, L1_ffn_W2, L1_ffn_b2, L1_ffn_gate_w, L1_ffn_gate_b, L1_ffn_temperature)
    return x

_drawn_inputs = setup_inputs


def setup_inputs(seed=0):
    import zlib

    import numpy as np

    out = dict(_drawn_inputs(seed))
    spreads = {'L0_attn_b_qkv': (0.0, 0.1),
     'L0_attn_b_out': (0.0, 0.1),
     'L0_xattn_bo': (0.0, 0.1),
     'L0_xattn_b1': (0.0, 0.1),
     'L0_xattn_b2': (0.0, 0.1),
     'L0_xattn_ln1_g': (1.0, 0.2),
     'L0_xattn_ln1_b': (0.0, 0.1),
     'L0_xattn_ln2_g': (1.0, 0.6),
     'L0_xattn_ln2_b': (0.0, 0.531),
     'L1_attn_q_norm_w': (1.0, 0.2),
     'L1_attn_v_norm_w': (1.0, 0.2),
     'L1_xattn_ln_g': (1.0, 0.6),
     'L1_xattn_ln_b': (0.0, 0.8),
     'L1_xattn_cln_g': (1.0, 0.6),
     'L1_xattn_cln_b': (0.0, 0.8),
     'L1_ffn_gate_b': (0.0, 0.8)}
    factors = {'L1_xattn_Wq': 8.0,
     'L1_xattn_Wkv': 8.0,
     'L1_xattn_Wout': 8.0,
     'L1_xattn_W1': 8.0,
     'L1_xattn_W2': 8.0,
     'L1_ffn_W1': 8.0,
     'L1_ffn_b1': 8.0,
     'L1_ffn_W2': 8.0,
     'L1_ffn_b2': 8.0,
     'L1_ffn_gate_w': 8.0}
    for name, (base, spread) in spreads.items():
        noise = np.random.default_rng([zlib.crc32(name.encode()), seed]).standard_normal(out[name].shape)
        drawn = base * np.exp(spread * noise) if base else spread * noise
        out[name] = jnp.asarray(drawn.astype(out[name].dtype))
    for name, factor in factors.items():
        out[name] = (out[name] * factor).astype(out[name].dtype)
    return out
```

```python
from contextlib import ExitStack

import numpy as np

import concourse.bass as bass
from concourse import mybir

F32 = mybir.dt.float32
F32R = mybir.dt.float32r
ALU = mybir.AluOpType
ACT = mybir.ActivationFunctionType
AX = mybir.AxisListType.X

P = 128
B, S, D = 8, 112, 256
N = B * S
NT = N // P
HALF = N // 2
KT = D // P
S2 = 375
CH, CP = 3, 125
H, DH = 16, 64
HP = H // 2
INNER = H * DH
EPS = 1e-5


def tile(t):
    return slice(t * P, (t + 1) * P)


class Chain:

    def __init__(self, eng, sem):
        self.eng, self.sem, self.n, self.off = eng, sem, 0, 0

    def link(self, ins):
        self.n += 1
        ins.then_inc(self.sem, 1)
        self.eng.wait_ge(self.sem, self.off + self.n)

    def enter(self, i, per):
        self.n0, self.per, self.off = self.n, per, i * per

    def leave(self, count):
        assert self.n - self.n0 == self.per, (self.n - self.n0, self.per)
        self.n, self.off = self.n0 + self.per * count, 0


class Stage:

    def __init__(self, nc, name):
        self.nc, self.name, self.ctx, self.sems = nc, name, ExitStack(), []

    def __enter__(self):
        self.ctx.__enter__()
        return self

    def __exit__(self, *a):
        if self.sems and a[0] is None:
            self.nc.clear_and_free_semaphores(self.sems)
            self.nc.all_engine_barrier()
        return self.ctx.__exit__(*a)

    def sb(self, name, shape, dt=F32):
        return self.ctx.enter_context(self.nc.sbuf_tensor(f"{self.name}_{name}", shape, dt))

    def pair(self, name, shape):
        return (self.sb(name + "_hi", shape, F32R), self.sb(name + "_lo", shape, F32R))

    def sem(self, name):
        self.sems.append(self.nc.alloc_semaphore(name=f"{self.name}_{name}"))
        return self.sems[-1]

    def sems_of(self, *names, prefix="", **more):
        return {n: self.sem(prefix + n) for n in names} | more

    def block(self):
        return self.nc.Block()


def cut(pair, *index):
    return tuple(x[index] for x in pair)


class Kernel:
    def __init__(self, nc, a, stop):
        self.nc, self.a, self.stop = nc, a, stop

    def mm(self, out, left, right, start, stop):
        te = self.nc.tensor
        if isinstance(left, tuple):
            (lh, ll), (rh, rl) = left, right
            te.matmul(out, lh, rh, start=start, stop=False)
            te.matmul(out, lh, rl, start=False, stop=False)
            return te.matmul(out, ll, rh, start=False, stop=stop)
        return te.matmul(out, left, right, start=start, stop=stop)

    def ln_buffers(self, st, name="ln"):
        return st.sems_of("chain", "var_ready", "std_ready", "norm_ready", "turned", "hi_ready", "lo_ready", "affine_ready", prefix=name + "_",
                          stats=st.sb(name + "_stats", [P, NT, 6]), mv=st.sb(name + "_mv", [P, NT, 2]),
                          std=st.sb(name + "_std", [P, NT]), rstd=st.sb(name + "_rstd", [P, NT]))

    def ln_vector(self, dve, o, x, xn, after=None):
        nc = self.nc
        o["c"] = Chain(dve, o["chain"])
        for t in range(NT):
            if after:
                after(t)
            last = nc.vector.bn_stats(o["stats"][:, t, :], x[:, t, :])
        o["c"].link(last)
        for t in range(NT):
            last = nc.vector.bn_aggr(o["mv"][:, t, :], o["stats"][:, t, :])
        o["c"].link(last)
        nc.vector.tensor_scalar(o["std"][:, :], o["mv"][:, :, 1], EPS, None, ALU.add).then_inc(o["var_ready"], 1)
        dve.wait_ge(o["std_ready"], 1)
        o["c"].link(nc.vector.reciprocal(o["rstd"][:, :], o["std"][:, :]))
        for t in range(NT):
            nc.vector.tensor_scalar(xn[:, t, :], x[:, t, :], o["mv"][:, t, 0:1], o["rstd"][:, t:t + 1],
                                    ALU.subtract, ALU.mult).then_inc(o["norm_ready"], 1)

    def ln_scalar_sqrt(self, act, o):
        act.wait_ge(o["var_ready"], 1)
        self.nc.scalar.activation(o["std"][:, :], o["std"][:, :], ACT.Sqrt).then_inc(o["std_ready"], 1)

    def turn_tensor(self, pe, o, xn):
        pe.wait_ge(self.ident_ready, 2)
        for g in range(2):
            for t in range(4 * g, min(4 * g + 4, NT)):
                pe.wait_ge(o["norm_ready"], t + 1)
                for k in range(KT):
                    last = self.nc.tensor.transpose(self.ps[2 * k + g][:, tile(t % 4)], xn[:, t, tile(k)], self.ident[:, :])
            last.then_inc(o["turned"], 1)

    def turn_pieces(self):
        for g in range(2):
            cols = slice(512 * g, min(512 * g + 512, N))
            for k in range(KT):
                yield g, k, cols, self.ps[2 * k + g][:, 0:cols.stop - cols.start]

    def split_scalar(self, act, o, xT, plain=None):
        for n, (g, k, cols, src) in enumerate(self.turn_pieces()):
            if plain is None:
                act.wait_ge(o["turned"], g + 1)
            else:
                act.wait_ge(o["affine_ready"], n + 1)
                src = plain[:, k, cols]
            self.nc.scalar.activation(xT[0][:, k, cols], src, ACT.Copy).then_inc(o["hi_ready"], 1)

    def split_vector(self, dve, o, xT, plain=None, gain=None, shift=None):
        nc = self.nc
        if plain is not None:
            for n, (g, k, cols, src) in enumerate(self.turn_pieces()):
                dve.wait_ge(o["turned"], g + 1)
                nc.vector.tensor_scalar(plain[:, k, cols], src, gain[:, k:k + 1], shift[:, k:k + 1],
                                        ALU.mult, ALU.add).then_inc(o["affine_ready"], 1)
        for n, (g, k, cols, src) in enumerate(self.turn_pieces()):
            dve.wait_ge(o["hi_ready"], n + 1)
            if plain is not None:
                dve.wait_ge(o["affine_ready"], n + 1)
                src = plain[:, k, cols]
            nc.vector.tensor_tensor(xT[1][:, k, cols], src, xT[0][:, k, cols].bitcast(F32),
                                    ALU.subtract).then_inc(o["lo_ready"], 1)

    def split_pool(self, pool, ready, raw, pair, index):
        nc = self.nc
        nc.gpsimd.tensor_copy(pair[0], raw).then_inc(ready, 1)
        pool.wait_ge(ready, 2 * index + 1)
        nc.gpsimd.tensor_tensor(pair[1], raw, pair[0].bitcast(F32), ALU.subtract).then_inc(ready, 1)

    def build(self):
        nc = self.nc
        with Stage(nc, "g") as g:
            self.ps = [g.ctx.enter_context(nc.psum_tensor(f"bank{i}", [P, 512], F32)) for i in range(8)]
            self.X = g.sb("x", [P, NT, D])
            self.ident = g.sb("ident", [P, P])
            self.k1T = g.sb("k1T", [P, B * S2])
            self.v1 = g.sb("v1", [CP, B * CH, DH])
            self.ident_ready = g.sem("ident_ready")
            self.x_loaded = g.sem("x_loaded")
            self.stored = g.sem("stored")
            self.prepare()
            with Stage(nc, "n0") as ahead:
                self.ahead_buffers(ahead)
                self.l0_attention()
                if self.stop > 1:
                    self.l0_cross_attention()
            if self.stop > 2:
                self.l0_experts()
            if self.stop > 3:
                with Stage(nc, "n1") as ahead:
                    self.ahead_buffers(ahead)
                    self.l1_attention()
                    if self.stop > 4:
                        self.l1_cross_attention()
            if self.stop > 5:
                self.l1_experts()
            self.finish()

    def ahead_buffers(self, st):
        self.ahead_raw = st.sb("raw", [P, 2 * INNER])
        self.ahead = st.pair("w", [P, 2 * INNER])

    def ahead_load(self, sp, s, src):
        sp.dma_start(self.ahead_raw[:, :], src).then_inc(s["ahead_loaded"], 16)

    def ahead_split(self, pool, s):
        pool.wait_ge(s["ahead_loaded"], 16)
        self.split_pool(pool, s["ahead_split"], self.ahead_raw[:, :], cut(self.ahead, slice(None)), 0)

    def ahead_as(self, **dims):
        return tuple(x[:, :].rearrange("p (a b) -> p a b", **dims) for x in self.ahead)

    def prepare(self):
        nc = self.nc
        with nc.Block() as block:
            @block.sync
            def _(sp):
                sp.dma_start(self.X[:, :, :], self.a["x"].rearrange("(t p) f -> p t f", p=P)).then_inc(self.x_loaded, 16)

            @block.gpsimd
            def _(pool):
                nc.gpsimd.memset(self.ident[:, :], 0.0).then_inc(self.ident_ready, 1)
                pool.wait_ge(self.ident_ready, 1)
                nc.gpsimd.affine_select(out=self.ident[:, :], in_=self.ident[:, :], compare_op=ALU.not_equal, fill=1.0,
                                        base=0, pattern=[[-1, P]], channel_multiplier=1).then_inc(self.ident_ready, 1)

    def finish(self):
        nc = self.nc
        with nc.Block() as block:
            @block.sync
            def _(sp):
                sp.wait_ge(self.x_loaded, 16)
                sp.dma_start(self.a["out"].rearrange("(t p) f -> p t f", p=P), self.X[:, :, :]).then_inc(self.stored, 16)
                sp.wait_ge(self.stored, 16)

    def l0_attention(self):
        nc, a, ps, X = self.nc, self.a, self.ps, self.X
        G = 4
        W = 3 * D
        with Stage(nc, "a") as st:
            xT = st.pair("xT", [P, KT, N])
            raw = st.sb("raw", [P, W + 2])
            w = st.pair("w", [P, W])
            bias = st.sb("bias", [P, 2])
            pos = st.sb("pos", [P, S])
            vb = st.sb("vb", [S, HP, P])
            woraw = st.sb("woraw", [P, HP, D])
            wo = st.pair("wo", [P, HP, D])
            bo = st.sb("bo", [P, D])
            oT = st.pair("oT", [P, HP, N])
            qT = st.sb("qT", [P, N])
            kz = st.sb("kz", [P, 2, N])
            v = st.sb("v", [S, B, P])
            prob = st.sb("prob", [S, G, 4, S])
            probT = st.sb("probT", [S, G, 4, S])
            mx = st.sb("mx", [S, G, 4])
            rs = st.sb("rs", [S, G, 4])
            xn = st.sb("xn", [P, NT, D])
            ln = self.ln_buffers(st)
            s = st.sems_of(
                "w_loaded", "const_loaded", "wo_loaded", "split_begun", "w_split", "bias_kept", "wo_split", "kz_cleared", "qk_ready", "v_ready",
                "s_ready", "q_kept", "k_kept", "v_kept", "shifted", "exps", "rsum", "norm", "p_turned", "pT_kept",
                "pv_ready", "o_hi", "o_lo", "dchain", "y_ready", "x_added",
                "ahead_loaded", "ahead_split")

            def q_w(pair, k):
                return cut(pair, slice(None), slice(k * 384, k * 384 + 128))

            def k_w(pair, k):
                return cut(pair, slice(None), slice(k * 384 + 128, k * 384 + 256))

            def v_w(pair, k):
                return cut(pair, slice(None), slice(k * 384 + 256, k * 384 + 384))

            with st.block() as block:
                @block.sync
                def _(sp):
                    sp.dma_start(raw[:, :], a["L0_qkv"][0]).then_inc(s["w_loaded"], 16)
                    sp.dma_start(pos[:, :], a["pos"]).then_inc(s["const_loaded"], 16)
                    sp.dma_start(vb[:, :, :], a["L0_bv"].partition_broadcast(S)).then_inc(s["const_loaded"], 16)
                    sp.dma_start(bo[:, :], a["L0_attn_b_out"].partition_broadcast(P)).then_inc(s["const_loaded"], 16)
                    sp.dma_start(woraw[:, :, :], a["L0_wo"]).then_inc(s["wo_loaded"], 16)
                    self.ahead_load(sp, s, a["L0_wq"].rearrange("p k n -> p (k n)"))
                    with sp.Fori(0, HP - 1) as i:
                        sp.wait_ge(s["bias_kept"], i + 1)
                        sp.dma_start(raw[:, :], a["L0_qkv"][bass.ds(i + 1, 1)].rearrange("o p w -> (o p) w")).then_inc(s["w_loaded"], 16)

                @block.gpsimd
                def _(pool):
                    nc.gpsimd.memset(kz[0:DH, 1, :], 0.0).then_inc(s["kz_cleared"], 1)
                    nc.gpsimd.memset(kz[DH:P, 0, :], 0.0).then_inc(s["kz_cleared"], 1)
                    pool.wait_ge(s["kz_cleared"], 2)

                    def split(hp):
                        pool.wait_ge(s["w_loaded"], (hp + 1) * 16)
                        pool.sem_inc(s["split_begun"], 1)
                        self.split_pool(pool, s["w_split"], raw[:, 0:W], cut(w, slice(None), slice(None)), hp)
                        nc.gpsimd.tensor_copy(bias[:, :], raw[:, W:W + 2]).then_inc(s["bias_kept"], 1)

                    def normalise(i):
                        for g in range(G):
                            pool.wait_ge(s["rsum"], G * i + g + 1)
                            nc.gpsimd.tensor_tensor(prob[:, g], prob[:, g], rs[:, g].unsqueeze(2).to_broadcast([S, 4, S]),
                                                    ALU.mult).then_inc(s["norm"], 1)

                    split(0)
                    pool.wait_ge(s["wo_loaded"], 16)
                    self.split_pool(pool, s["wo_split"], woraw[:, :, :], cut(wo, slice(None)), 0)
                    with pool.Fori(0, HP - 1) as i:
                        pool.wait_ge(s["v_ready"], 2 * i + 2)
                        pool.wait_ge(s["q_kept"], 2 * i + 2)
                        pool.wait_ge(s["k_kept"], 4 * i + 4)
                        split(i + 1)
                        normalise(i)
                    normalise(HP - 1)
                    self.ahead_split(pool, s)

                @block.scalar
                def _(act):
                    self.ln_scalar_sqrt(act, ln)
                    self.split_scalar(act, ln, xT)

                    def keep_q(hp):
                        act.wait_ge(s["bias_kept"], hp + 1)
                        for f in range(2):
                            act.wait_ge(s["qk_ready"], 4 * hp + 2 + f + 1)
                            nc.scalar.activation(qT[:, f * HALF:(f + 1) * HALF], ps[f][:, 0:HALF], ACT.Identity,
                                                 bias=bias[:, 0:1]).then_inc(s["q_kept"], 1)

                    def exps(i, g):
                        act.wait_ge(s["shifted"], G * i + g + 1)
                        nc.scalar.activation(prob[:, g], prob[:, g], ACT.Exp, scale=DH ** -0.5).then_inc(s["exps"], 1)

                    def keep_pT(i, g):
                        act.wait_ge(s["p_turned"], G * i + g + 1)
                        nc.scalar.activation(probT[:, g], ps[4 + g][0:S, 0:HALF].rearrange("p (a b) -> p a b", b=S),
                                             ACT.Copy).then_inc(s["pT_kept"], 1)

                    def keep_o(i, g):
                        act.wait_ge(s["pv_ready"], G * i + g + 1)
                        for h in range(2):
                            rows = slice(h * DH, (h + 1) * DH)
                            src = ps[g][rows, 0:HALF].rearrange("p (b h i) -> p b h i", b=2, h=2)[:, :, h, :]
                            dst = oT[0][rows, bass.ds(i, 1), 2 * g * S:(2 * g + 2) * S].rearrange("p o (b i) -> p (o b) i", b=2)
                            nc.scalar.activation(dst, src, ACT.Copy).then_inc(s["o_hi"], 1)

                    def body(i, more):
                        for g in range(G):
                            exps(i, g)
                        if more:
                            keep_q(i + 1)
                        keep_pT(i, 0)
                        keep_pT(i, 1)
                        keep_o(i, 0)
                        keep_pT(i, 2)
                        keep_o(i, 1)
                        keep_pT(i, 3)
                        keep_o(i, 2)
                        keep_o(i, 3)

                    keep_q(0)
                    with act.Fori(0, HP - 1) as i:
                        body(i, True)
                    body(HP - 1, False)

                @block.vector
                def _(dve):
                    dve.wait_ge(self.x_loaded, 16)
                    self.ln_vector(dve, ln, X, xn)
                    self.split_vector(dve, ln, xT)
                    dve.wait_ge(s["const_loaded"], 48)
                    c = Chain(dve, s["dchain"])
                    for t in range(NT):
                        last = nc.vector.tensor_tensor(X[:, t, :], X[:, t, :], bo[:, :], ALU.add)
                    c.link(last)

                    def keep_k(hp):
                        for f in range(2):
                            dve.wait_ge(s["qk_ready"], 4 * hp + f + 1)
                            for h in range(2):
                                rows = slice(h * DH, (h + 1) * DH)
                                nc.vector.scalar_tensor_tensor(
                                    out=kz[rows, h, f * HALF:(f + 1) * HALF].rearrange("p (b i) -> p b i", b=4),
                                    in0=ps[2 + f][rows, 0:HALF].rearrange("p (b i) -> p b i", b=4),
                                    scalar=bias[rows, 1:2], in1=pos[rows, :].unsqueeze(1).to_broadcast([DH, 4, S]),
                                    op0=ALU.add, op1=ALU.add).then_inc(s["k_kept"], 1)

                    def keep_v(hp):
                        for f in range(2):
                            dve.wait_ge(s["v_ready"], 2 * hp + f + 1)
                            nc.vector.tensor_tensor(v[:, 4 * f:4 * f + 4, :], ps[f][0:S, :].rearrange("p (b i) -> p b i", b=4),
                                                    vb[:, bass.ds(hp, 1), :].to_broadcast([S, 4, P]), ALU.add).then_inc(s["v_kept"], 1)

                    def shift(i, g):
                        dve.wait_ge(s["s_ready"], G * i + g + 1)
                        src = ps[4 + g][0:S, 0:HALF].rearrange("p (a b) -> p a b", b=S)
                        c.link(nc.vector.tensor_reduce(mx[:, g], src, AX, ALU.max))
                        nc.vector.tensor_tensor(prob[:, g], src, mx[:, g].unsqueeze(2).to_broadcast([S, 4, S]),
                                                ALU.subtract).then_inc(s["shifted"], 1)

                    def sums(i, g):
                        dve.wait_ge(s["exps"], G * i + g + 1)
                        c.link(nc.vector.tensor_reduce(rs[:, g], prob[:, g], AX, ALU.add))
                        nc.vector.reciprocal(rs[:, g], rs[:, g]).then_inc(s["rsum"], 1)

                    def keep_o(i, g):
                        for h in range(2):
                            dve.wait_ge(s["o_hi"], 2 * (G * i + g) + h + 1)
                            rows = slice(h * DH, (h + 1) * DH)
                            src = ps[g][rows, 0:HALF].rearrange("p (b h i) -> p b h i", b=2, h=2)[:, :, h, :]
                            at = (rows, bass.ds(i, 1), slice(2 * g * S, (2 * g + 2) * S))
                            dst, hi = (x[at].rearrange("p o (b i) -> p (o b) i", b=2) for x in (oT[1], oT[0]))
                            nc.vector.tensor_tensor(dst, src, hi.bitcast(F32), ALU.subtract).then_inc(s["o_lo"], 1)

                    def body(i, more):
                        shift(i, 0)
                        shift(i, 1)
                        sums(i, 0)
                        shift(i, 2)
                        sums(i, 1)
                        shift(i, 3)
                        sums(i, 2)
                        sums(i, 3)
                        if more:
                            keep_k(i + 1)
                        for g in range(G):
                            keep_o(i, g)
                        if more:
                            keep_v(i + 1)

                    dve.wait_ge(s["bias_kept"], 1)
                    dve.wait_ge(s["kz_cleared"], 2)
                    keep_k(0)
                    keep_v(0)
                    with dve.Fori(0, HP - 1) as i:
                        c.enter(i, 2 * G)
                        dve.wait_ge(s["bias_kept"], i + 2)
                        body(i, True)
                        c.leave(HP - 1)
                    body(HP - 1, False)
                    for t in range(NT):
                        dve.wait_ge(s["y_ready"], t + 1)
                        nc.vector.tensor_tensor(X[:, t, :], X[:, t, :], ps[t % 8][:, 0:D], ALU.add).then_inc(s["x_added"], 1)

                @block.tensor
                def _(pe):
                    self.turn_tensor(pe, ln, xn)
                    pe.wait_ge(ln["lo_ready"], 4)

                    def qk(hp, first=False):
                        for n, pick in ((1, k_w), (0, q_w)):
                            if n == 0 and not first:
                                pe.wait_ge(s["v_kept"], 2 * hp)
                            for f in range(2):
                                for k in range(KT):
                                    last = self.mm(ps[2 * n + f][:, 0:HALF], pick(w, k),
                                                   cut(xT, slice(None), k, slice(f * HALF, (f + 1) * HALF)), k == 0, k == KT - 1)
                                last.then_inc(s["qk_ready"], 1)

                    def values(hp, first=False):
                        for f in range(2):
                            if not first:
                                pe.wait_ge(s["o_lo"], 2 * G * (hp - 1) + 2 * f + 2)
                            for b in range(4):
                                for k in range(KT):
                                    last = self.mm(ps[f][0:S, tile(b)],
                                                   cut(xT, slice(None), k, slice((4 * f + b) * S, (4 * f + b + 1) * S)),
                                                   v_w(w, k), k == 0, k == KT - 1)
                            last.then_inc(s["v_ready"], 1)

                    def scores(i):
                        pe.wait_ge(s["q_kept"], 2 * i + 2)
                        pe.wait_ge(s["k_kept"], 4 * i + 4)
                        for g in range(G):
                            for j in range(2):
                                b = 2 * g + j
                                last = nc.tensor.matmul(
                                    ps[4 + g][0:S, j * 2 * S:(j + 1) * 2 * S].rearrange("p (h i) -> p h i", h=2),
                                    qT[:, b * S:(b + 1) * S], kz[:, :, b * S:(b + 1) * S], start=True, stop=True)
                            last.then_inc(s["s_ready"], 1)

                    def turn(i, g):
                        pe.wait_ge(s["norm"], G * i + g + 1)
                        for m in range(4):
                            last = nc.tensor.transpose(ps[4 + g][0:S, m * S:(m + 1) * S], prob[:, g, m, :], self.ident[0:S, 0:S])
                        last.then_inc(s["p_turned"], 1)

                    def mix(i, g):
                        pe.wait_ge(s["pT_kept"], G * i + g + 1)
                        for j in range(2):
                            last = nc.tensor.matmul(ps[g][:, j * 2 * S:(j + 1) * 2 * S].rearrange("p (h i) -> p h i", h=2),
                                                    v[:, 2 * g + j, :], probT[:, g, 2 * j:2 * j + 2, :], start=True, stop=True)
                        last.then_inc(s["pv_ready"], 1)

                    def body(i, more):
                        scores(i)
                        if more:
                            pe.wait_ge(s["w_split"], 2 * (i + 1) + 2)
                            qk(i + 1)
                        turn(i, 0)
                        turn(i, 1)
                        if more:
                            pe.wait_ge(s["q_kept"], 2 * i + 4)
                            pe.wait_ge(s["k_kept"], 4 * i + 8)
                        else:
                            pe.wait_ge(s["v_kept"], 2 * i + 2)
                        mix(i, 0)
                        turn(i, 2)
                        mix(i, 1)
                        turn(i, 3)
                        mix(i, 2)
                        mix(i, 3)
                        if more:
                            values(i + 1)
                        pe.wait_ge(s["o_lo"], 2 * G * i + 2 * G)

                    pe.wait_ge(s["w_split"], 2)
                    qk(0, first=True)
                    pe.wait_ge(s["q_kept"], 2)
                    values(0, first=True)
                    with pe.Fori(0, HP - 1) as i:
                        body(i, True)
                    body(HP - 1, False)
                    pe.wait_ge(s["wo_split"], 2)
                    self.project(pe, oT, wo, s["y_ready"])

    def project(self, pe, oT, w, y_ready, before=None):
        for t in range(NT):
            if before:
                before(t)
            for hp in range(HP):
                last = self.mm(self.ps[t % 8][:, 0:D], cut(oT, slice(None), hp, tile(t)), cut(w, slice(None), hp, slice(None)),
                               hp == 0, hp == HP - 1)
            last.then_inc(y_ready, 1)

    def ffn_sems(self, st, name):
        return st.sems_of("h_ready", "gate_done", "plain_done", "hid_hi", "hid_lo", "y_ready", "y_used", prefix=name + "_")

    def ffn_tensor(self, pe, o, e, xT, pick, gated, hid, w2, w2_ready, FT=8):
        pieces = 2 * FT
        for m in range(pieces):
            half, f = divmod(m, FT)
            depth = 2 if gated else 4
            if m >= depth:
                pe.wait_ge(o["plain_done"], pieces * e + m - depth + 1)
            for n in range(2 if gated else 1):
                bank = (2 * m + n) % 4 if gated else m % 4
                for k in range(KT):
                    last = self.mm(self.ps[bank][:, 0:HALF], pick(n, k, f),
                                   cut(xT, slice(None), k, slice(half * HALF, (half + 1) * HALF)), k == 0, k == KT - 1)
            last.then_inc(o["h_ready"], 1)
        w2_ready()
        for t in range(NT):
            if t == 0:
                pe.wait_ge(o["hid_lo"], pieces * e + FT)
            if t == 3:
                pe.wait_ge(o["hid_lo"], pieces * e + pieces)
            pe.wait_ge(o["y_used"], NT * e + (t - 3 if t >= 4 else 0) + 1)
            for f in range(FT):
                last = self.mm(self.ps[4 + t % 4][:, 0:D], cut(hid, slice(None), f, tile(t)),
                               cut(w2, slice(None), f, slice(None)), f == 0, f == FT - 1)
            last.then_inc(o["y_ready"], 1)

    def ffn_scalar(self, act, o, e, func, plain, gate, bias=None, FT=8):
        pieces = 2 * FT
        for m in range(pieces):
            act.wait_ge(o["h_ready"], pieces * e + m + 1)
            if gate is not None:
                if m >= 2:
                    act.wait_ge(o["plain_done"], pieces * e + m - 1)
                self.nc.scalar.activation(gate[:, m % 2], self.ps[(2 * m + 1) % 4][:, 0:HALF], func).then_inc(o["gate_done"], 1)
            else:
                if m >= 2:
                    act.wait_ge(o["hid_lo"], pieces * e + m - 1)
                self.nc.scalar.activation(plain[:, m % 2], self.ps[m % 4][:, 0:HALF], func,
                                          bias=bias[:, m % FT:m % FT + 1]).then_inc(o["plain_done"], 1)

    def ffn_vector(self, dve, o, e, plain, gate, hid, FT=8):
        nc = self.nc
        pieces = 2 * FT
        for m in range(pieces):
            half, f = divmod(m, FT)
            at = (slice(None), f, slice(half * HALF, (half + 1) * HALF))
            if gate is not None:
                dve.wait_ge(o["gate_done"], pieces * e + m + 1)
                nc.vector.tensor_tensor(plain[:, m % 2], gate[:, m % 2], self.ps[(2 * m) % 4][:, 0:HALF],
                                        ALU.mult).then_inc(o["plain_done"], 1)
            dve.wait_ge(o["plain_done"], pieces * e + m + 1)
            nc.vector.tensor_copy(hid[0][at], plain[:, m % 2]).then_inc(o["hid_hi"], 1)
            dve.wait_ge(o["hid_hi"], pieces * e + m + 1)
            nc.vector.tensor_tensor(hid[1][at], plain[:, m % 2], hid[0][at].bitcast(F32), ALU.subtract).then_inc(o["hid_lo"], 1)

    def l0_cross_attention(self):
        nc = self.nc
        with Stage(nc, "b") as st:
            self.Q = st.sb("q", [P, NT, D])
            self.qoT = st.sb("qoT", [P, HP, N])
            self.w1 = st.pair("w1", [P, KT, INNER])
            with Stage(nc, "bw") as sw:
                self.wk = sw.pair("wk", [P, KT, INNER])
                self.wv = sw.pair("wv", [P, KT, INNER])
                self.wkv = sw.sb("wkv", [P, KT, 192])
                self.w_ready = sw.sem("w_ready")
                self.cross_queries()
                self.cross_context()
            self.cross_output()

    def cross_queries(self):
        nc, a, ps = self.nc, self.a, self.ps
        with Stage(nc, "bq") as st:
            xT = st.pair("xT", [P, KT, N])
            plain = st.sb("plain", [P, KT, N])
            wq = self.ahead_as(a=KT)
            raw = st.sb("raw", [P, 2, KT, INNER])
            gb = st.sb("gb", [P, 2, KT])
            xn = st.sb("xn", [P, NT, D])
            qn = st.sb("qn", [P, 2, INNER])
            sq = st.sb("sq", [P, 2, 512])
            ssq = st.sb("ssq", [P, NT, H])
            ln, ln2 = self.ln_buffers(st, "ln"), self.ln_buffers(st, "lnb")
            s = st.sems_of("loaded", "w_split", "used", "g_loaded", "q_ready", "squared", "summed", "rooted", "chain",
                                          "scaled", "turned", "kept")
            with nc.Block() as block:
                @block.sync
                def _(sp):
                    sp.dma_start(gb[:, :, :], a["L0_ln1"]).then_inc(s["g_loaded"], 16)
                    sp.dma_start(raw[:, 0], a["L0_wk"]).then_inc(s["loaded"], 16)
                    sp.dma_start(raw[:, 1], a["L0_wv"]).then_inc(s["loaded"], 16)
                    sp.dma_start(self.wkv[:, :, :], a["L1_wkv"]).then_inc(s["loaded"], 16)

                @block.gpsimd
                def _(pool):
                    pool.wait_ge(s["loaded"], 48)
                    self.split_pool(pool, s["w_split"], raw[:, 0], cut(self.wk, slice(None)), 0)
                    self.split_pool(pool, s["w_split"], raw[:, 1], cut(self.wv, slice(None)), 1)

                @block.scalar
                def _(act):
                    self.ln_scalar_sqrt(act, ln)
                    self.ln_scalar_sqrt(act, ln2)
                    self.split_scalar(act, ln2, xT, plain)

                    def keep(t):
                        for n in range(2):
                            act.wait_ge(s["turned"], 2 * t + n + 1)
                            nc.scalar.activation(self.qoT[:, 4 * n:4 * n + 4, tile(t)],
                                                 ps[4 + 2 * (t % 2) + n][:, :].rearrange("p (a b) -> p a b", b=P), ACT.Copy).then_inc(s["kept"], 1)

                    for t in range(NT):
                        for n in range(2):
                            act.wait_ge(s["q_ready"], 2 * t + n + 1)
                            if t:
                                act.wait_ge(s["summed"], 2 * (t - 1) + n + 1)
                            nc.scalar.activation(sq[:, n], ps[(2 * t + n) % 4][:, :], ACT.Square).then_inc(s["squared"], 1)
                        act.wait_ge(s["summed"], 2 * t + 2)
                        nc.scalar.activation(ssq[:, t], ssq[:, t], ACT.Sqrt).then_inc(s["rooted"], 1)
                        if t:
                            keep(t - 1)
                    keep(NT - 1)

                @block.vector
                def _(dve):
                    self.ln_vector(dve, ln, self.X, self.Q)
                    dve.wait_ge(ln["norm_ready"], NT)
                    self.ln_vector(dve, ln2, self.Q, xn)
                    dve.wait_ge(s["g_loaded"], 16)
                    self.split_vector(dve, ln2, xT, plain, gb[:, 0], gb[:, 1])
                    c = Chain(dve, s["chain"])
                    for t in range(NT):
                        for n in range(2):
                            dve.wait_ge(s["squared"], 2 * t + n + 1)
                            nc.vector.tensor_reduce(ssq[:, t, 8 * n:8 * n + 8], sq[:, n].rearrange("p (h d) -> p h d", d=DH), AX, ALU.add).then_inc(s["summed"], 1)
                        dve.wait_ge(s["rooted"], t + 1)
                        c.link(nc.vector.tensor_scalar(ssq[:, t], ssq[:, t], 1e-12, None, ALU.max))
                        c.link(nc.vector.reciprocal(ssq[:, t], ssq[:, t]))
                        for n in range(2):
                            nc.vector.tensor_tensor(qn[:, t % 2, 512 * n:512 * n + 512].rearrange("p (h d) -> p h d", d=DH),
                                                    ps[(2 * t + n) % 4][:, :].rearrange("p (h d) -> p h d", d=DH),
                                                    ssq[:, t, 8 * n:8 * n + 8].unsqueeze(2).to_broadcast([P, 8, DH]),
                                                    ALU.mult).then_inc(s["scaled"], 1)

                @block.tensor
                def _(pe):
                    self.turn_tensor(pe, ln2, xn)
                    pe.wait_ge(ln2["lo_ready"], 4)

                    def turn(t):
                        pe.wait_ge(s["scaled"], 2 * t + 2)
                        if t >= 2:
                            pe.wait_ge(s["kept"], 2 * t - 2)
                        for n in range(2):
                            for m in range(4):
                                last = nc.tensor.transpose(ps[4 + 2 * (t % 2) + n][:, tile(m)], qn[:, t % 2, tile(4 * n + m)], self.ident[:, :])
                            last.then_inc(s["turned"], 1)

                    for t in range(NT):
                        for n in range(2):
                            if t >= 2:
                                pe.wait_ge(s["scaled"], 2 * (t - 2) + n + 1)
                            for k in range(KT):
                                last = self.mm(ps[(2 * t + n) % 4][:, :], cut(xT, slice(None), k, tile(t)),
                                               cut(wq, slice(None), k, slice(512 * n, 512 * n + 512)), k == 0, k == KT - 1)
                            last.then_inc(s["q_ready"], 1)
                        if t:
                            turn(t - 1)
                    turn(NT - 1)

    def cross_context(self):
        nc, a, ps, qoT = self.nc, self.a, self.ps, self.qoT
        with Stage(nc, "bc") as st:
            ctx = st.sb("ctx", [CP, CH, D])
            cn = st.sb("cn", [CP, CH, D])
            stats = st.sb("stats", [CP, CH, 6])
            mv = st.sb("mv", [CP, CH, 2])
            std = st.sb("std", [CP, CH])
            rstd = st.sb("rstd", [CP, CH])
            gb = st.sb("gb", [P, 2, 2, KT])
            scaled = st.sb("scaled", [P, 2, KT, S2])
            cT = st.pair("cT", [P, KT, S2])
            sq = st.sb("sq", [CP, 2, 512])
            ssq = st.sb("ssq", [CP, CH, H])
            kn = st.sb("kn", [CP, CH, INNER])
            v = st.sb("v", [CP, CH, INNER])
            w1raw = st.sb("w1raw", [P, 2 * INNER])
            kv = st.sb("kv", [P, HP, P])
            s = st.sems_of(
                "loaded", "g_loaded", "cleared", "chain", "aggr", "var", "root", "normed", "turned", "affine", "hi", "lo",
                "k_ready", "v_ready", "squared", "summed", "rooted", "k_kept", "v_kept", "l1_ready", "l1_kept",
                "kv_ready", "kv_kept_a", "kv_kept_d", "o_ready", "o_kept", "ahead_loaded", "ahead_split", "w1_loaded", "w1_split")
            with nc.Block() as block:
                @block.sync
                def _(sp):
                    sp.dma_start(gb[:, 0], a["L0_ln1"]).then_inc(s["g_loaded"], 16)
                    sp.dma_start(gb[:, 1], a["L1_cln"]).then_inc(s["g_loaded"], 16)
                    sp.dma_start(ctx[:, :, :], a["ctx"][0]).then_inc(s["loaded"], 16)
                    self.ahead_load(sp, s, a["L0_xwo"])
                    sp.dma_start(w1raw[:, :], a["L0_w1"]).then_inc(s["w1_loaded"], 16)
                    with sp.Fori(0, B - 1) as i:
                        sp.wait_ge(s["normed"], CH * i + CH)
                        sp.dma_start(ctx[:, :, :], a["ctx"][bass.ds(i + 1, 1)].rearrange("o p c d -> (o p) c d")).then_inc(s["loaded"], 16)

                @block.gpsimd
                def _(pool):
                    nc.gpsimd.memset(kv[:, :, :], 0.0).then_inc(s["cleared"], 1)
                    self.ahead_split(pool, s)
                    pool.wait_ge(s["w1_loaded"], 16)
                    self.split_pool(pool, s["w1_split"], w1raw[:, :], tuple(x[:, :, :].rearrange("p a b -> p (a b)") for x in self.w1), 0)

                @block.scalar
                def _(act):
                    act.sem_inc(s["o_kept"], 1)

                    def root(b):
                        act.wait_ge(s["var"], b + 1)
                        nc.scalar.activation(std[:, :], std[:, :], ACT.Sqrt).then_inc(s["root"], 1)

                    def split(b):
                        for k in range(KT):
                            act.wait_ge(s["affine"], 4 * b + 2 * k + 1)
                            nc.scalar.activation(cT[0][:, k], scaled[:, 0, k], ACT.Copy).then_inc(s["hi"], 1)

                    def body(i, more):
                        if more:
                            root(i + 1)
                        for c in range(CH):
                            for n in range(2):
                                act.wait_ge(s["k_ready"], 6 * i + 2 * c + n + 1)
                                if c:
                                    act.wait_ge(s["summed"], 6 * i + 2 * (c - 1) + n + 1)
                                nc.scalar.activation(sq[:, n], ps[6 * (c % 2) + n][0:CP, :], ACT.Square).then_inc(s["squared"], 1)
                            for n in range(2):
                                act.wait_ge(s["v_ready"], 6 * i + 2 * c + n + 1)
                                nc.scalar.activation(v[:, c, 512 * n:512 * n + 512], ps[2 + n][0:CP, :], ACT.Copy).then_inc(s["v_kept"], 1)
                            act.wait_ge(s["summed"], 6 * i + 2 * c + 2)
                            nc.scalar.activation(ssq[:, c], ssq[:, c], ACT.Sqrt).then_inc(s["rooted"], 1)
                        act.wait_ge(s["l1_ready"], 2 * i + 1)
                        nc.scalar.activation(self.k1T[:, bass.ds(i * S2, S2)], ps[4][:, 0:S2], ACT.Copy).then_inc(s["l1_kept"], 1)
                        act.wait_ge(s["l1_ready"], 2 * i + 2)
                        nc.scalar.activation(self.v1[:, bass.ds(i * CH, CH), :], ps[5][0:CP, 0:CH * DH].rearrange("p (c d) -> p c d", d=DH),
                                             ACT.Copy).then_inc(s["l1_kept"], 1)
                        if more:
                            split(i + 1)
                        for n in range(2):
                            act.wait_ge(s["kv_ready"], 2 * i + n + 1)
                            nc.scalar.activation(kv[0:DH, 4 * n:4 * n + 4, 0:DH],
                                                 ps[4 + n][0:DH, :].rearrange("p (a b) -> p a b", b=P)[:, :, 0:DH], ACT.Copy).then_inc(s["kv_kept_a"], 1)
                        for n in range(2):
                            act.wait_ge(s["o_ready"], 2 * i + n + 1)
                            nc.scalar.activation(qoT[:, 4 * n:4 * n + 4, bass.ds(i * S, S)],
                                                 ps[4 + n][:, 0:4 * S].rearrange("p (a b) -> p a b", b=S), ACT.Copy).then_inc(s["o_kept"], 1)

                    root(0)
                    split(0)
                    act.wait_ge(s["cleared"], 1)
                    with act.Fori(0, B - 1) as i:
                        body(i, True)
                    body(B - 1, False)

                @block.vector
                def _(dve):
                    c = Chain(dve, s["chain"])

                    def stat(b):
                        dve.wait_ge(s["loaded"], 16 * b + 16)
                        for n in range(CH):
                            last = nc.vector.bn_stats(stats[:, n], ctx[:, n])
                        c.link(last)
                        dve.sem_inc(s["aggr"], 1)
                        for n in range(CH):
                            last = nc.vector.bn_aggr(mv[:, n], stats[:, n])
                        c.link(last)
                        nc.vector.tensor_scalar(std[:, :], mv[:, :, 1], EPS, None, ALU.add).then_inc(s["var"], 1)

                    def norm(b):
                        dve.wait_ge(s["root"], b + 1)
                        c.link(nc.vector.reciprocal(rstd[:, :], std[:, :]))
                        for n in range(CH):
                            nc.vector.tensor_scalar(cn[:, n], ctx[:, n], mv[:, n, 0:1], rstd[:, n:n + 1],
                                                    ALU.subtract, ALU.mult).then_inc(s["normed"], 1)

                    def split(b):
                        for k in range(KT):
                            dve.wait_ge(s["turned"], 2 * b + k + 1)
                            for l in range(2):
                                nc.vector.tensor_scalar(scaled[:, l, k], ps[6 + k][:, 0:S2], gb[:, l, 0, k:k + 1], gb[:, l, 1, k:k + 1],
                                                        ALU.mult, ALU.add).then_inc(s["affine"], 1)
                        for k in range(KT):
                            dve.wait_ge(s["hi"], 2 * b + k + 1)
                            nc.vector.tensor_tensor(cT[1][:, k], scaled[:, 0, k], cT[0][:, k].bitcast(F32),
                                                    ALU.subtract).then_inc(s["lo"], 1)

                    def body(i, more):
                        if more:
                            stat(i + 1)
                        for m in range(CH):
                            for n in range(2):
                                dve.wait_ge(s["squared"], 6 * i + 2 * m + n + 1)
                                nc.vector.tensor_reduce(ssq[:, m, 8 * n:8 * n + 8], sq[:, n].rearrange("p (h d) -> p h d", d=DH), AX, ALU.add).then_inc(s["summed"], 1)
                            dve.wait_ge(s["rooted"], CH * i + m + 1)
                            c.link(nc.vector.tensor_scalar(ssq[:, m], ssq[:, m], 1e-12, None, ALU.max))
                            c.link(nc.vector.reciprocal(ssq[:, m], ssq[:, m]))
                            for n in range(2):
                                nc.vector.tensor_tensor(kn[:, m, 512 * n:512 * n + 512].rearrange("p (h d) -> p h d", d=DH),
                                                        ps[6 * (m % 2) + n][0:CP, :].rearrange("p (h d) -> p h d", d=DH),
                                                        ssq[:, m, 8 * n:8 * n + 8].unsqueeze(2).to_broadcast([CP, 8, DH]),
                                                        ALU.mult).then_inc(s["k_kept"], 1)
                            if m == 0 and more:
                                norm(i + 1)
                        if more:
                            split(i + 1)
                        for n in range(2):
                            dve.wait_ge(s["kv_ready"], 2 * i + n + 1)
                            nc.vector.tensor_copy(kv[DH:P, 4 * n:4 * n + 4, DH:P],
                                                  ps[4 + n][DH:P, :].rearrange("p (a b) -> p a b", b=P)[:, :, DH:P]).then_inc(s["kv_kept_d"], 1)

                    dve.wait_ge(s["g_loaded"], 32)
                    stat(0)
                    norm(0)
                    split(0)
                    dve.wait_ge(s["cleared"], 1)
                    with dve.Fori(0, B - 1) as i:
                        c.enter(i, 3 + 2 * CH)
                        body(i, True)
                        c.leave(B - 1)
                    body(B - 1, False)

                @block.tensor
                def _(pe):
                    def turn(b):
                        pe.wait_ge(s["normed"], CH * b + CH)
                        for k in range(KT):
                            for m in range(CH):
                                last = nc.tensor.transpose(ps[6 + k][:, m * CP:(m + 1) * CP], cn[:, m, tile(k)], self.ident[0:CP, 0:CP])
                            last.then_inc(s["turned"], 1)

                    def body(i, more):
                        pe.wait_ge(s["lo"], 2 * i + 2)
                        for m in range(CH):
                            rows = slice(m * CP, (m + 1) * CP)
                            for w, bank, ready in ((self.wk, 6 * (m % 2), s["k_ready"]), (self.wv, 2, s["v_ready"])):
                                if w is self.wk and m == 2:
                                    pe.wait_ge(s["k_kept"], 6 * i + 2)
                                if w is self.wv and m:
                                    pe.wait_ge(s["v_kept"], 6 * i + 2 * m)
                                for n in range(2):
                                    for k in range(KT):
                                        last = self.mm(ps[bank + n][0:CP, :], cut(cT, slice(None), k, rows),
                                                       cut(w, slice(None), k, slice(512 * n, 512 * n + 512)), k == 0, k == KT - 1)
                                    last.then_inc(ready, 1)
                        pe.wait_ge(s["o_kept"], 2 * i + 1)
                        for k in range(KT):
                            last = nc.tensor.matmul(ps[4][:, 0:S2], self.wkv[:, k, 0:P], scaled[:, 1, k], start=k == 0, stop=k == KT - 1)
                        last.then_inc(s["l1_ready"], 1)
                        for m in range(CH):
                            for k in range(KT):
                                last = nc.tensor.matmul(ps[5][0:CP, m * DH:(m + 1) * DH], scaled[:, 1, k, m * CP:(m + 1) * CP], self.wkv[:, k, P:P + DH],
                                                        start=k == 0, stop=k == KT - 1)
                        last.then_inc(s["l1_ready"], 1)
                        if more:
                            pe.wait_ge(s["k_kept"], 6 * i + 4)
                            turn(i + 1)
                        pe.wait_ge(s["k_kept"], 6 * i + 6)
                        pe.wait_ge(s["v_kept"], 6 * i + 6)
                        pe.wait_ge(s["l1_kept"], 2 * i + 2)
                        for n in range(2):
                            for hp in range(4 * n, 4 * n + 4):
                                for m in range(CH):
                                    last = nc.tensor.matmul(ps[4 + n][:, tile(hp % 4)], kn[:, m, tile(hp)], v[:, m, tile(hp)],
                                                            start=m == 0, stop=m == CH - 1)
                            last.then_inc(s["kv_ready"], 1)
                        pe.wait_ge(s["kv_kept_a"], 2 * i + 2)
                        pe.wait_ge(s["kv_kept_d"], 2 * i + 2)
                        for n in range(2):
                            for hp in range(4 * n, 4 * n + 4):
                                last = nc.tensor.matmul(ps[4 + n][:, (hp % 4) * S:(hp % 4 + 1) * S], kv[:, hp, :], qoT[:, hp, bass.ds(i * S, S)],
                                                        start=True, stop=True)
                            last.then_inc(s["o_ready"], 1)

                    turn(0)
                    with pe.Fori(0, B - 1) as i:
                        body(i, True)
                    body(B - 1, False)

    def cross_output(self):
        nc, a, ps, X, Q, qoT = self.nc, self.a, self.ps, self.X, self.Q, self.qoT
        with Stage(nc, "bo") as st:
            hid = st.pair("hid", [P, HP, N])
            wo, w1 = self.ahead_as(a=HP), self.w1
            w2 = st.pair("w2", [P, HP, D])
            xT = st.pair("xT", [P, KT, N])
            bo = st.sb("bo", [P, 2, D])
            gb = st.sb("gb", [P, 2, KT])
            b1 = st.sb("b1", [P, 8])
            plain = st.sb("plain", [P, 2, HALF])
            scaled = qoT[:, 0:KT, :]
            xn = qoT[:, 2:4, :].rearrange("p a b -> p (a b)").rearrange("p (t d) -> p t d", d=D)
            ln = self.ln_buffers(st)
            f = self.ffn_sems(st, "ffn")
            s = st.sems_of("loaded", "c_loaded", "w_split", "o_hi", "o_lo", "y_ready", "x_added", "added", "sum_ready")
            with nc.Block() as block:
                @block.sync
                def _(sp):
                    sp.dma_start(bo[:, 0], a["L0_xattn_bo"].partition_broadcast(P)).then_inc(s["c_loaded"], 16)
                    sp.dma_start(bo[:, 1], a["L0_xattn_b2"].partition_broadcast(P)).then_inc(s["c_loaded"], 16)
                    sp.dma_start(gb[:, :, :], a["L0_ln2"]).then_inc(s["c_loaded"], 16)
                    sp.dma_start(b1[:, :], a["L0_b1"]).then_inc(s["c_loaded"], 16)
                    sp.dma_start(self.ahead_raw[:, :], a["L0_w2"]).then_inc(s["loaded"], 16)

                @block.gpsimd
                def _(pool):
                    pool.wait_ge(s["loaded"], 16)
                    self.split_pool(pool, s["w_split"], self.ahead_raw[:, :], tuple(x[:, :, :].rearrange("p a b -> p (a b)") for x in w2), 0)

                @block.scalar
                def _(act):
                    for t in range(NT):
                        nc.scalar.activation(hid[0][:, :, tile(t)], qoT[:, :, tile(t)], ACT.Copy).then_inc(s["o_hi"], 1)
                    self.ln_scalar_sqrt(act, ln)
                    self.split_scalar(act, ln, xT, scaled)
                    self.ffn_scalar(act, f, 0, ACT.Gelu, plain, None, b1)

                @block.vector
                def _(dve):
                    for t in range(NT):
                        dve.wait_ge(s["o_hi"], t + 1)
                        nc.vector.tensor_tensor(hid[1][:, :, tile(t)], qoT[:, :, tile(t)], hid[0][:, :, tile(t)].bitcast(F32), ALU.subtract).then_inc(s["o_lo"], 1)
                    dve.wait_ge(s["c_loaded"], 64)
                    nc.vector.tensor_tensor(Q[:, :, :], Q[:, :, :], bo[:, 0].unsqueeze(1).to_broadcast([P, NT, D]), ALU.add).then_inc(s["added"], 1)
                    nc.vector.tensor_tensor(X[:, :, :], X[:, :, :], bo[:, 1].unsqueeze(1).to_broadcast([P, NT, D]), ALU.add).then_inc(s["added"], 1)
                    dve.wait_ge(s["added"], 2)
                    for t in range(NT):
                        dve.wait_ge(s["y_ready"], t + 1)
                        nc.vector.tensor_tensor(Q[:, t], Q[:, t], ps[t][:, 0:D], ALU.add).then_inc(s["x_added"], 1)
                    dve.wait_ge(s["x_added"], NT)
                    self.ln_vector(dve, ln, Q, xn)
                    self.split_vector(dve, ln, xT, scaled, gb[:, 0], gb[:, 1])
                    nc.vector.tensor_tensor(X[:, :, :], X[:, :, :], Q[:, :, :], ALU.add).then_inc(s["sum_ready"], 1)
                    dve.sem_inc(f["y_used"], 1)
                    self.ffn_vector(dve, f, 0, plain, None, hid)
                    dve.wait_ge(s["sum_ready"], 1)
                    for t in range(NT):
                        dve.wait_ge(f["y_ready"], t + 1)
                        nc.vector.tensor_tensor(X[:, t], X[:, t], ps[4 + t % 4][:, 0:D], ALU.add).then_inc(f["y_used"], 1)

                @block.tensor
                def _(pe):
                    self.project(pe, hid, wo, s["y_ready"], lambda t: pe.wait_ge(s["o_lo"], t + 1))
                    self.turn_tensor(pe, ln, xn)
                    pe.wait_ge(ln["lo_ready"], 4)
                    self.ffn_tensor(pe, f, 0, xT, lambda n, k, ft: cut(w1, slice(None), k, tile(ft)), False, hid, w2,
                                    lambda: pe.wait_ge(s["w_split"], 2))

    def rank(self, dve, c, vals, lt, n, more, same, out):
        nc = self.nc
        here = vals.unsqueeze(3).to_broadcast([P, NT, n, n])
        other = vals.unsqueeze(2).to_broadcast([P, NT, n, n])
        view = (slice(None), slice(None), slice(0, n), slice(0, n))
        nc_lt = lt[:, 0:n, 0:n].unsqueeze(1).to_broadcast([P, NT, n, n])
        c.link(nc.vector.tensor_tensor(more[view], other, here, ALU.is_gt))
        c.link(nc.vector.tensor_tensor(same[view], other, here, ALU.is_equal))
        c.link(nc.vector.tensor_tensor(same[view], same[view], nc_lt, ALU.mult))
        c.link(nc.vector.tensor_tensor(more[view], more[view], same[view], ALU.add))
        c.link(nc.vector.tensor_reduce(out, more[view], AX, ALU.add))

    def l0_experts(self):
        nc, a, ps, X = self.nc, self.a, self.ps, self.X
        E, SH, W = 16, 2, 6 * P
        with Stage(nc, "c") as st:
            xT = st.pair("xT", [P, KT, N])
            xn = st.sb("xn", [P, NT, D])
            raw = st.sb("raw", [P, 2, W])
            w = [st.pair(f"w{j}", [P, W]) for j in range(2)]
            graw = st.sb("graw", [P, KT, E])
            gw = st.pair("gw", [P, KT, E])
            gbias = st.sb("gbias", [P, E])
            lt = st.sb("lt", [P, E, E])
            score = st.sb("score", [P, NT, E])
            more = st.sb("more", [P, NT, E, E])
            same = st.sb("same", [P, NT, E, E])
            grp = st.sb("grp", [P, 8, NT, 4])
            keep = st.sb("keep", [P, NT, E])
            tot = st.sb("tot", [P, NT])
            share = st.sb("share", [P, NT, SH + E])
            col = st.sb("col", [P, 2, NT])
            gate = st.sb("gate", [P, 2, HALF])
            plain = st.sb("plain", [P, 2, HALF])
            hid = [st.pair(f"hid{j}", [P, N]) for j in range(2)]
            ln = self.ln_buffers(st)
            s = st.sems_of("c_loaded", "w_split", "begun", "g_split", "logit", "scored", "chain", "h_ready", "gate_done",
                                          "plain_done", "hid_hi", "hid_lo", "y_ready", "y_used")
            loaded = [st.sem(f"loaded{j}") for j in range(2)]
            with nc.Block() as block:
                @block.sync
                def _(sp):
                    sp.dma_start(graw[:, :, :], a["L0_gate"]).then_inc(s["c_loaded"], 16)
                    sp.dma_start(gbias[:, :], a["L0_ffn_gate_bias"].partition_broadcast(P)).then_inc(s["c_loaded"], 16)
                    sp.dma_start(lt[:, :, :], a["lower"].partition_broadcast(P)).then_inc(s["c_loaded"], 16)
                    sp.dma_start(raw[:, 0], a["L0_experts"][0]).then_inc(loaded[0], 16)
                    sp.dma_start(raw[:, 1], a["L0_experts"][1]).then_inc(loaded[1], 16)
                    with sp.Fori(0, (E + SH) // 2 - 1) as i:
                        for j in range(2):
                            sp.wait_ge(s["w_split"], 4 * i + 2 * j + 2)
                            sp.dma_start(raw[:, j], a["L0_experts"][bass.ds(2 * i + 2 + j, 1)].rearrange("o p w -> (o p) w")).then_inc(loaded[j], 16)

                @block.gpsimd
                def _(pool):
                    pool.wait_ge(s["c_loaded"], 48)
                    self.split_pool(pool, s["g_split"], graw[:, :, :], cut(gw, slice(None)), 0)

                    def split(i, j):
                        pool.wait_ge(loaded[j], 16 * i + 16)
                        pool.sem_inc(s["begun"], 1)
                        self.split_pool(pool, s["w_split"], raw[:, j], cut(w[j], slice(None)), 2 * i + j)

                    split(0, 0)
                    split(0, 1)
                    with pool.Fori(0, (E + SH) // 2 - 1) as i:
                        for j in range(2):
                            pool.wait_ge(s["y_ready"], NT * (2 * i + j) + NT)
                            split(i + 1, j)

                @block.scalar
                def _(act):
                    self.ln_scalar_sqrt(act, ln)
                    self.split_scalar(act, ln, xT)
                    act.wait_ge(s["logit"], 1)
                    nc.scalar.activation(score[:, :, :], ps[7][:, 0:NT * E].rearrange("p (t e) -> p t e", e=E), ACT.Sigmoid).then_inc(s["scored"], 1)
                    with act.Fori(0, (E + SH) // 2) as i:
                        for j in range(2):
                            for f in range(2):
                                q = 4 * i + 2 * j + f
                                act.wait_ge(s["h_ready"], q + 1)
                                act.wait_ge(s["plain_done"], q + 1)
                                nc.scalar.activation(gate[:, f], ps[2 * f][:, 0:HALF], ACT.Silu).then_inc(s["gate_done"], 1)

                @block.vector
                def _(dve):
                    dve.sem_inc(s["plain_done"], 2)
                    dve.sem_inc(s["y_used"], 1)
                    self.ln_vector(dve, ln, X, xn)
                    self.split_vector(dve, ln, xT)
                    c = Chain(dve, s["chain"])
                    dve.wait_ge(s["c_loaded"], 48)
                    dve.wait_ge(s["scored"], 1)
                    sfc = score
                    c.link(nc.vector.tensor_tensor(sfc[:, :, :], score[:, :, :], gbias[:, :].unsqueeze(1).to_broadcast([P, NT, E]), ALU.add))
                    g4 = sfc[:, :, :].rearrange("p t (g j) -> p t g j", j=4)
                    for n, (x, y, op) in enumerate(((0, 1, ALU.max), (2, 3, ALU.max), (0, 1, ALU.min), (2, 3, ALU.min))):
                        c.link(nc.vector.tensor_tensor(grp[:, n], g4[:, :, :, x], g4[:, :, :, y], op))
                    for to, x, y, op in ((4, 0, 1, ALU.max), (5, 0, 1, ALU.min), (6, 2, 3, ALU.max), (5, 5, 6, ALU.max), (7, 4, 5, ALU.add)):
                        c.link(nc.vector.tensor_tensor(grp[:, to], grp[:, x], grp[:, y], op))
                    self.rank(dve, c, grp[:, 7], lt, 4, more, same, grp[:, 0])
                    c.link(nc.vector.tensor_scalar(grp[:, 1], grp[:, 0], 2.0, None, ALU.is_lt))
                    c.link(nc.vector.tensor_tensor(g4, g4, grp[:, 1].unsqueeze(3).to_broadcast([P, NT, 4, 4]), ALU.mult))
                    self.rank(dve, c, sfc[:, :, :], lt, E, more, same, keep[:, :, :])
                    c.link(nc.vector.tensor_scalar(keep[:, :, :], keep[:, :, :], 4.0, None, ALU.is_lt))
                    c.link(nc.vector.tensor_tensor(keep[:, :, :], keep[:, :, :], sfc[:, :, :], ALU.mult))
                    c.link(nc.vector.tensor_reduce(tot[:, :], keep[:, :, :], AX, ALU.add))
                    c.link(nc.vector.tensor_scalar(tot[:, :], tot[:, :], 1e-20, None, ALU.add))
                    c.link(nc.vector.reciprocal(tot[:, :], tot[:, :]))
                    c.link(nc.vector.tensor_tensor(keep[:, :, :], keep[:, :, :], tot[:, :].unsqueeze(2).to_broadcast([P, NT, E]), ALU.mult))
                    c.link(nc.vector.memset(share[:, :, 0:SH], 1.0))
                    c.link(nc.vector.tensor_scalar(share[:, :, SH:SH + E], keep[:, :, :], 2.5, None, ALU.mult))
                    with dve.Fori(0, (E + SH) // 2) as i:
                        c.enter(i, 2)
                        for j in range(2):
                            c.link(nc.vector.tensor_copy(col[:, j].unsqueeze(2), share[:, :, bass.ds(2 * i + j, 1)]))
                        for j in range(2):
                            for f in range(2):
                                q = 4 * i + 2 * j + f
                                cols = slice(f * HALF, (f + 1) * HALF)
                                dve.wait_ge(s["gate_done"], q + 1)
                                nc.vector.tensor_tensor(plain[:, f], gate[:, f], ps[2 * f + 1][:, 0:HALF], ALU.mult).then_inc(s["plain_done"], 1)
                                dve.wait_ge(s["plain_done"], q + 3)
                                nc.vector.tensor_copy(hid[j][0][:, cols], plain[:, f]).then_inc(s["hid_hi"], 1)
                                dve.wait_ge(s["hid_hi"], q + 1)
                                nc.vector.tensor_tensor(hid[j][1][:, cols], plain[:, f], hid[j][0][:, cols].bitcast(F32), ALU.subtract).then_inc(s["hid_lo"], 1)
                        for j in range(2):
                            for t in range(NT):
                                dve.wait_ge(s["y_ready"], NT * (2 * i + j) + t + 1)
                                dve.wait_ge(s["y_used"], NT * (2 * i + j) + 1)
                                nc.vector.scalar_tensor_tensor(out=X[:, t], in0=ps[4 + t % 4][:, 0:D], scalar=col[:, j, t:t + 1], in1=X[:, t],
                                                               op0=ALU.mult, op1=ALU.add).then_inc(s["y_used"], 1)
                        c.leave((E + SH) // 2)

                @block.tensor
                def _(pe):
                    self.turn_tensor(pe, ln, xn)
                    pe.wait_ge(ln["lo_ready"], 4)
                    pe.wait_ge(s["g_split"], 2)
                    self.logits(pe, xT, gw, E, s["logit"])
                    pe.wait_ge(s["scored"], 1)
                    with pe.Fori(0, (E + SH) // 2) as i:
                        for j in range(2):
                            pe.wait_ge(s["w_split"], 4 * i + 2 * j + 2)
                            for f in range(2):
                                q = 4 * i + 2 * j + f
                                pe.wait_ge(s["plain_done"], q + 1)
                                for n in range(2):
                                    for k in range(KT):
                                        last = self.mm(ps[2 * f + n][:, 0:HALF], cut(w[j], slice(None), slice((2 * k + n) * P, (2 * k + n + 1) * P)),
                                                       cut(xT, slice(None), k, slice(f * HALF, (f + 1) * HALF)), k == 0, k == KT - 1)
                                last.then_inc(s["h_ready"], 1)
                        for j in range(2):
                            pe.wait_ge(s["hid_lo"], 4 * i + 2 * j + 2)
                            for t in range(NT):
                                pe.wait_ge(s["y_used"], NT * (2 * i + j) + (t - 3 if t >= 4 else 0) + 1)
                                self.mm(ps[4 + t % 4][:, 0:D], cut(hid[j], slice(None), tile(t)), cut(w[j], slice(None), slice(4 * P, 6 * P)),
                                        True, True).then_inc(s["y_ready"], 1)

    def logits(self, pe, xT, gw, n, ready):
        for t in range(NT):
            for k in range(KT):
                last = self.mm(self.ps[7][:, t * n:(t + 1) * n], cut(xT, slice(None), k, tile(t)), cut(gw, slice(None), k, slice(None)),
                               k == 0, k == KT - 1)
        last.then_inc(ready, 1)

    def l1_attention(self):
        nc, a, ps, X = self.nc, self.a, self.ps, self.X
        HD = 16
        with Stage(nc, "d") as st:
            xn = st.sb("xn", [P, NT, D])
            xT = st.sb("xT", [P, KT, N])
            w = st.sb("w", [P, KT, 2 * D])
            nw = st.sb("nw", [S, 2, D])
            own = st.sb("own", [P, 8, S])
            causal = st.sb("causal", [S, S])
            sq = st.sb("sq", [S, 2, 2 * D])
            ms = st.sb("ms", [S, 2, 2 * H])
            qv = st.sb("qv", [S, 2, 2 * D])
            qz = st.sb("qz", [P, KT, 8, S])
            sc = st.sb("sc", [S, H, S])
            out = st.sb("out", [S, B, D])
            back = st.sb("back", [P, NT, D])
            ln = self.ln_buffers(st)
            s = st.sems_of("loaded", "proj", "squared", "rooted", "chain", "mean", "qv_ready", "q_turned", "qz_ready", "s_ready",
                                          "s_kept", "o_ready", "o_kept", "spilled", "spilled_last", "back", "back_last", "added",
                                          "ahead_loaded", "ahead_split")
            full = (B - 1) * S // P
            spill_in, spill_out = a["spill"].rearrange("(b i) f -> i b f", i=S), a["spill"].rearrange("(t p) f -> p t f", p=P)
            with nc.Block() as block:
                @block.gpsimd
                def _(pool):
                    self.ahead_split(pool, s)

                @block.sync
                def _(sp):
                    sp.dma_start(w[:, :, :], a["L1_wqv"]).then_inc(s["loaded"], 16)
                    sp.dma_start(nw[:, :, :], a["L1_norm_w"].partition_broadcast(S)).then_inc(s["loaded"], 16)
                    sp.dma_start(own[:, :, :], a["own"]).then_inc(s["loaded"], 16)
                    sp.dma_start(causal[:, :], a["causal"]).then_inc(s["loaded"], 16)
                    self.ahead_load(sp, s, a["L1_wq"].rearrange("p k n -> p (k n)"))
                    sp.wait_ge(s["o_kept"], B - 1)
                    sp.dma_start(spill_in[:, 0:B - 1], out[:, 0:B - 1]).then_inc(s["spilled"], 16)
                    sp.wait_ge(s["spilled"], 16)
                    sp.dma_start(back[:, 0:full], spill_out[:, 0:full]).then_inc(s["back"], 16)
                    sp.wait_ge(s["o_kept"], B)
                    sp.dma_start(spill_in[:, B - 1:B], out[:, B - 1:B]).then_inc(s["spilled_last"], 16)
                    sp.wait_ge(s["spilled_last"], 16)
                    sp.dma_start(back[:, full:NT], spill_out[:, full:NT]).then_inc(s["back_last"], 16)

                @block.scalar
                def _(act):
                    self.ln_scalar_sqrt(act, ln)
                    for n, (g, k, cols, src) in enumerate(self.turn_pieces()):
                        act.wait_ge(ln["turned"], g + 1)
                        nc.scalar.activation(xT[:, k, cols], src, ACT.Copy).then_inc(ln["hi_ready"], 1)

                    def square(b):
                        act.wait_ge(s["proj"], b + 1)
                        if b >= 2:
                            act.wait_ge(s["mean"], b - 1)
                        nc.scalar.activation(sq[:, b % 2], ps[b % 2][0:S, :], ACT.Square).then_inc(s["squared"], 1)
                        act.wait_ge(s["mean"], b + 1)
                        nc.scalar.activation(ms[:, b % 2], ms[:, b % 2], ACT.Sqrt).then_inc(s["rooted"], 1)

                    square(0)
                    for b in range(B):
                        if b + 1 < B:
                            square(b + 1)
                        act.wait_ge(s["o_ready"], b + 1)
                        nc.scalar.activation(out[:, b], ps[3][0:S, 0:D], ACT.Copy).then_inc(s["o_kept"], 1)

                @block.vector
                def _(dve):
                    self.ln_vector(dve, ln, X, xn)
                    c = Chain(dve, s["chain"])
                    dve.wait_ge(s["loaded"], 64)

                    def norm(b):
                        dve.wait_ge(s["squared"], b + 1)
                        c.link(nc.vector.tensor_reduce(ms[:, b % 2], sq[:, b % 2].rearrange("p (h d) -> p h d", d=HD), AX, ALU.add))
                        nc.vector.tensor_scalar(ms[:, b % 2], ms[:, b % 2], 1.0 / HD, 1e-8, ALU.mult, ALU.add).then_inc(s["mean"], 1)
                        dve.wait_ge(s["rooted"], b + 1)
                        c.link(nc.vector.reciprocal(ms[:, b % 2], ms[:, b % 2]))
                        if b >= 2:
                            dve.wait_ge(s["o_ready"], b - 1)
                        c.link(nc.vector.tensor_tensor(qv[:, b % 2].rearrange("p (h d) -> p h d", d=HD), ps[b % 2][0:S, :].rearrange("p (h d) -> p h d", d=HD),
                                                       ms[:, b % 2].unsqueeze(2).to_broadcast([S, 2 * H, HD]), ALU.mult))
                        nc.vector.tensor_tensor(qv[:, b % 2], qv[:, b % 2], nw[:, :, :].rearrange("p a d -> p (a d)"), ALU.mult).then_inc(s["qv_ready"], 1)

                    norm(0)
                    for b in range(B):
                        for k in range(KT):
                            dve.wait_ge(s["q_turned"], b + 1)
                            nc.vector.tensor_tensor(qz[:, k], own[:, :, :], ps[2][:, k * S:(k + 1) * S].unsqueeze(1).to_broadcast([P, 8, S]),
                                                    ALU.mult).then_inc(s["qz_ready"], 1)
                        if b + 1 < B:
                            norm(b + 1)
                        for g in range(4):
                            dve.wait_ge(s["s_ready"], 4 * b + g + 1)
                            nc.vector.tensor_tensor(sc[:, 4 * g:4 * g + 4], ps[4 + g][0:S, 0:4 * S].rearrange("p (h i) -> p h i", i=S),
                                                    causal[:, :].unsqueeze(1).to_broadcast([S, 4, S]), ALU.mult).then_inc(s["s_kept"], 1)
                    dve.wait_ge(s["back"], 16)
                    nc.vector.tensor_tensor(X[:, 0:full], X[:, 0:full], back[:, 0:full], ALU.add).then_inc(s["added"], 1)
                    dve.wait_ge(s["back_last"], 16)
                    nc.vector.tensor_tensor(X[:, full:NT], X[:, full:NT], back[:, full:NT], ALU.add).then_inc(s["added"], 1)

                @block.tensor
                def _(pe):
                    self.turn_tensor(pe, ln, xn)
                    pe.wait_ge(ln["hi_ready"], 4)
                    pe.wait_ge(s["loaded"], 64)

                    def proj(b):
                        if b >= 2:
                            pe.wait_ge(s["qv_ready"], b - 1)
                        for k in range(KT):
                            last = nc.tensor.matmul(ps[b % 2][0:S, :], xT[:, k, b * S:(b + 1) * S], w[:, k, :], start=k == 0, stop=k == KT - 1)
                        last.then_inc(s["proj"], 1)

                    def turn(b):
                        pe.wait_ge(s["qv_ready"], b + 1)
                        for k in range(KT):
                            last = nc.tensor.transpose(ps[2][:, k * S:(k + 1) * S], qv[:, b % 2, tile(k)], self.ident[0:S, 0:S])
                        last.then_inc(s["q_turned"], 1)

                    proj(0)
                    proj(1)
                    turn(0)
                    for b in range(B):
                        for g in range(4):
                            pe.wait_ge(s["qz_ready"], KT * b + g // 2 + 1)
                            last = nc.tensor.matmul(ps[4 + g][0:S, 0:4 * S].rearrange("p (h i) -> p h i", i=S), xT[:, g // 2, b * S:(b + 1) * S],
                                                    qz[:, g // 2, 4 * (g % 2):4 * (g % 2) + 4, :], start=True, stop=True)
                            last.then_inc(s["s_ready"], 1)
                        if b + 1 < B:
                            turn(b + 1)
                        if b + 2 < B:
                            proj(b + 2)
                        if b:
                            pe.wait_ge(s["o_kept"], b)
                        for h in range(H):
                            pe.wait_ge(s["s_kept"], 4 * b + h // 4 + 1)
                            last = nc.tensor.matmul(ps[3][0:S, h * HD:(h + 1) * HD], sc[:, h, :], qv[:, b % 2, D + h * HD:D + (h + 1) * HD], start=True, stop=True)
                        last.then_inc(s["o_ready"], 1)

    def l1_cross_attention(self):
        nc = self.nc
        with Stage(nc, "e") as st:
            self.qoT = st.sb("qoT", [P, HP, N])
            self.masks = st.sb("masks", [S, B, S2])
            self.mask_loaded = st.sem("mask_loaded")
            self.qz = st.sb("qz", [P, H, S])
            with Stage(nc, "ex") as sx:
                self.xT1 = sx.pair("xT", [P, KT, N])
                self.w1 = sx.pair("w1", [P, KT, 2 * INNER])
                self.multi_queries()
                self.gated_ffn()
            with Stage(nc, "ey") as sy:
                self.oT = sy.pair("oT", [P, HP, N])
                self.multi_attention()
                self.multi_output()

    def multi_queries(self):
        nc, a, ps = self.nc, self.a, self.ps
        xT = self.xT1
        with Stage(nc, "eq") as st:
            xn = st.sb("xn", [P, NT, D])
            scaled = st.sb("scaled", [P, KT, N])
            raw = st.sb("raw", [P, KT, 2 * INNER])
            wq = self.ahead_as(a=KT)
            gb = st.sb("gb", [P, 2, KT])
            ln = self.ln_buffers(st)
            s = st.sems_of("loaded", "w_loaded", "w_split", "q_ready", "kept")
            with nc.Block() as block:
                @block.sync
                def _(sp):
                    sp.dma_start(gb[:, :, :], a["L1_ln"]).then_inc(s["loaded"], 16)
                    sp.dma_start(raw[:, :, :], a["L1_w1"]).then_inc(s["w_loaded"], 16)
                    sp.dma_start(self.masks[:, :, :], a["mask"].rearrange("b i j -> i b j")).then_inc(self.mask_loaded, 16)

                @block.gpsimd
                def _(pool):
                    pool.wait_ge(s["w_loaded"], 16)
                    for k in range(KT):
                        self.split_pool(pool, s["w_split"], raw[:, k], cut(self.w1, slice(None), k), k)

                @block.scalar
                def _(act):
                    self.ln_scalar_sqrt(act, ln)
                    self.split_scalar(act, ln, xT, scaled)
                    for m in range(2 * HP):
                        hp, f = divmod(m, 2)
                        act.wait_ge(s["q_ready"], m + 1)
                        nc.scalar.activation(self.qoT[:, hp, f * HALF:(f + 1) * HALF], ps[m % 8][:, 0:HALF], ACT.Copy, scale=DH ** -0.5).then_inc(s["kept"], 1)

                @block.vector
                def _(dve):
                    self.ln_vector(dve, ln, self.X, xn)
                    dve.wait_ge(s["loaded"], 16)
                    self.split_vector(dve, ln, xT, scaled, gb[:, 0], gb[:, 1])

                @block.tensor
                def _(pe):
                    self.turn_tensor(pe, ln, xn)
                    pe.wait_ge(ln["lo_ready"], 4)
                    for m in range(2 * HP):
                        hp, f = divmod(m, 2)
                        if m >= 8:
                            pe.wait_ge(s["kept"], m - 7)
                        for k in range(KT):
                            last = self.mm(ps[m % 8][:, 0:HALF], cut(wq, slice(None), k, tile(hp)), cut(xT, slice(None), k, slice(f * HALF, (f + 1) * HALF)),
                                           k == 0, k == KT - 1)
                        last.then_inc(s["q_ready"], 1)

    def gated_ffn(self):
        nc, a, ps, X = self.nc, self.a, self.ps, self.X
        with Stage(nc, "ef") as st:
            w1, w2 = self.w1, self.ahead_as(a=8)
            hid = st.pair("hid", [P, 8, N])
            plain = st.sb("plain", [P, 2, HALF])
            gate = st.sb("gate", [P, 2, HALF])
            f = self.ffn_sems(st, "ffn")
            s = st.sems_of("ahead_loaded", "ahead_split", "cleared", "q_placed")
            with nc.Block() as block:
                @block.sync
                def _(sp):
                    self.ahead_load(sp, s, a["L1_w2"])

                @block.gpsimd
                def _(pool):
                    self.ahead_split(pool, s)
                    nc.gpsimd.memset(self.qz[:, :, :], 0.0).then_inc(s["cleared"], 1)
                    pool.wait_ge(s["cleared"], 1)
                    for h in range(2):
                        rows = slice(h * DH, (h + 1) * DH)
                        nc.gpsimd.tensor_copy(self.qz[rows, h:H:2, :], self.qoT[rows, :, 0:S]).then_inc(s["q_placed"], 1)
                        pool.wait_ge(s["q_placed"], h + 1)

                @block.scalar
                def _(act):
                    self.ffn_scalar(act, f, 0, ACT.Silu, plain, gate)

                @block.vector
                def _(dve):
                    dve.sem_inc(f["y_used"], 1)
                    self.ffn_vector(dve, f, 0, plain, gate, hid)
                    for t in range(NT):
                        dve.wait_ge(f["y_ready"], t + 1)
                        nc.vector.tensor_tensor(X[:, t], X[:, t], ps[4 + t % 4][:, 0:D], ALU.add).then_inc(f["y_used"], 1)

                @block.tensor
                def _(pe):
                    self.ffn_tensor(pe, f, 0, self.xT1, lambda n, k, ft: cut(w1, slice(None), k, slice(n * INNER + ft * P, n * INNER + (ft + 1) * P)),
                                    True, hid, w2, lambda: pe.wait_ge(s["ahead_split"], 2))

    def multi_attention(self):
        nc, ps, qoT, qz, oT = self.nc, self.ps, self.qoT, self.qz, self.oT
        with Stage(nc, "em") as st:
            p = st.sb("p", [S, 4, S2])
            mask = st.sb("mask", [S, S2])
            mx = st.sb("mx", [S, H])
            sm = st.sb("sm", [S, H])
            pT = st.sb("pT", [CP, 4, CH, S])
            on = st.sb("on", [S, 2, 512])
            s = st.sems_of("ahead_loaded", "ahead_split", "begun", "q_placed", "oT_lo", "seen", "s_ready", "shifted", "exps", "turned", "pT_a", "pT_d",
                                                      "o_ready", "chain", "o_norm", "oT_ready", "oT_kept")
            with nc.Block() as block:
                @block.sync
                def _(sp):
                    self.ahead_load(sp, s, self.a["L1_wo"])

                @block.gpsimd
                def _(pool):
                    def place(b):
                        for h in range(2):
                            rows = slice(h * DH, (h + 1) * DH)
                            nc.gpsimd.tensor_copy(qz[rows, h:H:2, :], qoT[rows, :, bass.ds(b * S, S)]).then_inc(s["q_placed"], 1)
                            pool.wait_ge(s["q_placed"], 2 * b + h + 1)
                            pool.sem_inc(s["begun"], 1)

                    def low(b, n):
                        at = (slice(None), slice(4 * n, 4 * n + 4), bass.ds(b * S, S))
                        pool.wait_ge(s["oT_kept"], 2 * (2 * b + n) + 3)
                        nc.gpsimd.tensor_tensor(oT[1][at], qoT[at], oT[0][at].bitcast(F32), ALU.subtract).then_inc(s["oT_lo"], 1)

                    pool.sem_inc(s["q_placed"], 2)
                    self.ahead_split(pool, s)
                    with pool.Fori(0, B - 1) as i:
                        low(i, 0)
                        pool.wait_ge(s["s_ready"], H * i + H)
                        pool.sem_inc(s["begun"], 1)
                        place(i + 1)
                        low(i, 1)
                    low(B - 1, 0)
                    low(B - 1, 1)

                @block.scalar
                def _(act):
                    act.sem_inc(s["oT_kept"], 1)

                    def body(i):
                        def exp(h):
                            act.wait_ge(s["shifted"], H * i + h + 1)
                            nc.scalar.activation(p[:, h % 4], p[:, h % 4], ACT.Exp, bias=mx[:, h:h + 1], scale=-1.0,
                                                 accum_out=sm[:, h:h + 1]).then_inc(s["exps"], 1)

                        def keep(n):
                            act.wait_ge(s["oT_ready"], 2 * i + n + 1)
                            for to in (oT[0], qoT):
                                nc.scalar.activation(to[:, 4 * n:4 * n + 4, bass.ds(i * S, S)],
                                                     ps[7][:, 0:4 * S].rearrange("p (a b) -> p a b", b=S), ACT.Copy).then_inc(s["oT_kept"], 1)

                        exp(0)
                        for h in range(H):
                            if h + 1 < H:
                                exp(h + 1)
                            if h % 2 == 0:
                                act.wait_ge(s["turned"], H * i + h + 1)
                                nc.scalar.activation(pT[:, h % 4], ps[3 + h % 2][0:CP, 0:CH * S].rearrange("p (c i) -> p c i", i=S), ACT.Copy).then_inc(s["pT_a"], 1)
                            if h == 11:
                                keep(0)
                        keep(1)

                    with act.Fori(0, B) as i:
                        body(i)

                @block.vector
                def _(dve):
                    c = Chain(dve, s["chain"])
                    dve.wait_ge(self.mask_loaded, 16)

                    def body(i):
                        def shift(h):
                            dve.wait_ge(s["s_ready"], H * i + h + 1)
                            dve.sem_inc(s["seen"], 1)
                            nc.vector.tensor_tensor_reduce(out=p[:, h % 4], in0=ps[h % 3][0:S, 0:S2], in1=mask[:, :],
                                                           scale=-1.0, scalar=3.0e38, op0=ALU.add, op1=ALU.min, accum_out=mx[:, h:h + 1]).then_inc(s["shifted"], 1)

                        def norm(n):
                            dve.wait_ge(s["o_ready"], 2 * i + n + 1)
                            c.link(nc.vector.reciprocal(sm[:, 8 * n:8 * n + 8], sm[:, 8 * n:8 * n + 8]))
                            nc.vector.tensor_tensor(on[:, n].rearrange("p (h d) -> p h d", d=DH), ps[5 + n][0:S, :].rearrange("p (h d) -> p h d", d=DH),
                                                    sm[:, 8 * n:8 * n + 8].unsqueeze(2).to_broadcast([S, 8, DH]), ALU.mult).then_inc(s["o_norm"], 1)

                        c.link(nc.vector.tensor_copy(mask[:, :].unsqueeze(1), self.masks[:, bass.ds(i, 1), :]))
                        shift(0)
                        shift(1)
                        for h in range(H):
                            if h + 2 < H:
                                shift(h + 2)
                            if h % 2:
                                dve.wait_ge(s["turned"], H * i + h + 1)
                                nc.vector.tensor_copy(pT[:, h % 4], ps[3 + h % 2][0:CP, 0:CH * S].rearrange("p (c i) -> p c i", i=S)).then_inc(s["pT_d"], 1)
                            if h == 9:
                                norm(0)
                        norm(1)

                    with dve.Fori(0, B) as i:
                        c.enter(i, 3)
                        body(i)
                        c.leave(B)

                @block.tensor
                def _(pe):
                    def body(i):
                        def score(h):
                            nc.tensor.matmul(ps[h % 3][0:S, 0:S2], qz[:, h, :], self.k1T[:, bass.ds(i * S2, S2)], start=True, stop=True).then_inc(s["s_ready"], 1)

                        def turn(h):
                            pe.wait_ge(s["exps"], H * i + h + 1)
                            for m in range(CH):
                                last = nc.tensor.transpose(ps[3 + h % 2][0:CP, m * S:(m + 1) * S], p[:, h % 4, m * CP:(m + 1) * CP], self.ident[0:S, 0:S])
                            last.then_inc(s["turned"], 1)

                        def mix(h):
                            if h % 2:
                                pe.wait_ge(s["pT_d"], 8 * i + h // 2 + 1)
                            else:
                                pe.wait_ge(s["pT_a"], 8 * i + h // 2 + 1)
                            for m in range(CH):
                                last = nc.tensor.matmul(ps[5 + h // 8][0:S, (h % 8) * DH:(h % 8 + 1) * DH], pT[:, h % 4, m, :],
                                                        self.v1[:, bass.ds(i * CH + m, 1), :].rearrange("p o d -> p (o d)"), start=m == 0, stop=m == CH - 1)
                            if h % 8 == 7:
                                last.then_inc(s["o_ready"], 1)

                        def back(n):
                            pe.wait_ge(s["o_norm"], 2 * i + n + 1)
                            pe.wait_ge(s["oT_kept"], 2 * (2 * i + n) + 1)
                            for m in range(4):
                                last = nc.tensor.transpose(ps[7][:, m * S:(m + 1) * S], on[:, n, tile(m)], self.ident[0:S, 0:S])
                            last.then_inc(s["oT_ready"], 1)

                        pe.wait_ge(s["q_placed"], 2 * i + 2)
                        score(0)
                        score(1)
                        for h in range(H):
                            if h + 2 < H:
                                score(h + 2)
                            turn(h)
                            if h:
                                mix(h - 1)
                            if h == 11:
                                back(0)
                        mix(H - 1)
                        back(1)

                    with pe.Fori(0, B) as i:
                        body(i)

    def multi_output(self):
        nc, ps, X = self.nc, self.ps, self.X
        with Stage(nc, "eo") as st:
            s = st.sems_of("y_ready", "x_added")
            with nc.Block() as block:
                @block.vector
                def _(dve):
                    for t in range(NT):
                        dve.wait_ge(s["y_ready"], t + 1)
                        nc.vector.tensor_tensor(X[:, t], X[:, t], ps[t][:, 0:D], ALU.add).then_inc(s["x_added"], 1)

                @block.tensor
                def _(pe):
                    self.project(pe, self.oT, self.ahead_as(a=HP), s["y_ready"])

    def l1_experts(self):
        nc, a, ps, X = self.nc, self.a, self.ps, self.X
        E = 8
        W1 = KT * INNER
        with Stage(nc, "f") as st:
            xT = st.pair("xT", [P, KT, N])
            xn = st.sb("xn", [P, NT, D])
            raw1 = st.sb("raw1", [P, W1 + 8])
            raw2 = st.sb("raw2", [P, 8 * D])
            w1 = st.pair("w1", [P, W1])
            w2 = st.pair("w2", [P, 8, D])
            b1 = st.sb("b1", [P, 8])
            b2 = st.sb("b2", [E, D])
            graw = st.sb("graw", [P, KT, E])
            gw = st.pair("gw", [P, KT, E])
            gbias = st.sb("gbias", [P, E])
            temp = st.sb("temp", [P, 1])
            lt = st.sb("lt", [P, 16, 16])
            logit = st.sb("logit", [P, NT, E])
            more = st.sb("more", [P, NT, E, E])
            same = st.sb("same", [P, NT, E, E])
            rank = st.sb("rank", [P, NT, E])
            top = st.sb("top", [P, NT])
            share = st.sb("share", [P, NT, E])
            shareT = st.sb("shareT", [E, N])
            col = st.sb("col", [P, NT])
            plain = st.sb("plain", [P, 2, HALF])
            hid = st.pair("hid", [P, 8, N])
            ln = self.ln_buffers(st)
            f = self.ffn_sems(st, "ffn")
            s = st.sems_of("c_loaded", "loaded1", "loaded2", "split1", "split2", "b1_kept", "begun", "g_split", "logit",
                                                      "shifted", "exps", "chain", "shared", "sh_turned", "sh_kept", "bias_ready", "bias_added")
            with nc.Block() as block:
                @block.sync
                def _(sp):
                    sp.dma_start(graw[:, :, :], a["L1_gate"]).then_inc(s["c_loaded"], 16)
                    sp.dma_start(gbias[:, :], a["L1_ffn_gate_b"].partition_broadcast(P)).then_inc(s["c_loaded"], 16)
                    sp.dma_start(temp[:, :], a["temperature"].partition_broadcast(P)).then_inc(s["c_loaded"], 16)
                    sp.dma_start(lt[:, :, :], a["lower"].partition_broadcast(P)).then_inc(s["c_loaded"], 16)
                    sp.dma_start(b2[:, :], a["L1_ffn_b2"]).then_inc(s["c_loaded"], 16)
                    sp.dma_start(raw1[:, :], a["L1_e1"][0]).then_inc(s["loaded1"], 16)
                    sp.dma_start(raw2[:, :], a["L1_e2"][0]).then_inc(s["loaded2"], 16)
                    with sp.Fori(0, E - 1) as i:
                        sp.wait_ge(s["b1_kept"], i + 1)
                        sp.dma_start(raw1[:, :], a["L1_e1"][bass.ds(i + 1, 1)].rearrange("o p w -> (o p) w")).then_inc(s["loaded1"], 16)
                        sp.wait_ge(s["split2"], 2 * i + 2)
                        sp.dma_start(raw2[:, :], a["L1_e2"][bass.ds(i + 1, 1)].rearrange("o p w -> (o p) w")).then_inc(s["loaded2"], 16)

                @block.gpsimd
                def _(pool):
                    pool.wait_ge(s["c_loaded"], 80)
                    self.split_pool(pool, s["g_split"], graw[:, :, :], cut(gw, slice(None)), 0)

                    def first(e):
                        pool.wait_ge(s["loaded1"], 16 * e + 16)
                        pool.sem_inc(s["begun"], 1)
                        self.split_pool(pool, s["split1"], raw1[:, 0:W1], cut(w1, slice(None)), e)
                        nc.gpsimd.tensor_copy(b1[:, :], raw1[:, W1:W1 + 8]).then_inc(s["b1_kept"], 1)

                    def second(e):
                        pool.wait_ge(s["loaded2"], 16 * e + 16)
                        pool.sem_inc(s["begun"], 1)
                        self.split_pool(pool, s["split2"], raw2[:, :], tuple(x[:, :, :].rearrange("p a b -> p (a b)") for x in w2), e)

                    first(0)
                    second(0)
                    with pool.Fori(0, E - 1) as i:
                        pool.wait_ge(f["plain_done"], 16 * i + 16)
                        first(i + 1)
                        pool.wait_ge(f["y_ready"], NT * i + NT)
                        second(i + 1)

                @block.scalar
                def _(act):
                    self.ln_scalar_sqrt(act, ln)
                    self.split_scalar(act, ln, xT)
                    act.wait_ge(s["shifted"], 1)
                    nc.scalar.activation(logit[:, :, :], logit[:, :, :], ACT.Exp).then_inc(s["exps"], 1)
                    for g in range(2):
                        act.wait_ge(s["sh_turned"], g + 1)
                        n = min(512, N - 512 * g)
                        nc.scalar.activation(shareT[:, 512 * g:512 * g + n], ps[g][0:E, 0:n], ACT.Copy).then_inc(s["sh_kept"], 1)
                    with act.Fori(0, E) as i:
                        act.wait_ge(s["b1_kept"], i + 1)
                        self.ffn_scalar(act, f, i, ACT.Gelu, plain, None, b1)

                @block.vector
                def _(dve):
                    dve.sem_inc(f["y_used"], 1)
                    self.ln_vector(dve, ln, X, xn)
                    self.split_vector(dve, ln, xT)
                    c = Chain(dve, s["chain"])
                    dve.wait_ge(s["c_loaded"], 80)
                    dve.wait_ge(s["logit"], 1)
                    c.link(nc.vector.tensor_tensor(logit[:, :, :], ps[7][:, 0:NT * E].rearrange("p (t e) -> p t e", e=E),
                                                   gbias[:, :].unsqueeze(1).to_broadcast([P, NT, E]), ALU.add))
                    c.link(nc.vector.reciprocal(temp[:, :], temp[:, :]))
                    c.link(nc.vector.tensor_scalar(logit[:, :, :], logit[:, :, :], temp[:, 0:1], None, ALU.mult))
                    self.rank(dve, c, logit[:, :, :], lt, E, more, same, rank[:, :, :])
                    c.link(nc.vector.tensor_reduce(top[:, :], logit[:, :, :], AX, ALU.max))
                    nc.vector.tensor_tensor(logit[:, :, :], logit[:, :, :], top[:, :].unsqueeze(2).to_broadcast([P, NT, E]), ALU.subtract).then_inc(s["shifted"], 1)
                    dve.wait_ge(s["exps"], 1)
                    c.link(nc.vector.tensor_scalar(rank[:, :, :], rank[:, :, :], 2.0, None, ALU.is_lt))
                    c.link(nc.vector.tensor_tensor(share[:, :, :], rank[:, :, :], logit[:, :, :], ALU.mult))
                    c.link(nc.vector.tensor_reduce(top[:, :], share[:, :, :], AX, ALU.add))
                    c.link(nc.vector.reciprocal(top[:, :], top[:, :]))
                    nc.vector.tensor_tensor(share[:, :, :], share[:, :, :], top[:, :].unsqueeze(2).to_broadcast([P, NT, E]), ALU.mult).then_inc(s["shared"], 1)
                    for t in range(NT):
                        dve.wait_ge(s["bias_ready"], t + 1)
                        nc.vector.tensor_tensor(X[:, t], X[:, t], ps[2 + t % 4][:, 0:D], ALU.add).then_inc(s["bias_added"], 1)
                    dve.wait_ge(s["bias_added"], NT)
                    dve.wait_ge(s["shared"], 1)
                    with dve.Fori(0, E) as i:
                        c.enter(i, 1)
                        dve.wait_ge(f["y_used"], NT * i + 1)
                        c.link(nc.vector.tensor_copy(col[:, :].unsqueeze(2), share[:, :, bass.ds(i, 1)]))
                        self.ffn_vector(dve, f, i, plain, None, hid)
                        for t in range(NT):
                            dve.wait_ge(f["y_ready"], NT * i + t + 1)
                            dve.wait_ge(f["y_used"], NT * i + 1)
                            nc.vector.scalar_tensor_tensor(out=X[:, t], in0=ps[4 + t % 4][:, 0:D], scalar=col[:, t:t + 1], in1=X[:, t],
                                                           op0=ALU.mult, op1=ALU.add).then_inc(f["y_used"], 1)
                        c.leave(E)

                @block.tensor
                def _(pe):
                    self.turn_tensor(pe, ln, xn)
                    pe.wait_ge(ln["lo_ready"], 4)
                    pe.wait_ge(s["g_split"], 2)
                    self.logits(pe, xT, gw, E, s["logit"])
                    pe.wait_ge(s["shared"], 1)
                    for t in range(NT):
                        last = nc.tensor.transpose(ps[t // 4][0:E, tile(t % 4)], share[:, t, :], self.ident[:, :])
                        if t in (3, NT - 1):
                            last.then_inc(s["sh_turned"], 1)
                    pe.wait_ge(s["sh_kept"], 2)
                    for t in range(NT):
                        if t >= 4:
                            pe.wait_ge(s["bias_added"], t - 3)
                        nc.tensor.matmul(ps[2 + t % 4][:, 0:D], shareT[:, tile(t)], b2[:, :], start=True, stop=True).then_inc(s["bias_ready"], 1)
                    pe.wait_ge(s["bias_added"], NT)
                    with pe.Fori(0, E) as i:
                        pe.wait_ge(s["split1"], 2 * i + 2)
                        self.ffn_tensor(pe, f, i, xT, lambda n, k, ft: cut(w1, slice(None), slice(k * INNER + ft * P, k * INNER + (ft + 1) * P)),
                                        False, hid, w2, lambda: pe.wait_ge(s["split2"], 2 * i + 2))


STOP = 6


def _pos_enc():
    position = np.arange(S, dtype=np.float32)[:, None]
    div = np.exp(np.arange(0, DH, 2, dtype=np.float32) * np.float32(-(np.log(10000.0) / DH)))
    pe = np.zeros((S, DH), np.float32)
    pe[:, 0::2] = np.sin(position * div)
    pe[:, 1::2] = np.cos(position * div)
    return np.ascontiguousarray(np.concatenate([pe.T, pe.T], 0))


def _ktiles(w):
    return w.reshape(-1, P, w.shape[-1]).transpose(1, 0, 2)


def kernel(**inputs):
    import concourse.bacc as bacc
    from concourse.bass_utils import run_bass_kernel_spmd

    i = {k: np.asarray(v) for k, v in inputs.items()}
    wqkv = i["L0_attn_W_qkv"].reshape(KT, P, 3, HP, P).transpose(3, 1, 0, 2, 4).reshape(HP, P, KT * 3 * P)
    bqkv = i["L0_attn_b_qkv"].reshape(3, HP, P)
    arrays = {
        "x": i["x"].reshape(N, D),
        "L0_qkv": np.concatenate([wqkv, bqkv[0][:, :, None], bqkv[1][:, :, None]], 2),
        "L0_bv": bqkv[2],
        "L0_attn_b_out": i["L0_attn_b_out"],
        "L0_wo": _ktiles(i["L0_attn_W_out"]),
        "pos": _pos_enc(),
    }
    def gs(g, b):
        return np.stack([i[g].reshape(KT, P).T, i[b].reshape(KT, P).T], 1)

    experts = np.concatenate([
        np.stack([i["L0_ffn_sw_gate"].reshape(KT, P, 2, P).transpose(2, 1, 0, 3), i["L0_ffn_sw_up"].reshape(KT, P, 2, P).transpose(2, 1, 0, 3)], 3),
        np.stack([i["L0_ffn_w_gate"].reshape(16, KT, P, P).transpose(0, 2, 1, 3), i["L0_ffn_w_up"].reshape(16, KT, P, P).transpose(0, 2, 1, 3)], 3),
    ], 0).reshape(18, P, 4 * P)
    down = np.concatenate([i["L0_ffn_sw_down"].reshape(2, P, D), i["L0_ffn_w_down"]], 0)
    arrays.update({
        "ctx": i["ctx_1024"].reshape(B, CH, CP, D).transpose(0, 2, 1, 3),
        "mask": i["mask_BxSxS2_ff0"],
        "L0_ln1": gs("L0_xattn_ln1_g", "L0_xattn_ln1_b"),
        "L0_ln2": gs("L0_xattn_ln2_g", "L0_xattn_ln2_b"),
        "L1_cln": gs("L1_xattn_cln_g", "L1_xattn_cln_b"),
        "L1_ln": gs("L1_xattn_ln_g", "L1_xattn_ln_b"),
        "L0_wq": _ktiles(i["L0_xattn_wq"]), "L0_wk": _ktiles(i["L0_xattn_wk"]), "L0_wv": _ktiles(i["L0_xattn_wv"]),
        "L0_xwo": _ktiles(i["L0_xattn_wo"]).reshape(P, -1), "L0_w1": _ktiles(i["L0_xattn_w1"]).reshape(P, -1),
        "L0_w2": _ktiles(i["L0_xattn_w2"]).reshape(P, -1),
        "L0_b1": i["L0_xattn_b1"].reshape(8, P).T, "L0_xattn_bo": i["L0_xattn_bo"], "L0_xattn_b2": i["L0_xattn_b2"],
        "L1_wkv": _ktiles(np.concatenate([i["L1_xattn_Wkv"][:, :DH], i["L1_xattn_Wkv"]], 1)),
        "L0_gate": _ktiles(i["L0_ffn_gate_kernel"]), "L0_ffn_gate_bias": i["L0_ffn_gate_bias"],
        "L0_experts": np.concatenate([experts, down], 2),
        "lower": np.tril(np.ones((16, 16), np.float32), -1),
        "L1_wqv": _ktiles(np.concatenate([i["L1_attn_Wq"].T, i["L1_attn_Wv"].T], 1)),
        "L1_norm_w": np.stack([i["L1_attn_q_norm_w"].reshape(-1), i["L1_attn_v_norm_w"].reshape(-1)]),
        "own": np.repeat(np.where(np.arange(P)[:, None] // 16 == np.arange(8)[None, :], np.float32(1), np.float32(0))[:, :, None], S, 2),
        "causal": np.triu(np.ones((S, S), np.float32)),
        "L1_wq": _ktiles(i["L1_xattn_Wq"]),
        "L1_w1": _ktiles(i["L1_xattn_W1"]), "L1_w2": _ktiles(i["L1_xattn_W2"]).reshape(P, -1),
        "L1_wo": _ktiles(i["L1_xattn_Wout"]).reshape(P, -1),
        "L1_e1": np.concatenate([i["L1_ffn_W1"].reshape(8, KT, P, 1024).transpose(0, 2, 1, 3).reshape(8, P, -1),
                                 i["L1_ffn_b1"].reshape(8, 8, P).transpose(0, 2, 1)], 2),
        "L1_e2": i["L1_ffn_W2"].reshape(8, 8, P, D).transpose(0, 2, 1, 3).reshape(8, P, -1),
        "L1_gate": _ktiles(i["L1_ffn_gate_w"]), "L1_ffn_gate_b": i["L1_ffn_gate_b"], "L1_ffn_b2": i["L1_ffn_b2"],
        "temperature": i["L1_ffn_temperature"].reshape(1),
    })
    nc = bacc.Bacc("TRN2", target_bir_lowering=False, num_devices=1)
    arrays = {k: np.ascontiguousarray(v) for k, v in arrays.items()}
    aps = {k: nc.dram_tensor(k, v.shape, F32, kind="ExternalInput").ap() for k, v in arrays.items()}
    aps["spill"] = nc.dram_tensor("spill", (N, D), F32, kind="Internal").ap()
    aps["out"] = nc.dram_tensor("out", (N, D), F32, kind="ExternalOutput").ap()
    Kernel(nc, aps, STOP).build()
    r = run_bass_kernel_spmd(nc, [arrays], core_ids=[0])
    return r.results[0]["out"].reshape(B, S, D)
```

```python
from contextlib import ExitStack

import numpy as np

import concourse.bass as bass
from concourse import mybir

F32 = mybir.dt.float32
F32R = mybir.dt.float32r
ALU = mybir.AluOpType
ACT = mybir.ActivationFunctionType
AX = mybir.AxisListType.X

P = 128
B, S, D = 8, 112, 256
N = B * S
NT = N // P
HALF = N // 2
KT = D // P
S2 = 375
S2E = S2 + S2 % 2
CH, CP = 3, 125
H, DH = 16, 64
HP = H // 2
INNER = H * DH
EPS = 1e-5


def tile(t):
    return slice(t * P, (t + 1) * P)


class Chain:

    def __init__(self, eng, sem):
        self.eng, self.sem, self.n, self.off = eng, sem, 0, 0

    def link(self, ins):
        self.n += 1
        ins.then_inc(self.sem, 1)
        self.eng.wait_ge(self.sem, self.off + self.n)

    def enter(self, i, per):
        self.n0, self.per, self.off = self.n, per, i * per

    def leave(self, count):
        assert self.n - self.n0 == self.per, (self.n - self.n0, self.per)
        self.n, self.off = self.n0 + self.per * count, 0


class Stage:

    def __init__(self, nc, name):
        self.nc, self.name, self.ctx, self.sems = nc, name, ExitStack(), []

    def __enter__(self):
        self.ctx.__enter__()
        return self

    def __exit__(self, *a):
        if self.sems and a[0] is None:
            self.nc.clear_and_free_semaphores(self.sems)
            self.nc.all_engine_barrier()
        return self.ctx.__exit__(*a)

    def sb(self, name, shape, dt=F32):
        return self.ctx.enter_context(self.nc.sbuf_tensor(f"{self.name}_{name}", shape, dt))

    def pair(self, name, shape):
        return (self.sb(name + "_hi", shape, F32R), self.sb(name + "_lo", shape, F32R))

    def sem(self, name):
        self.sems.append(self.nc.alloc_semaphore(name=f"{self.name}_{name}"))
        return self.sems[-1]

    def sems_of(self, *names, prefix="", **more):
        return {n: self.sem(prefix + n) for n in names} | more

    def block(self):
        return self.nc.Block()


def cut(pair, *index):
    return tuple(x[index] for x in pair)


class Kernel:
    def __init__(self, nc, a, stop):
        self.nc, self.a, self.stop = nc, a, stop

    def mm(self, out, left, right, start, stop):
        te = self.nc.tensor
        if isinstance(left, tuple):
            (lh, ll), (rh, rl) = left, right
            te.matmul(out, lh, rh, start=start, stop=False)
            te.matmul(out, lh, rl, start=False, stop=False)
            return te.matmul(out, ll, rh, start=False, stop=stop)
        return te.matmul(out, left, right, start=start, stop=stop)

    def ln_buffers(self, st, name="ln"):
        return st.sems_of("chain", "var_ready", "std_ready", "norm_ready", "turned", "hi_ready", "lo_ready", "affine_ready", prefix=name + "_",
                          stats=st.sb(name + "_stats", [P, NT, 6]), mv=st.sb(name + "_mv", [P, NT, 2]),
                          std=st.sb(name + "_std", [P, NT]), rstd=st.sb(name + "_rstd", [P, NT]))

    def ln_vector(self, dve, o, x, xn, after=None):
        nc = self.nc
        o["c"] = Chain(dve, o["chain"])
        for t in range(NT):
            if after:
                after(t)
            last = nc.vector.bn_stats(o["stats"][:, t, :], x[:, t, :])
        o["c"].link(last)
        for t in range(NT):
            last = nc.vector.bn_aggr(o["mv"][:, t, :], o["stats"][:, t, :])
        o["c"].link(last)
        nc.vector.tensor_scalar(o["std"][:, :], o["mv"][:, :, 1], EPS, None, ALU.add).then_inc(o["var_ready"], 1)
        dve.wait_ge(o["std_ready"], 1)
        o["c"].link(nc.vector.reciprocal(o["rstd"][:, :], o["std"][:, :]))
        for t in range(NT):
            nc.vector.tensor_scalar(xn[:, t, :], x[:, t, :], o["mv"][:, t, 0:1], o["rstd"][:, t:t + 1],
                                    ALU.subtract, ALU.mult).then_inc(o["norm_ready"], 1)

    def ln_scalar_sqrt(self, act, o):
        act.wait_ge(o["var_ready"], 1)
        self.nc.scalar.activation(o["std"][:, :], o["std"][:, :], ACT.Sqrt).then_inc(o["std_ready"], 1)

    def turn_tensor(self, pe, o, xn):
        pe.wait_ge(self.ident_ready, 2)
        for g in range(2):
            for t in range(4 * g, min(4 * g + 4, NT)):
                pe.wait_ge(o["norm_ready"], t + 1)
                for k in range(KT):
                    last = self.nc.tensor.transpose(self.ps[4 + 2 * k + g][:, tile(t % 4)], xn[:, t, tile(k)], self.ident[:, :])
            last.then_inc(o["turned"], 1)

    def turn_pieces(self):
        for g in range(2):
            cols = slice(512 * g, min(512 * g + 512, N))
            for k in range(KT):
                yield g, k, cols, self.ps[4 + 2 * k + g][:, 0:cols.stop - cols.start]

    def split_scalar(self, act, o, xT, plain=None):
        for n, (g, k, cols, src) in enumerate(self.turn_pieces()):
            if plain is None:
                act.wait_ge(o["turned"], g + 1)
            else:
                act.wait_ge(o["affine_ready"], n + 1)
                src = plain[:, k, cols]
            self.nc.scalar.activation(xT[0][:, k, cols], src, ACT.Copy).then_inc(o["hi_ready"], 1)

    def split_vector(self, dve, o, xT, plain=None, gain=None, shift=None):
        nc = self.nc
        pieces = list(enumerate(self.turn_pieces()))
        for group in (pieces[:KT], pieces[KT:]):
            if plain is not None:
                for n, (g, k, cols, src) in group:
                    dve.wait_ge(o["turned"], g + 1)
                    nc.vector.tensor_scalar(plain[:, k, cols], src, gain[:, k:k + 1], shift[:, k:k + 1],
                                            ALU.mult, ALU.add).then_inc(o["affine_ready"], 1)
            for n, (g, k, cols, src) in group:
                dve.wait_ge(o["hi_ready"], n + 1)
                if plain is not None:
                    dve.wait_ge(o["affine_ready"], n + 1)
                    src = plain[:, k, cols]
                nc.vector.tensor_tensor(xT[1][:, k, cols], src, xT[0][:, k, cols].bitcast(F32),
                                        ALU.subtract).then_inc(o["lo_ready"], 1)

    def split_pool(self, pool, ready, raw, pair, index):
        nc = self.nc
        nc.gpsimd.tensor_copy(pair[0], raw).then_inc(ready, 1)
        pool.wait_ge(ready, 2 * index + 1)
        nc.gpsimd.tensor_tensor(pair[1], raw, pair[0].bitcast(F32), ALU.subtract).then_inc(ready, 1)

    def build(self):
        nc = self.nc
        with Stage(nc, "g") as g:
            self.ps = [g.ctx.enter_context(nc.psum_tensor(f"bank{i}", [P, 512], F32)) for i in range(8)]
            self.X = g.sb("x", [P, NT, D])
            self.ident = g.sb("ident", [P, P])
            self.k1T = g.pair("k1T", [P, B * S2E])
            self.v1 = g.sb("v1", [CP, B * CH, DH])
            self.ident_ready = g.sem("ident_ready")
            self.x_loaded = g.sem("x_loaded")
            self.stored = g.sem("stored")
            self.prepare()
            with Stage(nc, "n0") as ahead:
                self.ahead_buffers(ahead)
                self.l0_attention()
                if self.stop > 1:
                    self.l0_cross_attention()
            if self.stop > 2:
                self.l0_experts()
            if self.stop > 3:
                with Stage(nc, "n1") as ahead:
                    self.ahead_buffers(ahead)
                    self.l1_attention()
                    if self.stop > 4:
                        self.l1_cross_attention()
            if self.stop > 5:
                self.l1_experts()
            self.finish()

    def ahead_buffers(self, st):
        self.ahead_raw = st.sb("raw", [P, 2 * INNER])
        self.ahead = st.pair("w", [P, 2 * INNER])

    def ahead_load(self, sp, s, src):
        sp.dma_start(self.ahead_raw[:, :], src).then_inc(s["ahead_loaded"], 16)

    def ahead_split(self, pool, s):
        pool.wait_ge(s["ahead_loaded"], 16)
        self.split_pool(pool, s["ahead_split"], self.ahead_raw[:, :], cut(self.ahead, slice(None)), 0)

    def ahead_as(self, **dims):
        return tuple(x[:, :].rearrange("p (a b) -> p a b", **dims) for x in self.ahead)

    def prepare(self):
        nc = self.nc
        with nc.Block() as block:
            @block.sync
            def _(sp):
                sp.dma_start(self.X[:, :, :], self.a["x"].rearrange("(t p) f -> p t f", p=P)).then_inc(self.x_loaded, 16)

            @block.gpsimd
            def _(pool):
                nc.gpsimd.memset(self.ident[:, :], 0.0).then_inc(self.ident_ready, 1)
                pool.wait_ge(self.ident_ready, 1)
                nc.gpsimd.affine_select(out=self.ident[:, :], in_=self.ident[:, :], compare_op=ALU.not_equal, fill=1.0,
                                        base=0, pattern=[[-1, P]], channel_multiplier=1).then_inc(self.ident_ready, 1)

    def finish(self):
        nc = self.nc
        with nc.Block() as block:
            @block.sync
            def _(sp):
                sp.wait_ge(self.x_loaded, 16)
                sp.dma_start(self.a["out"].rearrange("(t p) f -> p t f", p=P), self.X[:, :, :]).then_inc(self.stored, 16)
                sp.wait_ge(self.stored, 16)

    def l0_attention(self):
        nc, a, ps, X = self.nc, self.a, self.ps, self.X
        G = 4
        W = 3 * D
        with Stage(nc, "a") as st:
            xT = st.pair("xT", [P, KT, N])
            raw = st.sb("raw", [P, W + 3])
            w = st.pair("w", [P, W])
            bias = st.sb("bias", [P, 2, 3])
            pos = st.sb("pos", [P, S])
            woraw = st.sb("woraw", [P, HP, D])
            wo = st.pair("wo", [P, HP, D])
            bo = st.sb("bo", [P, D])
            oT = st.pair("oT", [P, HP, N])
            qT = st.sb("qT", [P, N])
            kz = st.sb("kz", [P, 2, N])
            v = st.sb("v", [S, 2, B, P])
            prob = st.sb("prob", [S, G, 4, S])
            probT = st.sb("probT", [S, G, 4, S])
            mx = st.sb("mx", [S, G, 4])
            rs = st.sb("rs", [S, G, 4])
            xn = st.sb("xn", [P, NT, D])
            ln = self.ln_buffers(st)
            s = st.sems_of(
                "w_loaded", "const_loaded", "wo_loaded", "split_begun", "w_split", "bias_kept", "wo_split", "kz_cleared", "qk_ready", "v_ready",
                "s_ready", "q_kept", "k_kept", "v_kept", "shifted", "exps", "rsum", "norm", "p_turned", "pT_kept",
                "pv_ready", "o_hi", "o_lo", "dchain", "y_ready", "x_added",
                "ahead_loaded", "ahead_split")

            def q_w(pair, k):
                return cut(pair, slice(None), slice(k * 384, k * 384 + 128))

            def k_w(pair, k):
                return cut(pair, slice(None), slice(k * 384 + 128, k * 384 + 256))

            def v_w(pair, k):
                return cut(pair, slice(None), slice(k * 384 + 256, k * 384 + 384))

            with st.block() as block:
                @block.sync
                def _(sp):
                    sp.dma_start(raw[:, :], a["L0_qkv"][0]).then_inc(s["w_loaded"], 16)
                    sp.dma_start(pos[:, :], a["pos"]).then_inc(s["const_loaded"], 16)
                    sp.dma_start(bo[:, :], a["L0_attn_b_out"].partition_broadcast(P)).then_inc(s["const_loaded"], 16)
                    sp.dma_start(woraw[:, :, :], a["L0_wo"]).then_inc(s["wo_loaded"], 16)
                    self.ahead_load(sp, s, a["L0_wq"].rearrange("p k n -> p (k n)"))
                    with sp.Fori(0, HP - 1) as i:
                        sp.wait_ge(s["bias_kept"], i + 1)
                        sp.dma_start(raw[:, :], a["L0_qkv"][bass.ds(i + 1, 1)].rearrange("o p w -> (o p) w")).then_inc(s["w_loaded"], 16)

                @block.gpsimd
                def _(pool):
                    nc.gpsimd.memset(kz[0:DH, 1, :], 0.0).then_inc(s["kz_cleared"], 1)
                    nc.gpsimd.memset(kz[DH:P, 0, :], 0.0).then_inc(s["kz_cleared"], 1)
                    pool.wait_ge(s["kz_cleared"], 2)

                    def split(hp, j, used=None):
                        pool.wait_ge(s["w_loaded"], (hp + 1) * 16)
                        pool.sem_inc(s["split_begun"], 1)
                        self.split_pool(pool, s["w_split"], raw[:, 0:W], cut(w, slice(None), slice(None)), hp)
                        if used is not None:
                            pool.wait_ge(s["o_lo"], used)
                            pool.sem_inc(s["split_begun"], 1)
                        nc.gpsimd.tensor_copy(bias[:, j], raw[:, W:W + 3]).then_inc(s["bias_kept"], 1)

                    def normalise(i):
                        for g in range(G):
                            pool.wait_ge(s["rsum"], G * i + g + 1)
                            nc.gpsimd.tensor_tensor(prob[:, g], prob[:, g], rs[:, g].unsqueeze(2).to_broadcast([S, 4, S]),
                                                    ALU.mult).then_inc(s["norm"], 1)

                    split(0, 0)
                    pool.wait_ge(s["wo_loaded"], 16)
                    self.split_pool(pool, s["wo_split"], woraw[:, :, :], cut(wo, slice(None)), 0)
                    pool.wait_ge(s["v_ready"], 2)
                    split(1, 1)
                    with pool.Fori(0, HP // 2 - 1) as p:
                        for j in range(2):
                            normalise(2 * p + j)
                            pool.wait_ge(s["v_ready"], 4 * p + 2 * j + 4)
                            split(2 * p + (j + 2), j, 4 * G * p + (2 * G * j + 2 * G + 1))
                    normalise(HP - 2)
                    normalise(HP - 1)
                    self.ahead_split(pool, s)

                @block.scalar
                def _(act):
                    self.ln_scalar_sqrt(act, ln)
                    self.split_scalar(act, ln, xT)

                    def keep_q(hp, j):
                        act.wait_ge(s["bias_kept"], hp + 1)
                        for f in range(2):
                            act.wait_ge(s["qk_ready"], 4 * hp + 2 + f + 1)
                            nc.scalar.activation(qT[:, f * HALF:(f + 1) * HALF], ps[f][:, 0:HALF], ACT.Identity,
                                                 bias=bias[:, j, 0:1]).then_inc(s["q_kept"], 1)

                    def keep_v(hp, j):
                        for f in range(2):
                            act.wait_ge(s["v_ready"], 2 * hp + f + 1)
                            nc.scalar.activation(v[:, j, 4 * f:4 * f + 4, :], ps[f][0:S, :].rearrange("p (b i) -> p b i", b=4),
                                                 ACT.Copy).then_inc(s["v_kept"], 1)

                    def exps(i, g):
                        act.wait_ge(s["shifted"], G * i + g + 1)
                        nc.scalar.activation(prob[:, g], prob[:, g], ACT.Exp, scale=DH ** -0.5).then_inc(s["exps"], 1)

                    def keep_pT(i, g):
                        act.wait_ge(s["p_turned"], G * i + g + 1)
                        nc.scalar.activation(probT[:, g], ps[4 + g][0:S, 0:HALF].rearrange("p (a b) -> p a b", b=S),
                                             ACT.Copy).then_inc(s["pT_kept"], 1)

                    def keep_o(i, j, g):
                        act.wait_ge(s["pv_ready"], G * i + g + 1)
                        for h in range(2):
                            rows = slice(h * DH, (h + 1) * DH)
                            src = ps[g][rows, 0:HALF].rearrange("p (b h i) -> p b h i", b=2, h=2)[:, :, h, :]
                            dst = oT[0][rows, bass.ds(i, 1), 2 * g * S:(2 * g + 2) * S].rearrange("p o (b i) -> p (o b) i", b=2)
                            nc.scalar.activation(dst, src, ACT.Identity, bias=bias[rows, j, 2:3]).then_inc(s["o_hi"], 1)

                    def body(i, j, more):
                        exps(i, 0)
                        exps(i, 1)
                        if more:
                            keep_q(i + 1, 1 - j)
                        exps(i, 2)
                        exps(i, 3)
                        if more:
                            keep_v(i + 1, 1 - j)
                        keep_pT(i, 0)
                        keep_pT(i, 1)
                        keep_o(i, j, 0)
                        keep_pT(i, 2)
                        keep_o(i, j, 1)
                        keep_pT(i, 3)
                        keep_o(i, j, 2)
                        keep_o(i, j, 3)

                    keep_q(0, 0)
                    keep_v(0, 0)
                    with act.Fori(0, HP // 2 - 1) as p:
                        body(2 * p, 0, True)
                        body(2 * p + 1, 1, True)
                    body(HP - 2, 0, True)
                    body(HP - 1, 1, False)

                @block.vector
                def _(dve):
                    dve.wait_ge(self.x_loaded, 16)
                    self.ln_vector(dve, ln, X, xn)
                    self.split_vector(dve, ln, xT)
                    dve.wait_ge(s["const_loaded"], 32)
                    c = Chain(dve, s["dchain"])
                    for t in range(NT):
                        last = nc.vector.tensor_tensor(X[:, t, :], X[:, t, :], bo[:, :], ALU.add)
                    c.link(last)

                    def keep_k(hp, j):
                        dve.wait_ge(s["bias_kept"], hp + 1)
                        for f in range(2):
                            dve.wait_ge(s["qk_ready"], 4 * hp + f + 1)
                            for h in range(2):
                                rows = slice(h * DH, (h + 1) * DH)
                                nc.vector.scalar_tensor_tensor(
                                    out=kz[rows, h, f * HALF:(f + 1) * HALF].rearrange("p (b i) -> p b i", b=4),
                                    in0=ps[2 + f][rows, 0:HALF].rearrange("p (b i) -> p b i", b=4),
                                    scalar=bias[rows, j, 1:2], in1=pos[rows, :].unsqueeze(1).to_broadcast([DH, 4, S]),
                                    op0=ALU.add, op1=ALU.add).then_inc(s["k_kept"], 1)

                    def shift(i, g):
                        dve.wait_ge(s["s_ready"], G * i + g + 1)
                        src = ps[4 + g][0:S, 0:HALF].rearrange("p (a b) -> p a b", b=S)
                        c.link(nc.vector.tensor_reduce(mx[:, g], src, AX, ALU.max))
                        nc.vector.tensor_tensor(prob[:, g], src, mx[:, g].unsqueeze(2).to_broadcast([S, 4, S]),
                                                ALU.subtract).then_inc(s["shifted"], 1)

                    def sums(i, g):
                        dve.wait_ge(s["exps"], G * i + g + 1)
                        c.link(nc.vector.tensor_reduce(rs[:, g], prob[:, g], AX, ALU.add))
                        nc.vector.reciprocal(rs[:, g], rs[:, g]).then_inc(s["rsum"], 1)

                    def keep_o(i, j, g):
                        for h in range(2):
                            dve.wait_ge(s["o_hi"], 2 * (G * i + g) + h + 1)
                            rows = slice(h * DH, (h + 1) * DH)
                            src = ps[g][rows, 0:HALF].rearrange("p (b h i) -> p b h i", b=2, h=2)[:, :, h, :]
                            at = (rows, bass.ds(i, 1), slice(2 * g * S, (2 * g + 2) * S))
                            dst, hi = (x[at].rearrange("p o (b i) -> p (o b) i", b=2) for x in (oT[1], oT[0]))
                            nc.vector.scalar_tensor_tensor(out=dst, in0=src, scalar=bias[rows, j, 2:3], in1=hi.bitcast(F32),
                                                           op0=ALU.add, op1=ALU.subtract).then_inc(s["o_lo"], 1)

                    def body(i, j, more):
                        shift(i, 0)
                        shift(i, 1)
                        sums(i, 0)
                        shift(i, 2)
                        sums(i, 1)
                        shift(i, 3)
                        sums(i, 2)
                        sums(i, 3)
                        if more:
                            keep_k(i + 1, 1 - j)
                        for g in range(G):
                            keep_o(i, j, g)

                    dve.sem_inc(s["o_lo"], 1)
                    dve.wait_ge(s["kz_cleared"], 2)
                    keep_k(0, 0)
                    with dve.Fori(0, HP // 2 - 1) as p:
                        c.enter(p, 4 * G)
                        body(2 * p, 0, True)
                        body(2 * p + 1, 1, True)
                        c.leave(HP // 2 - 1)
                    body(HP - 2, 0, True)
                    body(HP - 1, 1, False)
                    for t in range(NT):
                        dve.wait_ge(s["y_ready"], t + 1)
                        nc.vector.tensor_tensor(X[:, t, :], X[:, t, :], ps[t % 8][:, 0:D], ALU.add).then_inc(s["x_added"], 1)

                @block.tensor
                def _(pe):
                    self.turn_tensor(pe, ln, xn)

                    def qk(hp, first=False):
                        for n, pick in ((1, k_w), (0, q_w)):
                            for f in range(2):
                                if first:
                                    pe.wait_ge(ln["lo_ready"], 2 * f + 2)
                                for k in range(KT):
                                    last = self.mm(ps[2 * n + f][:, 0:HALF], pick(w, k),
                                                   cut(xT, slice(None), k, slice(f * HALF, (f + 1) * HALF)), k == 0, k == KT - 1)
                                last.then_inc(s["qk_ready"], 1)

                    def values(hp):
                        for f in range(2):
                            pe.wait_ge(s["q_kept"], 2 * hp + f + 1)
                            for b in range(4):
                                for k in range(KT):
                                    last = self.mm(ps[f][0:S, tile(b)],
                                                   cut(xT, slice(None), k, slice((4 * f + b) * S, (4 * f + b + 1) * S)),
                                                   v_w(w, k), k == 0, k == KT - 1)
                            last.then_inc(s["v_ready"], 1)

                    def scores(i):
                        pe.wait_ge(s["q_kept"], 2 * i + 2)
                        pe.wait_ge(s["k_kept"], 4 * i + 4)
                        for g in range(G):
                            for j in range(2):
                                b = 2 * g + j
                                last = nc.tensor.matmul(
                                    ps[4 + g][0:S, j * 2 * S:(j + 1) * 2 * S].rearrange("p (h i) -> p h i", h=2),
                                    qT[:, b * S:(b + 1) * S], kz[:, :, b * S:(b + 1) * S], start=True, stop=True)
                            last.then_inc(s["s_ready"], 1)

                    def turn(i, g):
                        pe.wait_ge(s["norm"], G * i + g + 1)
                        for m in range(4):
                            last = nc.tensor.transpose(ps[4 + g][0:S, m * S:(m + 1) * S], prob[:, g, m, :], self.ident[0:S, 0:S])
                        last.then_inc(s["p_turned"], 1)

                    def mix(i, j2, g):
                        pe.wait_ge(s["pT_kept"], G * i + g + 1)
                        for j in range(2):
                            last = nc.tensor.matmul(ps[g][:, j * 2 * S:(j + 1) * 2 * S].rearrange("p (h i) -> p h i", h=2),
                                                    v[:, j2, 2 * g + j, :], probT[:, g, 2 * j:2 * j + 2, :], start=True, stop=True)
                        last.then_inc(s["pv_ready"], 1)

                    def body(i, j, more):
                        scores(i)
                        if more:
                            pe.wait_ge(s["w_split"], 2 * (i + 1) + 2)
                            pe.wait_ge(s["o_lo"], 2 * G * i + 1)
                            qk(i + 1)
                            values(i + 1)
                        else:
                            pe.wait_ge(s["o_lo"], 2 * G * i + 1)
                        turn(i, 0)
                        turn(i, 1)
                        for g in range(G):
                            if more and g < 2:
                                pe.wait_ge(s["v_kept"], 2 * i + 2 + g + 1)
                            elif more:
                                pe.wait_ge(s["k_kept"], 4 * i + 4 + 2 * (g - 2) + 2)
                            else:
                                pe.wait_ge(s["v_kept"], 2 * i + 2)
                            mix(i, j, g)
                            if g < 2:
                                turn(i, g + 2)

                    pe.wait_ge(s["w_split"], 2)
                    qk(0, first=True)
                    values(0)
                    pe.wait_ge(s["v_kept"], 2)
                    with pe.Fori(0, HP // 2 - 1) as p:
                        body(2 * p, 0, True)
                        body(2 * p + 1, 1, True)
                    body(HP - 2, 0, True)
                    body(HP - 1, 1, False)
                    pe.wait_ge(s["o_lo"], 2 * G * HP + 1)
                    pe.wait_ge(s["wo_split"], 2)
                    self.project(pe, oT, wo, s["y_ready"])

    def project(self, pe, oT, w, y_ready, before=None):
        for t in range(NT):
            if before:
                before(t)
            for hp in range(HP):
                last = self.mm(self.ps[t % 8][:, 0:D], cut(oT, slice(None), hp, tile(t)), cut(w, slice(None), hp, slice(None)),
                               hp == 0, hp == HP - 1)
            last.then_inc(y_ready, 1)

    def ffn_sems(self, st, name):
        return st.sems_of("h_ready", "gate_done", "plain_done", "hid_hi", "hid_lo", "y_ready", "y_used", prefix=name + "_")

    def ffn_tensor(self, pe, o, e, xT, pick, gated, hid, w2, w2_ready, half_ready=None, FT=8):
        pieces = 2 * FT
        for m in range(pieces):
            half, f = divmod(m, FT)
            if m == FT and half_ready:
                half_ready()
            depth = 2 if gated else 4
            if m >= depth:
                pe.wait_ge(o["plain_done"], pieces * e + m - depth + 1)
            for n in range(2 if gated else 1):
                bank = (2 * m + n) % 4 if gated else m % 4
                for k in range(KT):
                    last = self.mm(self.ps[bank][:, 0:HALF], pick(n, k, f),
                                   cut(xT, slice(None), k, slice(half * HALF, (half + 1) * HALF)), k == 0, k == KT - 1)
            last.then_inc(o["h_ready"], 1)
        w2_ready()
        for t in range(NT):
            if t == 0:
                pe.wait_ge(o["hid_lo"], pieces * e + FT)
            if t == 3:
                pe.wait_ge(o["hid_lo"], pieces * e + pieces)
            pe.wait_ge(o["y_used"], NT * e + (t - 3 if t >= 4 else 0) + 1)
            for f in range(FT):
                last = self.mm(self.ps[4 + t % 4][:, 0:D], cut(hid, slice(None), f, tile(t)),
                               cut(w2, slice(None), f, slice(None)), f == 0, f == FT - 1)
            last.then_inc(o["y_ready"], 1)

    def ffn_scalar(self, act, o, e, func, plain, gate, bias=None, FT=8):
        pieces = 2 * FT
        for m in range(pieces):
            act.wait_ge(o["h_ready"], pieces * e + m + 1)
            if gate is not None:
                if m >= 2:
                    act.wait_ge(o["plain_done"], pieces * e + m - 1)
                self.nc.scalar.activation(gate[:, m % 2], self.ps[(2 * m + 1) % 4][:, 0:HALF], func).then_inc(o["gate_done"], 1)
            else:
                if m >= 2:
                    act.wait_ge(o["hid_lo"], pieces * e + m - 1)
                self.nc.scalar.activation(plain[:, m % 2], self.ps[m % 4][:, 0:HALF], func,
                                          bias=bias[:, m % FT:m % FT + 1]).then_inc(o["plain_done"], 1)

    def ffn_vector(self, dve, o, e, plain, gate, hid, FT=8):
        nc = self.nc
        pieces = 2 * FT
        for m in range(pieces):
            half, f = divmod(m, FT)
            at = (slice(None), f, slice(half * HALF, (half + 1) * HALF))
            if gate is not None:
                dve.wait_ge(o["gate_done"], pieces * e + m + 1)
                nc.vector.tensor_tensor(plain[:, m % 2], gate[:, m % 2], self.ps[(2 * m) % 4][:, 0:HALF],
                                        ALU.mult).then_inc(o["plain_done"], 1)
            dve.wait_ge(o["plain_done"], pieces * e + m + 1)
            nc.vector.tensor_copy(hid[0][at], plain[:, m % 2]).then_inc(o["hid_hi"], 1)
            dve.wait_ge(o["hid_hi"], pieces * e + m + 1)
            nc.vector.tensor_tensor(hid[1][at], plain[:, m % 2], hid[0][at].bitcast(F32), ALU.subtract).then_inc(o["hid_lo"], 1)

    def l0_cross_attention(self):
        nc = self.nc
        with Stage(nc, "b") as st:
            self.Q = st.sb("q", [P, NT, D])
            self.qoT = st.sb("qoT", [P, HP, N])
            self.w1 = st.pair("w1", [P, KT, INNER])
            with Stage(nc, "bw") as sw:
                self.wk = sw.pair("wk", [P, KT, INNER])
                self.wv = sw.pair("wv", [P, KT, INNER])
                self.wkv = sw.sb("wkv", [P, KT, 192])
                self.ctx = sw.sb("ctx", [CP, CH, D])
                self.cn = sw.sb("cn", [CP, CH, D])
                self.gb = sw.sb("gb", [P, 2, 2, KT])
                self.cross_queries()
                self.cross_context()
            self.cross_output()

    def cross_queries(self):
        nc, a, ps = self.nc, self.a, self.ps
        with Stage(nc, "bq") as st:
            xT = st.pair("xT", [P, KT, N])
            plain = st.sb("plain", [P, KT, N])
            wq = self.ahead_as(a=KT)
            raw = (self.ahead_raw[:, :].rearrange("p (a b) -> p a b", a=KT), st.sb("raw", [P, KT, INNER])[:, :, :])
            gb, ctx, cn = self.gb[:, 0], self.ctx, self.cn
            cstats = st.sb("cstats", [CP, CH, 6])
            cmv = st.sb("cmv", [CP, CH, 2])
            cstd = st.sb("cstd", [CP, CH])
            xn = st.sb("xn", [P, NT, D])
            qn = st.sb("qn", [P, 2, INNER])
            sq = st.sb("sq", [P, 2, 512])
            ssq = st.sb("ssq", [P, NT, H])
            ln, ln2 = self.ln_buffers(st, "ln"), self.ln_buffers(st, "lnb")
            s = st.sems_of("loaded", "w_split", "g_loaded", "q_ready", "squared", "summed", "rooted", "chain",
                                          "scaled", "turned", "kept", "ctx_loaded", "ctx_var", "ctx_root", "ctx_normed")
            with nc.Block() as block:
                @block.sync
                def _(sp):
                    sp.dma_start(self.gb[:, 0], a["L0_ln1"]).then_inc(s["g_loaded"], 16)
                    sp.dma_start(self.gb[:, 1], a["L1_cln"]).then_inc(s["g_loaded"], 16)
                    sp.dma_start(ctx[:, :, :], a["ctx"][0]).then_inc(s["ctx_loaded"], 16)
                    sp.dma_start(raw[0], a["L0_wk"]).then_inc(s["loaded"], 16)
                    sp.dma_start(raw[1], a["L0_wv"]).then_inc(s["loaded"], 16)
                    sp.dma_start(self.wkv[:, :, :], a["L1_wkv"]).then_inc(s["loaded"], 16)

                @block.gpsimd
                def _(pool):
                    pool.wait_ge(s["loaded"], 48)
                    self.split_pool(pool, s["w_split"], raw[0], cut(self.wk, slice(None)), 0)
                    self.split_pool(pool, s["w_split"], raw[1], cut(self.wv, slice(None)), 1)

                @block.scalar
                def _(act):
                    self.ln_scalar_sqrt(act, ln)
                    self.ln_scalar_sqrt(act, ln2)
                    self.split_scalar(act, ln2, xT, plain)
                    act.wait_ge(s["ctx_var"], 1)
                    nc.scalar.activation(cstd[:, :], cstd[:, :], ACT.Sqrt).then_inc(s["ctx_root"], 1)

                    def keep(t):
                        for n in range(2):
                            act.wait_ge(s["turned"], 2 * t + n + 1)
                            nc.scalar.activation(self.qoT[:, 4 * n:4 * n + 4, tile(t)],
                                                 ps[4 + 2 * (t % 2) + n][:, :].rearrange("p (a b) -> p a b", b=P), ACT.Copy).then_inc(s["kept"], 1)

                    for t in range(NT):
                        for n in range(2):
                            act.wait_ge(s["q_ready"], 2 * t + n + 1)
                            if t:
                                act.wait_ge(s["summed"], 2 * (t - 1) + n + 1)
                            nc.scalar.activation(sq[:, n], ps[(2 * t + n) % 4][:, :], ACT.Square).then_inc(s["squared"], 1)
                        act.wait_ge(s["summed"], 2 * t + 2)
                        nc.scalar.activation(ssq[:, t], ssq[:, t], ACT.Sqrt).then_inc(s["rooted"], 1)
                        if t:
                            keep(t - 1)
                    keep(NT - 1)

                @block.vector
                def _(dve):
                    self.ln_vector(dve, ln, self.X, self.Q)
                    dve.wait_ge(ln["norm_ready"], NT)
                    self.ln_vector(dve, ln2, self.Q, xn)
                    dve.wait_ge(s["g_loaded"], 32)
                    self.split_vector(dve, ln2, xT, plain, gb[:, 0], gb[:, 1])
                    c = Chain(dve, s["chain"])
                    dve.wait_ge(s["ctx_loaded"], 16)
                    for n in range(CH):
                        last = nc.vector.bn_stats(cstats[:, n], ctx[:, n])
                    c.link(last)
                    for n in range(CH):
                        last = nc.vector.bn_aggr(cmv[:, n], cstats[:, n])
                    c.link(last)
                    nc.vector.tensor_scalar(cstd[:, :], cmv[:, :, 1], EPS, None, ALU.add).then_inc(s["ctx_var"], 1)
                    dve.wait_ge(s["ctx_root"], 1)
                    c.link(nc.vector.reciprocal(cstd[:, :], cstd[:, :]))
                    for n in range(CH):
                        nc.vector.tensor_scalar(cn[:, n], ctx[:, n], cmv[:, n, 0:1], cstd[:, n:n + 1],
                                                ALU.subtract, ALU.mult).then_inc(s["ctx_normed"], 1)
                    for t in range(NT):
                        for n in range(2):
                            dve.wait_ge(s["squared"], 2 * t + n + 1)
                            nc.vector.tensor_reduce(ssq[:, t, 8 * n:8 * n + 8], sq[:, n].rearrange("p (h d) -> p h d", d=DH), AX, ALU.add).then_inc(s["summed"], 1)
                        dve.wait_ge(s["rooted"], t + 1)
                        c.link(nc.vector.tensor_scalar(ssq[:, t], ssq[:, t], 1e-12, None, ALU.max))
                        c.link(nc.vector.reciprocal(ssq[:, t], ssq[:, t]))
                        for n in range(2):
                            nc.vector.tensor_tensor(qn[:, t % 2, 512 * n:512 * n + 512].rearrange("p (h d) -> p h d", d=DH),
                                                    ps[(2 * t + n) % 4][:, :].rearrange("p (h d) -> p h d", d=DH),
                                                    ssq[:, t, 8 * n:8 * n + 8].unsqueeze(2).to_broadcast([P, 8, DH]),
                                                    ALU.mult).then_inc(s["scaled"], 1)

                @block.tensor
                def _(pe):
                    self.turn_tensor(pe, ln2, xn)

                    def turn(t):
                        pe.wait_ge(s["scaled"], 2 * t + 2)
                        if t >= 2:
                            pe.wait_ge(s["kept"], 2 * t - 2)
                        for n in range(2):
                            for m in range(4):
                                last = nc.tensor.transpose(ps[4 + 2 * (t % 2) + n][:, tile(m)], qn[:, t % 2, tile(4 * n + m)], self.ident[:, :])
                            last.then_inc(s["turned"], 1)

                    for t in range(NT):
                        if t < 2:
                            pe.wait_ge(ln2["lo_ready"], 2 + 2 * t)
                        for n in range(2):
                            if t >= 2:
                                pe.wait_ge(s["scaled"], 2 * (t - 2) + n + 1)
                            for k in range(KT):
                                last = self.mm(ps[(2 * t + n) % 4][:, :], cut(xT, slice(None), k, tile(t)),
                                               cut(wq, slice(None), k, slice(512 * n, 512 * n + 512)), k == 0, k == KT - 1)
                            last.then_inc(s["q_ready"], 1)
                        if t:
                            turn(t - 1)
                    turn(NT - 1)

    def cross_context(self):
        nc, a, ps, qoT = self.nc, self.a, self.ps, self.qoT
        with Stage(nc, "bc") as st:
            ctx, cn, gb = self.ctx, self.cn, self.gb
            stats = st.sb("stats", [CP, CH, 6])
            mv = st.sb("mv", [CP, CH, 2])
            std = st.sb("std", [CP, CH])
            rstd = st.sb("rstd", [CP, CH])
            scaled = st.sb("scaled", [P, 2, KT, S2E])
            cT = st.pair("cT", [P, KT, S2])
            sq = st.sb("sq", [CP, 2, 512])
            ssq = st.sb("ssq", [CP, CH, H])
            kn = st.sb("kn", [CP, CH, INNER])
            v = st.sb("v", [CP, CH, INNER])
            w1raw = st.sb("w1raw", [P, 2 * INNER])
            kv = st.sb("kv", [P, HP, P])
            s = st.sems_of(
                "loaded", "cleared", "chain", "aggr", "var", "root", "normed", "turned", "affine", "hi", "lo",
                "k_ready", "v_ready", "squared", "summed", "rooted", "k_kept", "v_kept", "l1_ready", "l1_hi", "l1_lo", "l1_kept",
                "kv_ready", "kv_kept_a", "kv_kept_d", "o_ready", "o_kept", "ahead_loaded", "ahead_split", "w1_loaded", "w1_split")
            with nc.Block() as block:
                @block.sync
                def _(sp):
                    sp.sem_inc(s["loaded"], 16)
                    self.ahead_load(sp, s, a["L0_xwo"])
                    sp.dma_start(w1raw[:, :], a["L0_w1"]).then_inc(s["w1_loaded"], 16)
                    with sp.Fori(0, B - 1) as i:
                        sp.wait_ge(s["normed"], CH * i + CH)
                        sp.dma_start(ctx[:, :, :], a["ctx"][bass.ds(i + 1, 1)].rearrange("o p c d -> (o p) c d")).then_inc(s["loaded"], 16)

                @block.gpsimd
                def _(pool):
                    nc.gpsimd.memset(scaled[:, 1, :, S2:S2E], 0.0).then_inc(s["cleared"], 1)
                    nc.gpsimd.memset(kv[:, :, :], 0.0).then_inc(s["cleared"], 1)
                    self.ahead_split(pool, s)
                    pool.wait_ge(s["w1_loaded"], 16)
                    self.split_pool(pool, s["w1_split"], w1raw[:, :], tuple(x[:, :, :].rearrange("p a b -> p (a b)") for x in self.w1), 0)

                @block.scalar
                def _(act):
                    act.sem_inc(s["o_kept"], 1)

                    def root(b):
                        act.wait_ge(s["var"], b + 1)
                        nc.scalar.activation(std[:, :], std[:, :], ACT.Sqrt).then_inc(s["root"], 1)

                    def split(b):
                        for k in range(KT):
                            act.wait_ge(s["affine"], 4 * b + 2 * k + 1)
                            nc.scalar.activation(cT[0][:, k], scaled[:, 0, k, 0:S2], ACT.Copy).then_inc(s["hi"], 1)

                    def body(i, more):
                        if more:
                            root(i + 1)
                        for c in range(CH):
                            for n in range(2):
                                act.wait_ge(s["k_ready"], 6 * i + 2 * c + n + 1)
                                if c:
                                    act.wait_ge(s["summed"], 6 * i + 2 * (c - 1) + n + 1)
                                nc.scalar.activation(sq[:, n], ps[6 * (c % 2) + n][0:CP, :], ACT.Square).then_inc(s["squared"], 1)
                            for n in range(2):
                                act.wait_ge(s["v_ready"], 6 * i + 2 * c + n + 1)
                                nc.scalar.activation(v[:, c, 512 * n:512 * n + 512], ps[2 + n][0:CP, :], ACT.Copy).then_inc(s["v_kept"], 1)
                            act.wait_ge(s["summed"], 6 * i + 2 * c + 2)
                            nc.scalar.activation(ssq[:, c], ssq[:, c], ACT.Sqrt).then_inc(s["rooted"], 1)
                        act.wait_ge(s["l1_ready"], 2 * i + 1)
                        nc.scalar.activation(self.k1T[0][:, bass.ds(i * S2E, S2E)], ps[4][:, 0:S2E], ACT.Copy).then_inc(s["l1_hi"], 1)
                        act.wait_ge(s["l1_ready"], 2 * i + 2)
                        nc.scalar.activation(self.v1[:, bass.ds(i * CH, CH), :], ps[5][0:CP, 0:CH * DH].rearrange("p (c d) -> p c d", d=DH),
                                             ACT.Copy).then_inc(s["l1_kept"], 1)
                        if more:
                            split(i + 1)
                        for n in range(2):
                            act.wait_ge(s["kv_ready"], 2 * i + n + 1)
                            nc.scalar.activation(kv[0:DH, 4 * n:4 * n + 4, 0:DH],
                                                 ps[4 + n][0:DH, :].rearrange("p (a b) -> p a b", b=P)[:, :, 0:DH], ACT.Copy).then_inc(s["kv_kept_a"], 1)
                        for n in range(2):
                            act.wait_ge(s["o_ready"], 2 * i + n + 1)
                            nc.scalar.activation(qoT[:, 4 * n:4 * n + 4, bass.ds(i * S, S)],
                                                 ps[4 + n][:, 0:4 * S].rearrange("p (a b) -> p a b", b=S), ACT.Copy).then_inc(s["o_kept"], 1)

                    act.sem_inc(s["root"], 1)
                    split(0)
                    act.wait_ge(s["cleared"], 2)
                    with act.Fori(0, B - 1) as i:
                        body(i, True)
                    body(B - 1, False)

                @block.vector
                def _(dve):
                    c = Chain(dve, s["chain"])

                    def stat(b):
                        dve.wait_ge(s["loaded"], 16 * b + 16)
                        for n in range(CH):
                            last = nc.vector.bn_stats(stats[:, n], ctx[:, n])
                        c.link(last)
                        dve.sem_inc(s["aggr"], 1)
                        for n in range(CH):
                            last = nc.vector.bn_aggr(mv[:, n], stats[:, n])
                        c.link(last)
                        nc.vector.tensor_scalar(std[:, :], mv[:, :, 1], EPS, None, ALU.add).then_inc(s["var"], 1)

                    def norm(b):
                        dve.wait_ge(s["root"], b + 1)
                        c.link(nc.vector.reciprocal(rstd[:, :], std[:, :]))
                        for n in range(CH):
                            nc.vector.tensor_scalar(cn[:, n], ctx[:, n], mv[:, n, 0:1], rstd[:, n:n + 1],
                                                    ALU.subtract, ALU.mult).then_inc(s["normed"], 1)

                    def split(b):
                        for k in range(KT):
                            dve.wait_ge(s["turned"], 2 * b + k + 1)
                            for l in range(2):
                                nc.vector.tensor_scalar(scaled[:, l, k, 0:S2], ps[6 + k][:, 0:S2], gb[:, l, 0, k:k + 1], gb[:, l, 1, k:k + 1],
                                                        ALU.mult, ALU.add).then_inc(s["affine"], 1)
                        for k in range(KT):
                            dve.wait_ge(s["hi"], 2 * b + k + 1)
                            nc.vector.tensor_tensor(cT[1][:, k], scaled[:, 0, k, 0:S2], cT[0][:, k].bitcast(F32),
                                                    ALU.subtract).then_inc(s["lo"], 1)

                    def body(i, more):
                        if more:
                            stat(i + 1)
                        for m in range(CH):
                            for n in range(2):
                                dve.wait_ge(s["squared"], 6 * i + 2 * m + n + 1)
                                nc.vector.tensor_reduce(ssq[:, m, 8 * n:8 * n + 8], sq[:, n].rearrange("p (h d) -> p h d", d=DH), AX, ALU.add).then_inc(s["summed"], 1)
                            dve.wait_ge(s["rooted"], CH * i + m + 1)
                            c.link(nc.vector.tensor_scalar(ssq[:, m], ssq[:, m], 1e-12, None, ALU.max))
                            c.link(nc.vector.reciprocal(ssq[:, m], ssq[:, m]))
                            for n in range(2):
                                nc.vector.tensor_tensor(kn[:, m, 512 * n:512 * n + 512].rearrange("p (h d) -> p h d", d=DH),
                                                        ps[6 * (m % 2) + n][0:CP, :].rearrange("p (h d) -> p h d", d=DH),
                                                        ssq[:, m, 8 * n:8 * n + 8].unsqueeze(2).to_broadcast([CP, 8, DH]),
                                                        ALU.mult).then_inc(s["k_kept"], 1)
                            if m == 0 and more:
                                norm(i + 1)
                        at = (slice(None), bass.ds(i * S2E, S2E))
                        dve.wait_ge(s["l1_hi"], i + 1)
                        nc.vector.tensor_tensor(self.k1T[1][at], ps[4][:, 0:S2E], self.k1T[0][at].bitcast(F32), ALU.subtract).then_inc(s["l1_lo"], 1)
                        if more:
                            split(i + 1)
                        for n in range(2):
                            dve.wait_ge(s["kv_ready"], 2 * i + n + 1)
                            nc.vector.tensor_copy(kv[DH:P, 4 * n:4 * n + 4, DH:P],
                                                  ps[4 + n][DH:P, :].rearrange("p (a b) -> p a b", b=P)[:, :, DH:P]).then_inc(s["kv_kept_d"], 1)

                    dve.sem_inc(s["var"], 1)
                    dve.sem_inc(s["normed"], CH)
                    split(0)
                    dve.wait_ge(s["cleared"], 2)
                    with dve.Fori(0, B - 1) as i:
                        c.enter(i, 3 + 2 * CH)
                        body(i, True)
                        c.leave(B - 1)
                    body(B - 1, False)

                @block.tensor
                def _(pe):
                    def turn(b):
                        pe.wait_ge(s["normed"], CH * b + CH)
                        for k in range(KT):
                            for m in range(CH):
                                last = nc.tensor.transpose(ps[6 + k][:, m * CP:(m + 1) * CP], cn[:, m, tile(k)], self.ident[0:CP, 0:CP])
                            last.then_inc(s["turned"], 1)

                    def body(i, more):
                        pe.wait_ge(s["lo"], 2 * i + 2)
                        for m in range(CH):
                            rows = slice(m * CP, (m + 1) * CP)
                            for w, bank, ready in ((self.wk, 6 * (m % 2), s["k_ready"]), (self.wv, 2, s["v_ready"])):
                                if w is self.wk and m == 2:
                                    pe.wait_ge(s["k_kept"], 6 * i + 2)
                                if w is self.wv and m:
                                    pe.wait_ge(s["v_kept"], 6 * i + 2 * m)
                                for n in range(2):
                                    for k in range(KT):
                                        last = self.mm(ps[bank + n][0:CP, :], cut(cT, slice(None), k, rows),
                                                       cut(w, slice(None), k, slice(512 * n, 512 * n + 512)), k == 0, k == KT - 1)
                                    last.then_inc(ready, 1)
                        pe.wait_ge(s["o_kept"], 2 * i + 1)
                        for k in range(KT):
                            last = nc.tensor.matmul(ps[4][:, 0:S2E], self.wkv[:, k, 0:P], scaled[:, 1, k], start=k == 0, stop=k == KT - 1)
                        last.then_inc(s["l1_ready"], 1)
                        for m in range(CH):
                            for k in range(KT):
                                last = nc.tensor.matmul(ps[5][0:CP, m * DH:(m + 1) * DH], scaled[:, 1, k, m * CP:(m + 1) * CP], self.wkv[:, k, P:P + DH],
                                                        start=k == 0, stop=k == KT - 1)
                        last.then_inc(s["l1_ready"], 1)
                        if more:
                            pe.wait_ge(s["k_kept"], 6 * i + 4)
                            turn(i + 1)
                        pe.wait_ge(s["k_kept"], 6 * i + 6)
                        pe.wait_ge(s["v_kept"], 6 * i + 6)
                        pe.wait_ge(s["l1_lo"], i + 1)
                        pe.wait_ge(s["l1_kept"], i + 1)
                        for n in range(2):
                            for hp in range(4 * n, 4 * n + 4):
                                for m in range(CH):
                                    last = nc.tensor.matmul(ps[4 + n][:, tile(hp % 4)], kn[:, m, tile(hp)], v[:, m, tile(hp)],
                                                            start=m == 0, stop=m == CH - 1)
                            last.then_inc(s["kv_ready"], 1)
                        pe.wait_ge(s["kv_kept_a"], 2 * i + 2)
                        pe.wait_ge(s["kv_kept_d"], 2 * i + 2)
                        for n in range(2):
                            for hp in range(4 * n, 4 * n + 4):
                                last = nc.tensor.matmul(ps[4 + n][:, (hp % 4) * S:(hp % 4 + 1) * S], kv[:, hp, :], qoT[:, hp, bass.ds(i * S, S)],
                                                        start=True, stop=True)
                            last.then_inc(s["o_ready"], 1)

                    turn(0)
                    pe.wait_ge(s["cleared"], 2)
                    with pe.Fori(0, B - 1) as i:
                        body(i, True)
                    body(B - 1, False)

    def cross_output(self):
        nc, a, ps, X, Q, qoT = self.nc, self.a, self.ps, self.X, self.Q, self.qoT
        with Stage(nc, "bo") as st:
            hid = st.pair("hid", [P, HP, N])
            wo, w1 = self.ahead_as(a=HP), self.w1
            w2 = st.pair("w2", [P, HP, D])
            xT = st.pair("xT", [P, KT, N])
            bo = st.sb("bo", [P, 2, D])
            gb = st.sb("gb", [P, 2, KT])
            b1 = st.sb("b1", [P, 8])
            plain = st.sb("plain", [P, 2, HALF])
            scaled = qoT[:, 0:KT, :]
            xn = qoT[:, 2:4, :].rearrange("p a b -> p (a b)").rearrange("p (t d) -> p t d", d=D)
            ln = self.ln_buffers(st)
            f = self.ffn_sems(st, "ffn")
            s = st.sems_of("loaded", "c_loaded", "w_split", "o_hi", "o_lo", "y_ready", "x_added", "added", "sum_ready")
            with nc.Block() as block:
                @block.sync
                def _(sp):
                    sp.dma_start(bo[:, 0], a["L0_xattn_bo"].partition_broadcast(P)).then_inc(s["c_loaded"], 16)
                    sp.dma_start(bo[:, 1], a["L0_xattn_b2"].partition_broadcast(P)).then_inc(s["c_loaded"], 16)
                    sp.dma_start(gb[:, :, :], a["L0_ln2"]).then_inc(s["c_loaded"], 16)
                    sp.dma_start(b1[:, :], a["L0_b1"]).then_inc(s["c_loaded"], 16)
                    sp.dma_start(self.ahead_raw[:, :], a["L0_w2"]).then_inc(s["loaded"], 16)

                @block.gpsimd
                def _(pool):
                    pool.wait_ge(s["loaded"], 16)
                    self.split_pool(pool, s["w_split"], self.ahead_raw[:, :], tuple(x[:, :, :].rearrange("p a b -> p (a b)") for x in w2), 0)

                @block.scalar
                def _(act):
                    for t in range(NT):
                        nc.scalar.activation(hid[0][:, :, tile(t)], qoT[:, :, tile(t)], ACT.Copy).then_inc(s["o_hi"], 1)
                    self.ln_scalar_sqrt(act, ln)
                    self.split_scalar(act, ln, xT, scaled)
                    self.ffn_scalar(act, f, 0, ACT.Gelu, plain, None, b1)

                @block.vector
                def _(dve):
                    for t in range(NT):
                        dve.wait_ge(s["o_hi"], t + 1)
                        nc.vector.tensor_tensor(hid[1][:, :, tile(t)], qoT[:, :, tile(t)], hid[0][:, :, tile(t)].bitcast(F32), ALU.subtract).then_inc(s["o_lo"], 1)
                    dve.wait_ge(s["c_loaded"], 64)
                    nc.vector.tensor_tensor(Q[:, :, :], Q[:, :, :], bo[:, 0].unsqueeze(1).to_broadcast([P, NT, D]), ALU.add).then_inc(s["added"], 1)
                    nc.vector.tensor_tensor(X[:, :, :], X[:, :, :], bo[:, 1].unsqueeze(1).to_broadcast([P, NT, D]), ALU.add).then_inc(s["added"], 1)
                    dve.wait_ge(s["added"], 2)
                    for t in range(NT):
                        dve.wait_ge(s["y_ready"], t + 1)
                        nc.vector.tensor_tensor(Q[:, t], Q[:, t], ps[t][:, 0:D], ALU.add).then_inc(s["x_added"], 1)
                    dve.wait_ge(s["x_added"], NT)
                    self.ln_vector(dve, ln, Q, xn)
                    self.split_vector(dve, ln, xT, scaled, gb[:, 0], gb[:, 1])
                    nc.vector.tensor_tensor(X[:, :, :], X[:, :, :], Q[:, :, :], ALU.add).then_inc(s["sum_ready"], 1)
                    dve.sem_inc(f["y_used"], 1)
                    self.ffn_vector(dve, f, 0, plain, None, hid)
                    dve.wait_ge(s["sum_ready"], 1)
                    for t in range(NT):
                        dve.wait_ge(f["y_ready"], t + 1)
                        nc.vector.tensor_tensor(X[:, t], X[:, t], ps[4 + t % 4][:, 0:D], ALU.add).then_inc(f["y_used"], 1)

                @block.tensor
                def _(pe):
                    self.project(pe, hid, wo, s["y_ready"], lambda t: pe.wait_ge(s["o_lo"], t + 1))
                    self.turn_tensor(pe, ln, xn)
                    pe.wait_ge(ln["lo_ready"], 2)
                    self.ffn_tensor(pe, f, 0, xT, lambda n, k, ft: cut(w1, slice(None), k, tile(ft)), False, hid, w2,
                                    lambda: pe.wait_ge(s["w_split"], 2), lambda: pe.wait_ge(ln["lo_ready"], 4))

    def rank(self, dve, c, vals, lt, n, more, same, out):
        nc = self.nc
        here = vals.unsqueeze(3).to_broadcast([P, NT, n, n])
        other = vals.unsqueeze(2).to_broadcast([P, NT, n, n])
        view = (slice(None), slice(None), slice(0, n), slice(0, n))
        nc_lt = lt[:, 0:n, 0:n].unsqueeze(1).to_broadcast([P, NT, n, n])
        c.link(nc.vector.tensor_tensor(more[view], other, here, ALU.is_gt))
        c.link(nc.vector.tensor_tensor(same[view], other, here, ALU.is_equal))
        c.link(nc.vector.tensor_tensor(same[view], same[view], nc_lt, ALU.mult))
        c.link(nc.vector.tensor_tensor(more[view], more[view], same[view], ALU.add))
        c.link(nc.vector.tensor_reduce(out, more[view], AX, ALU.add))

    def l0_experts(self):
        nc, a, ps, X = self.nc, self.a, self.ps, self.X
        E, SH, W = 16, 2, 6 * P
        U = 3
        GROUPS = (E + SH) // U
        with Stage(nc, "c") as st:
            xT = st.pair("xT", [P, KT, N])
            xn = st.sb("xn", [P, NT, D])
            raw = st.sb("raw", [P, U, W])
            w = [st.pair(f"w{j}", [P, W]) for j in range(U)]
            graw = st.sb("graw", [P, KT, E])
            gw = st.pair("gw", [P, KT, E])
            gbias = st.sb("gbias", [P, E])
            lt = st.sb("lt", [P, E, E])
            score = st.sb("score", [P, NT, E])
            more = st.sb("more", [P, NT, E, E])
            same = st.sb("same", [P, NT, E, E])
            grp = st.sb("grp", [P, 8, NT, 4])
            keep = st.sb("keep", [P, NT, E])
            tot = st.sb("tot", [P, NT])
            share = st.sb("share", [P, NT, SH + E])
            col = st.sb("col", [P, U, NT])
            gate = st.sb("gate", [P, 2, HALF])
            plain = st.sb("plain", [P, 2, HALF])
            hid = [st.pair(f"hid{j}", [P, N]) for j in range(U)]
            ln = self.ln_buffers(st)
            s = st.sems_of("c_loaded", "w_split", "begun", "g_split", "logit", "scored", "chain", "h_ready", "gate_done",
                                          "plain_done", "hid_hi", "hid_lo", "y_ready", "y_used")
            loaded = [st.sem(f"loaded{j}") for j in range(U)]
            with nc.Block() as block:
                @block.sync
                def _(sp):
                    sp.dma_start(graw[:, :, :], a["L0_gate"]).then_inc(s["c_loaded"], 16)
                    sp.dma_start(gbias[:, :], a["L0_ffn_gate_bias"].partition_broadcast(P)).then_inc(s["c_loaded"], 16)
                    sp.dma_start(lt[:, :, :], a["lower"].partition_broadcast(P)).then_inc(s["c_loaded"], 16)
                    for j in range(U):
                        sp.dma_start(raw[:, j], a["L0_experts"][j]).then_inc(loaded[j], 16)
                    with sp.Fori(0, GROUPS - 1) as i:
                        for j in range(U):
                            sp.wait_ge(s["w_split"], 2 * U * i + (2 * j + 2))
                            sp.dma_start(raw[:, j], a["L0_experts"][bass.ds(U * i + (U + j), 1)].rearrange("o p w -> (o p) w")).then_inc(loaded[j], 16)

                @block.gpsimd
                def _(pool):
                    pool.wait_ge(s["c_loaded"], 48)
                    self.split_pool(pool, s["g_split"], graw[:, :, :], cut(gw, slice(None)), 0)

                    def split(i, j):
                        pool.wait_ge(loaded[j], 16 * i + 16)
                        pool.sem_inc(s["begun"], 1)
                        self.split_pool(pool, s["w_split"], raw[:, j], cut(w[j], slice(None)), U * i + j)

                    for j in range(U):
                        split(0, j)
                    with pool.Fori(0, GROUPS - 1) as i:
                        for j in range(U):
                            pool.wait_ge(s["y_ready"], U * NT * i + (NT * j + NT))
                            split(i + 1, j)

                @block.scalar
                def _(act):
                    self.ln_scalar_sqrt(act, ln)
                    self.split_scalar(act, ln, xT)
                    act.wait_ge(s["logit"], 1)
                    nc.scalar.activation(score[:, :, :], ps[0][:, 0:NT * E].rearrange("p (t e) -> p t e", e=E), ACT.Sigmoid).then_inc(s["scored"], 1)
                    with act.Fori(0, GROUPS) as i:
                        for j in range(U):
                            for f in range(2):
                                q = 2 * U * i + (2 * j + f)
                                act.wait_ge(s["h_ready"], q + 1)
                                act.wait_ge(s["plain_done"], q + 1)
                                nc.scalar.activation(gate[:, f], ps[2 * f][:, 0:HALF], ACT.Silu).then_inc(s["gate_done"], 1)
                            for f in range(2):
                                act.wait_ge(s["plain_done"], 2 * U * i + (2 * j + f + 3))
                                nc.scalar.activation(hid[j][0][:, f * HALF:(f + 1) * HALF], plain[:, f], ACT.Copy).then_inc(s["hid_hi"], 1)

                @block.vector
                def _(dve):
                    dve.sem_inc(s["plain_done"], 2)
                    dve.sem_inc(s["y_used"], NT)
                    self.ln_vector(dve, ln, X, xn)
                    self.split_vector(dve, ln, xT)
                    c = Chain(dve, s["chain"])

                    def hidden(i, j, first=False):
                        if not first:
                            dve.wait_ge(s["hid_lo"], 2 * U * i + 2 * j)
                        for f in range(2):
                            dve.wait_ge(s["gate_done"], 2 * U * i + (2 * j + f + 1))
                            nc.vector.tensor_tensor(plain[:, f], gate[:, f], ps[2 * f + 1][:, 0:HALF], ALU.mult).then_inc(s["plain_done"], 1)
                        for f in range(2):
                            cols = slice(f * HALF, (f + 1) * HALF)
                            dve.wait_ge(s["hid_hi"], 2 * U * i + (2 * j + f + 1))
                            nc.vector.tensor_tensor(hid[j][1][:, cols], plain[:, f], hid[j][0][:, cols].bitcast(F32), ALU.subtract).then_inc(s["hid_lo"], 1)

                    def add(i, j):
                        for t in range(NT):
                            dve.wait_ge(s["y_ready"], U * NT * i + (NT * j + min(t | 1, NT - 1) + 1))
                            dve.wait_ge(s["y_used"], U * NT * i + (NT * j + NT))
                            nc.vector.scalar_tensor_tensor(out=X[:, t], in0=ps[4 + t // 2][:, D * (t % 2):D * (t % 2) + D], scalar=col[:, j, t:t + 1], in1=X[:, t],
                                                           op0=ALU.mult, op1=ALU.add).then_inc(s["y_used"], 1)

                    def columns(i, first=0):
                        for j in range(first, U):
                            c.link(nc.vector.tensor_copy(col[:, j].unsqueeze(2), share[:, :, bass.ds(U * i + j, 1)]))

                    c.link(nc.vector.memset(share[:, :, 0:SH], 1.0))
                    c.link(nc.vector.memset(col[:, 0:SH], 1.0))
                    hidden(0, 0, first=True)
                    dve.wait_ge(s["c_loaded"], 48)
                    dve.wait_ge(s["scored"], 1)
                    sfc = score
                    c.link(nc.vector.tensor_tensor(sfc[:, :, :], score[:, :, :], gbias[:, :].unsqueeze(1).to_broadcast([P, NT, E]), ALU.add))
                    g4 = sfc[:, :, :].rearrange("p t (g j) -> p t g j", j=4)
                    for n, (x, y, op) in enumerate(((0, 1, ALU.max), (2, 3, ALU.max), (0, 1, ALU.min), (2, 3, ALU.min))):
                        c.link(nc.vector.tensor_tensor(grp[:, n], g4[:, :, :, x], g4[:, :, :, y], op))
                    for to, x, y, op in ((4, 0, 1, ALU.max), (5, 0, 1, ALU.min), (6, 2, 3, ALU.max), (5, 5, 6, ALU.max), (7, 4, 5, ALU.add)):
                        c.link(nc.vector.tensor_tensor(grp[:, to], grp[:, x], grp[:, y], op))
                    self.rank(dve, c, grp[:, 7], lt, 4, more, same, grp[:, 0])
                    c.link(nc.vector.tensor_scalar(grp[:, 1], grp[:, 0], 2.0, None, ALU.is_lt))
                    hidden(0, 1)
                    c.link(nc.vector.tensor_tensor(g4, g4, grp[:, 1].unsqueeze(3).to_broadcast([P, NT, 4, 4]), ALU.mult))
                    add(0, 0)
                    hidden(0, 2)
                    add(0, 1)
                    self.rank(dve, c, sfc[:, :, :], lt, E, more, same, keep[:, :, :])
                    c.link(nc.vector.tensor_scalar(keep[:, :, :], keep[:, :, :], 4.0, None, ALU.is_lt))
                    c.link(nc.vector.tensor_tensor(keep[:, :, :], keep[:, :, :], sfc[:, :, :], ALU.mult))
                    c.link(nc.vector.tensor_reduce(tot[:, :], keep[:, :, :], AX, ALU.add))
                    c.link(nc.vector.tensor_scalar(tot[:, :], tot[:, :], 1e-20, None, ALU.add))
                    c.link(nc.vector.reciprocal(tot[:, :], tot[:, :]))
                    c.link(nc.vector.tensor_tensor(keep[:, :, :], keep[:, :, :], tot[:, :].unsqueeze(2).to_broadcast([P, NT, E]), ALU.mult))
                    c.link(nc.vector.tensor_scalar(share[:, :, SH:SH + E], keep[:, :, :], 2.5, None, ALU.mult))
                    columns(0, SH)
                    hidden(1, 0)
                    add(0, 2)

                    def body(i, more):
                        columns(i)
                        for j in range(U):
                            if j + 1 < U:
                                hidden(i, j + 1)
                            elif more:
                                hidden(i + 1, 0)
                            add(i, j)

                    with dve.Fori(0, GROUPS - 2) as i:
                        c.enter(i, U)
                        body(i + 1, True)
                        c.leave(GROUPS - 2)
                    body(GROUPS - 1, False)

                @block.tensor
                def _(pe):
                    self.turn_tensor(pe, ln, xn)
                    pe.wait_ge(s["g_split"], 2)
                    self.logits(pe, ln, xT, gw, E, s["logit"])
                    pe.wait_ge(s["scored"], 1)

                    def hidden(i, j):
                        pe.wait_ge(s["w_split"], 2 * U * i + (2 * j + 2))
                        for f in range(2):
                            pe.wait_ge(s["plain_done"], 2 * U * i + (2 * j + f + 1))
                            for n in range(2):
                                for k in range(KT):
                                    last = self.mm(ps[2 * f + n][:, 0:HALF], cut(w[j], slice(None), slice((2 * k + n) * P, (2 * k + n + 1) * P)),
                                                   cut(xT, slice(None), k, slice(f * HALF, (f + 1) * HALF)), k == 0, k == KT - 1)
                            last.then_inc(s["h_ready"], 1)

                    def down(i, j):
                        pe.wait_ge(s["hid_lo"], 2 * U * i + (2 * j + 2))
                        for t in range(NT):
                            pe.wait_ge(s["y_used"], U * NT * i + (NT * j + min(t | 1, NT - 1) + 1))
                            self.mm(ps[4 + t // 2][:, D * (t % 2):D * (t % 2) + D], cut(hid[j], slice(None), tile(t)), cut(w[j], slice(None), slice(4 * P, 6 * P)),
                                    True, True).then_inc(s["y_ready"], 1)

                    def body(i, more):
                        for j in range(U):
                            if j + 1 < U:
                                hidden(i, j + 1)
                            elif more:
                                hidden(i + 1, 0)
                            down(i, j)

                    hidden(0, 0)
                    with pe.Fori(0, GROUPS - 1) as i:
                        body(i, True)
                    body(GROUPS - 1, False)

    def logits(self, pe, ln, xT, gw, n, ready):
        for t in range(NT):
            if t in (0, 4):
                pe.wait_ge(ln["lo_ready"], 2 + t // 2)
            for k in range(KT):
                last = self.mm(self.ps[0][:, t * n:(t + 1) * n], cut(xT, slice(None), k, tile(t)), cut(gw, slice(None), k, slice(None)),
                               k == 0, k == KT - 1)
        last.then_inc(ready, 1)

    def l1_attention(self):
        nc, a, ps, X = self.nc, self.a, self.ps, self.X
        HD = 16
        with Stage(nc, "d") as st:
            xn = st.sb("xn", [P, NT, D])
            xT = st.sb("xT", [P, KT, N])
            w = st.sb("w", [P, KT, 2 * D])
            nw = st.sb("nw", [S, 2, D])
            own = st.sb("own", [P, 8, S])
            causal = st.sb("causal", [S, S])
            sq = st.sb("sq", [S, 2, 2 * D])
            ms = st.sb("ms", [S, 2, 2 * H])
            qv = st.sb("qv", [S, 2, 2 * D])
            qz = st.sb("qz", [P, KT, 8, S])
            sc = st.sb("sc", [S, H, S])
            out = st.sb("out", [S, B, D])
            back = st.sb("back", [P, NT, D])
            ln = self.ln_buffers(st)
            s = st.sems_of("loaded", "proj", "squared", "rooted", "chain", "mean", "qv_ready", "q_turned", "qz_ready", "s_ready",
                                          "s_kept", "o_ready", "o_kept", "spilled", "spilled_last", "back", "back_last", "added",
                                          "ahead_loaded", "ahead_split")
            full = (B - 1) * S // P
            spill_in, spill_out = a["spill"].rearrange("(b i) f -> i b f", i=S), a["spill"].rearrange("(t p) f -> p t f", p=P)
            with nc.Block() as block:
                @block.gpsimd
                def _(pool):
                    self.ahead_split(pool, s)

                @block.sync
                def _(sp):
                    sp.dma_start(w[:, :, :], a["L1_wqv"]).then_inc(s["loaded"], 16)
                    sp.dma_start(nw[:, :, :], a["L1_norm_w"].partition_broadcast(S)).then_inc(s["loaded"], 16)
                    sp.dma_start(own[:, :, :], a["own"]).then_inc(s["loaded"], 16)
                    sp.dma_start(causal[:, :], a["causal"]).then_inc(s["loaded"], 16)
                    self.ahead_load(sp, s, a["L1_wq"].rearrange("p k n -> p (k n)"))
                    sp.wait_ge(s["o_kept"], B - 1)
                    sp.dma_start(spill_in[:, 0:B - 1], out[:, 0:B - 1]).then_inc(s["spilled"], 16)
                    sp.wait_ge(s["spilled"], 16)
                    sp.dma_start(back[:, 0:full], spill_out[:, 0:full]).then_inc(s["back"], 16)
                    sp.wait_ge(s["o_kept"], B)
                    sp.dma_start(spill_in[:, B - 1:B], out[:, B - 1:B]).then_inc(s["spilled_last"], 16)
                    sp.wait_ge(s["spilled_last"], 16)
                    sp.dma_start(back[:, full:NT], spill_out[:, full:NT]).then_inc(s["back_last"], 16)

                @block.scalar
                def _(act):
                    self.ln_scalar_sqrt(act, ln)
                    for n, (g, k, cols, src) in enumerate(self.turn_pieces()):
                        act.wait_ge(ln["turned"], g + 1)
                        nc.scalar.activation(xT[:, k, cols], src, ACT.Copy).then_inc(ln["hi_ready"], 1)

                    def square(b):
                        act.wait_ge(s["proj"], b + 1)
                        if b >= 2:
                            act.wait_ge(s["mean"], b - 1)
                        nc.scalar.activation(sq[:, b % 2], ps[b % 2][0:S, :], ACT.Square).then_inc(s["squared"], 1)
                        act.wait_ge(s["mean"], b + 1)
                        nc.scalar.activation(ms[:, b % 2], ms[:, b % 2], ACT.Sqrt).then_inc(s["rooted"], 1)

                    square(0)
                    for b in range(B):
                        if b + 1 < B:
                            square(b + 1)
                        act.wait_ge(s["o_ready"], b + 1)
                        nc.scalar.activation(out[:, b], ps[3][0:S, 0:D], ACT.Copy).then_inc(s["o_kept"], 1)

                @block.vector
                def _(dve):
                    self.ln_vector(dve, ln, X, xn)
                    c = Chain(dve, s["chain"])
                    dve.wait_ge(s["loaded"], 64)

                    def norm(b):
                        dve.wait_ge(s["squared"], b + 1)
                        c.link(nc.vector.tensor_reduce(ms[:, b % 2], sq[:, b % 2].rearrange("p (h d) -> p h d", d=HD), AX, ALU.add))
                        nc.vector.tensor_scalar(ms[:, b % 2], ms[:, b % 2], 1.0 / HD, 1e-8, ALU.mult, ALU.add).then_inc(s["mean"], 1)
                        dve.wait_ge(s["rooted"], b + 1)
                        c.link(nc.vector.reciprocal(ms[:, b % 2], ms[:, b % 2]))
                        if b >= 2:
                            dve.wait_ge(s["o_ready"], b - 1)
                        c.link(nc.vector.tensor_tensor(qv[:, b % 2].rearrange("p (h d) -> p h d", d=HD), ps[b % 2][0:S, :].rearrange("p (h d) -> p h d", d=HD),
                                                       ms[:, b % 2].unsqueeze(2).to_broadcast([S, 2 * H, HD]), ALU.mult))
                        nc.vector.tensor_tensor(qv[:, b % 2], qv[:, b % 2], nw[:, :, :].rearrange("p a d -> p (a d)"), ALU.mult).then_inc(s["qv_ready"], 1)

                    norm(0)
                    for b in range(B):
                        for k in range(KT):
                            dve.wait_ge(s["q_turned"], b + 1)
                            nc.vector.tensor_tensor(qz[:, k], own[:, :, :], ps[2][:, k * S:(k + 1) * S].unsqueeze(1).to_broadcast([P, 8, S]),
                                                    ALU.mult).then_inc(s["qz_ready"], 1)
                        if b + 1 < B:
                            norm(b + 1)
                        for g in range(4):
                            dve.wait_ge(s["s_ready"], 4 * b + g + 1)
                            nc.vector.tensor_tensor(sc[:, 4 * g:4 * g + 4], ps[4 + g][0:S, 0:4 * S].rearrange("p (h i) -> p h i", i=S),
                                                    causal[:, :].unsqueeze(1).to_broadcast([S, 4, S]), ALU.mult).then_inc(s["s_kept"], 1)
                    dve.wait_ge(s["back"], 16)
                    nc.vector.tensor_tensor(X[:, 0:full], X[:, 0:full], back[:, 0:full], ALU.add).then_inc(s["added"], 1)
                    dve.wait_ge(s["back_last"], 16)
                    nc.vector.tensor_tensor(X[:, full:NT], X[:, full:NT], back[:, full:NT], ALU.add).then_inc(s["added"], 1)

                @block.tensor
                def _(pe):
                    self.turn_tensor(pe, ln, xn)
                    pe.wait_ge(s["loaded"], 64)

                    def proj(b):
                        if b == 0:
                            pe.wait_ge(ln["hi_ready"], 2)
                        if b >= 2:
                            pe.wait_ge(s["qv_ready"], b - 1)
                        for k in range(KT):
                            last = nc.tensor.matmul(ps[b % 2][0:S, :], xT[:, k, b * S:(b + 1) * S], w[:, k, :], start=k == 0, stop=k == KT - 1)
                        last.then_inc(s["proj"], 1)

                    def turn(b):
                        pe.wait_ge(s["qv_ready"], b + 1)
                        for k in range(KT):
                            last = nc.tensor.transpose(ps[2][:, k * S:(k + 1) * S], qv[:, b % 2, tile(k)], self.ident[0:S, 0:S])
                        last.then_inc(s["q_turned"], 1)

                    proj(0)
                    proj(1)
                    turn(0)
                    pe.wait_ge(ln["hi_ready"], 4)
                    for b in range(B):
                        for g in range(4):
                            pe.wait_ge(s["qz_ready"], KT * b + g // 2 + 1)
                            last = nc.tensor.matmul(ps[4 + g][0:S, 0:4 * S].rearrange("p (h i) -> p h i", i=S), xT[:, g // 2, b * S:(b + 1) * S],
                                                    qz[:, g // 2, 4 * (g % 2):4 * (g % 2) + 4, :], start=True, stop=True)
                            last.then_inc(s["s_ready"], 1)
                        if b + 1 < B:
                            turn(b + 1)
                        if b + 2 < B:
                            proj(b + 2)
                        if b:
                            pe.wait_ge(s["o_kept"], b)
                        for h in range(H):
                            pe.wait_ge(s["s_kept"], 4 * b + h // 4 + 1)
                            last = nc.tensor.matmul(ps[3][0:S, h * HD:(h + 1) * HD], sc[:, h, :], qv[:, b % 2, D + h * HD:D + (h + 1) * HD], start=True, stop=True)
                        last.then_inc(s["o_ready"], 1)

    def l1_cross_attention(self):
        nc = self.nc
        with Stage(nc, "e") as st:
            self.qoT = st.sb("qoT", [P, HP, N])
            self.qz = st.sb("qz", [P, H, S], F32R)
            with Stage(nc, "ex") as sx:
                self.xT1 = sx.pair("xT", [P, KT, N])
                self.w1 = sx.pair("w1", [P, KT, 2 * INNER])
                self.multi_queries()
                self.gated_ffn()
            with Stage(nc, "ey") as sy:
                self.oT = sy.pair("oT", [P, HP, N])
                self.multi_attention()
                self.multi_output()

    def multi_queries(self):
        nc, a, ps = self.nc, self.a, self.ps
        xT = self.xT1
        with Stage(nc, "eq") as st:
            xn = st.sb("xn", [P, NT, D])
            scaled = st.sb("scaled", [P, KT, N])
            raw = st.sb("raw", [P, KT, 2 * INNER])
            wq = self.ahead_as(a=KT)
            gb = st.sb("gb", [P, 2, KT])
            ln = self.ln_buffers(st)
            s = st.sems_of("loaded", "w_loaded", "w_split", "q_ready", "kept")
            with nc.Block() as block:
                @block.sync
                def _(sp):
                    sp.dma_start(gb[:, :, :], a["L1_ln"]).then_inc(s["loaded"], 16)
                    sp.dma_start(raw[:, :, :], a["L1_w1"]).then_inc(s["w_loaded"], 16)

                @block.gpsimd
                def _(pool):
                    pool.wait_ge(s["w_loaded"], 16)
                    for k in range(KT):
                        self.split_pool(pool, s["w_split"], raw[:, k], cut(self.w1, slice(None), k), k)

                @block.scalar
                def _(act):
                    self.ln_scalar_sqrt(act, ln)
                    self.split_scalar(act, ln, xT, scaled)
                    for m in range(2 * HP):
                        f, hp = divmod(m, HP)
                        act.wait_ge(s["q_ready"], m + 1)
                        nc.scalar.activation(self.qoT[:, hp, f * HALF:(f + 1) * HALF], ps[m % 8][:, 0:HALF], ACT.Copy, scale=DH ** -0.5).then_inc(s["kept"], 1)

                @block.vector
                def _(dve):
                    self.ln_vector(dve, ln, self.X, xn)
                    dve.wait_ge(s["loaded"], 16)
                    self.split_vector(dve, ln, xT, scaled, gb[:, 0], gb[:, 1])

                @block.tensor
                def _(pe):
                    self.turn_tensor(pe, ln, xn)
                    for m in range(2 * HP):
                        f, hp = divmod(m, HP)
                        if m in (0, 4):
                            pe.wait_ge(ln["lo_ready"], 2 + m // 2)
                        if m >= 8:
                            pe.wait_ge(s["kept"], m - 7)
                        for k in range(KT):
                            last = self.mm(ps[m % 8][:, 0:HALF], cut(wq, slice(None), k, tile(hp)), cut(xT, slice(None), k, slice(f * HALF, (f + 1) * HALF)),
                                           k == 0, k == KT - 1)
                        last.then_inc(s["q_ready"], 1)

    def gated_ffn(self):
        nc, a, ps, X = self.nc, self.a, self.ps, self.X
        with Stage(nc, "ef") as st:
            w1, w2 = self.w1, self.ahead_as(a=8)
            hid = st.pair("hid", [P, 8, N])
            plain = st.sb("plain", [P, 2, HALF])
            gate = st.sb("gate", [P, 2, HALF])
            f = self.ffn_sems(st, "ffn")
            s = st.sems_of("ahead_loaded", "ahead_split", "q_placed")
            with nc.Block() as block:
                @block.sync
                def _(sp):
                    self.ahead_load(sp, s, a["L1_w2"])

                @block.gpsimd
                def _(pool):
                    self.ahead_split(pool, s)
                    for n in range(2):
                        self.place_queries(pool, s, n, 0, 4 * n)

                @block.scalar
                def _(act):
                    self.ffn_scalar(act, f, 0, ACT.Silu, plain, gate)

                @block.vector
                def _(dve):
                    dve.sem_inc(f["y_used"], 1)
                    self.ffn_vector(dve, f, 0, plain, gate, hid)
                    for t in range(NT):
                        dve.wait_ge(f["y_ready"], t + 1)
                        nc.vector.tensor_tensor(X[:, t], X[:, t], ps[4 + t % 4][:, 0:D], ALU.add).then_inc(f["y_used"], 1)

                @block.tensor
                def _(pe):
                    self.ffn_tensor(pe, f, 0, self.xT1, lambda n, k, ft: cut(w1, slice(None), k, slice(n * INNER + ft * P, n * INNER + (ft + 1) * P)),
                                    True, hid, w2, lambda: pe.wait_ge(s["ahead_split"], 2))

    def place_queries(self, pool, s, n, b, count, begun=None):
        nc = self.nc
        for h in range(2):
            rows, others = slice(h * DH, (h + 1) * DH), slice((1 - h) * DH, (2 - h) * DH)
            heads = slice(8 * n + h, 8 * n + 8, 2)
            src = self.qoT[rows, 4 * n:4 * n + 4, bass.ds(b * S, S)]
            for low in range(2):
                if low:
                    nc.gpsimd.tensor_tensor(self.qz[others, heads, :], src, self.qz[rows, heads, :].bitcast(F32), ALU.subtract).then_inc(s["q_placed"], 1)
                else:
                    nc.gpsimd.tensor_copy(self.qz[rows, heads, :], src).then_inc(s["q_placed"], 1)
                pool.wait_ge(s["q_placed"], count + (2 * h + low + 1))
                if begun is not None:
                    pool.sem_inc(begun, 1)

    def multi_attention(self):
        nc, ps, qoT, qz, oT = self.nc, self.ps, self.qoT, self.qz, self.oT
        with Stage(nc, "em") as st:
            masks = st.sb("masks", [S, B, S2])
            p = st.sb("p", [S, 4, S2])
            mask = st.sb("mask", [S, S2])
            mx = st.sb("mx", [S, H])
            sm = st.sb("sm", [S, H])
            pT = st.sb("pT", [CP, 4, CH, S])
            on = st.sb("on", [S, 2, 512])
            s = st.sems_of("first_mask", "mask_loaded", "ahead_loaded", "ahead_split", "begun", "q_placed", "oT_lo", "seen", "s_ready", "shifted", "exps", "turned", "pT_a", "pT_d",
                                                      "o_ready", "chain", "o_norm", "oT_ready", "oT_kept")
            with nc.Block() as block:
                @block.sync
                def _(sp):
                    by_row = self.a["mask"].rearrange("b i j -> i b j")
                    sp.dma_start(masks[:, 0:1, :], by_row[:, 0:1, :]).then_inc(s["first_mask"], 16)
                    sp.dma_start(masks[:, 1:B, :], by_row[:, 1:B, :]).then_inc(s["mask_loaded"], 16)
                    self.ahead_load(sp, s, self.a["L1_wo"])

                @block.gpsimd
                def _(pool):
                    def replace(b, n):
                        pool.wait_ge(s["s_ready"], H * b + (8 * n + 8))
                        pool.sem_inc(s["begun"], 1)
                        self.place_queries(pool, s, n, b + 1, 8 * b + (8 + 4 * n), s["begun"])

                    def low(b, n):
                        at = (slice(None), slice(4 * n, 4 * n + 4), bass.ds(b * S, S))
                        pool.wait_ge(s["oT_kept"], 2 * (2 * b + n) + 3)
                        nc.gpsimd.tensor_tensor(oT[1][at], qoT[at], oT[0][at].bitcast(F32), ALU.subtract).then_inc(s["oT_lo"], 1)

                    pool.sem_inc(s["q_placed"], 8)
                    self.ahead_split(pool, s)
                    replace(0, 0)
                    low(0, 0)
                    replace(0, 1)
                    with pool.Fori(0, B - 2) as m:
                        low(m, 1)
                        replace(m + 1, 0)
                        low(m + 1, 0)
                        replace(m + 1, 1)
                    low(B - 2, 1)
                    low(B - 1, 0)
                    low(B - 1, 1)

                @block.scalar
                def _(act):
                    act.sem_inc(s["oT_kept"], 1)

                    def keep(b, n):
                        act.wait_ge(s["oT_ready"], 2 * b + n + 1)
                        for to in (oT[0], qoT):
                            nc.scalar.activation(to[:, 4 * n:4 * n + 4, bass.ds(b * S, S)],
                                                 ps[7][:, 0:4 * S].rearrange("p (a b) -> p a b", b=S), ACT.Copy).then_inc(s["oT_kept"], 1)

                    def body(i, last):
                        def exp(h):
                            act.wait_ge(s["shifted"], H * i + h + 1)
                            nc.scalar.activation(p[:, h % 4], p[:, h % 4], ACT.Exp, bias=mx[:, h:h + 1], scale=-1.0,
                                                 accum_out=sm[:, h:h + 1]).then_inc(s["exps"], 1)

                        exp(0)
                        for h in range(H):
                            if h + 1 < H:
                                exp(h + 1)
                            if h % 2 == 0:
                                act.wait_ge(s["turned"], H * i + h + 1)
                                nc.scalar.activation(pT[:, h % 4], ps[3 + h % 2][0:CP, 0:CH * S].rearrange("p (c i) -> p c i", i=S), ACT.Copy).then_inc(s["pT_a"], 1)
                            if h == 4 and last is not None:
                                keep(last, 1)
                            if h == 11:
                                keep(i, 0)

                    body(0, None)
                    with act.Fori(0, B - 1) as m:
                        body(m + 1, m)
                    keep(B - 1, 1)

                @block.vector
                def _(dve):
                    c = Chain(dve, s["chain"])
                    dve.wait_ge(s["first_mask"], 16)

                    def norm(b, n):
                        dve.wait_ge(s["o_ready"], 2 * b + n + 1)
                        c.link(nc.vector.reciprocal(sm[:, 8 * n:8 * n + 8], sm[:, 8 * n:8 * n + 8]))
                        nc.vector.tensor_tensor(on[:, n].rearrange("p (h d) -> p h d", d=DH), ps[5 + n][0:S, :].rearrange("p (h d) -> p h d", d=DH),
                                                sm[:, 8 * n:8 * n + 8].unsqueeze(2).to_broadcast([S, 8, DH]), ALU.mult).then_inc(s["o_norm"], 1)

                    def body(i, last):
                        def shift(h):
                            dve.wait_ge(s["s_ready"], H * i + h + 1)
                            dve.sem_inc(s["seen"], 1)
                            nc.vector.tensor_tensor_reduce(out=p[:, h % 4], in0=ps[h % 3][0:S, 0:S2], in1=mask[:, :],
                                                           scale=-1.0, scalar=3.0e38, op0=ALU.add, op1=ALU.min, accum_out=mx[:, h:h + 1]).then_inc(s["shifted"], 1)

                        c.link(nc.vector.tensor_copy(mask[:, :].unsqueeze(1), masks[:, bass.ds(i, 1), :]))
                        shift(0)
                        shift(1)
                        for h in range(H):
                            if h + 2 < H:
                                shift(h + 2)
                            if h % 2:
                                dve.wait_ge(s["turned"], H * i + h + 1)
                                nc.vector.tensor_copy(pT[:, h % 4], ps[3 + h % 2][0:CP, 0:CH * S].rearrange("p (c i) -> p c i", i=S)).then_inc(s["pT_d"], 1)
                            if h == 1 and last is not None:
                                norm(last, 1)
                            if h == 9:
                                norm(i, 0)

                    body(0, None)
                    dve.wait_ge(s["mask_loaded"], 16)
                    with dve.Fori(0, B - 1) as m:
                        c.enter(m, 3)
                        body(m + 1, m)
                        c.leave(B - 1)
                    norm(B - 1, 1)

                @block.tensor
                def _(pe):
                    def back(b, n):
                        pe.wait_ge(s["o_norm"], 2 * b + n + 1)
                        pe.wait_ge(s["oT_kept"], 2 * (2 * b + n) + 1)
                        for m in range(4):
                            last = nc.tensor.transpose(ps[7][:, m * S:(m + 1) * S], on[:, n, tile(m)], self.ident[0:S, 0:S])
                        last.then_inc(s["oT_ready"], 1)

                    def body(i, before):
                        def score(h):
                            if h % 8 == 0:
                                pe.wait_ge(s["q_placed"], 8 * i + (h // 2 + 4))
                            for part in range(2):
                                last = nc.tensor.matmul(ps[h % 3][0:S, 0:S2E], qz[:, h, :], self.k1T[part][:, bass.ds(i * S2E, S2E)],
                                                        start=part == 0, stop=part == 1)
                            last.then_inc(s["s_ready"], 1)

                        def turn(h):
                            pe.wait_ge(s["exps"], H * i + h + 1)
                            for m in range(CH):
                                last = nc.tensor.transpose(ps[3 + h % 2][0:CP, m * S:(m + 1) * S], p[:, h % 4, m * CP:(m + 1) * CP], self.ident[0:S, 0:S])
                            last.then_inc(s["turned"], 1)

                        def mix(h):
                            if h % 2:
                                pe.wait_ge(s["pT_d"], 8 * i + h // 2 + 1)
                            else:
                                pe.wait_ge(s["pT_a"], 8 * i + h // 2 + 1)
                            for m in range(CH):
                                last = nc.tensor.matmul(ps[5 + h // 8][0:S, (h % 8) * DH:(h % 8 + 1) * DH], pT[:, h % 4, m, :],
                                                        self.v1[:, bass.ds(i * CH + m, 1), :].rearrange("p o d -> p (o d)"), start=m == 0, stop=m == CH - 1)
                            if h % 8 == 7:
                                last.then_inc(s["o_ready"], 1)

                        score(0)
                        score(1)
                        for h in range(H):
                            if h + 2 < H:
                                score(h + 2)
                            turn(h)
                            if h:
                                mix(h - 1)
                            if h == 3 and before is not None:
                                back(before, 1)
                            if h == 11:
                                back(i, 0)
                        mix(H - 1)

                    body(0, None)
                    with pe.Fori(0, B - 1) as m:
                        body(m + 1, m)
                    back(B - 1, 1)

    def multi_output(self):
        nc, ps, X = self.nc, self.ps, self.X
        with Stage(nc, "eo") as st:
            s = st.sems_of("y_ready", "x_added")
            with nc.Block() as block:
                @block.vector
                def _(dve):
                    for t in range(NT):
                        dve.wait_ge(s["y_ready"], t + 1)
                        nc.vector.tensor_tensor(X[:, t], X[:, t], ps[t][:, 0:D], ALU.add).then_inc(s["x_added"], 1)

                @block.tensor
                def _(pe):
                    self.project(pe, self.oT, self.ahead_as(a=HP), s["y_ready"])

    def l1_experts(self):
        nc, a, ps, X = self.nc, self.a, self.ps, self.X
        E = 8
        W1 = KT * INNER
        with Stage(nc, "f") as st:
            xT = st.pair("xT", [P, KT, N])
            xn = st.sb("xn", [P, NT, D])
            raw1 = st.sb("raw1", [P, W1 + 8])
            raw2 = st.sb("raw2", [P, 8 * D])
            w1 = st.pair("w1", [P, W1])
            w2 = st.pair("w2", [P, 8, D])
            b1 = st.sb("b1", [P, 8])
            b2 = st.sb("b2", [E, D])
            graw = st.sb("graw", [P, KT, E])
            gw = st.pair("gw", [P, KT, E])
            gbias = st.sb("gbias", [P, E])
            temp = st.sb("temp", [P, 1])
            lt = st.sb("lt", [P, 16, 16])
            logit = st.sb("logit", [P, NT, E])
            more = st.sb("more", [P, NT, E, E])
            same = st.sb("same", [P, NT, E, E])
            rank = st.sb("rank", [P, NT, E])
            top = st.sb("top", [P, NT])
            share = st.sb("share", [P, NT, E])
            shareT = st.sb("shareT", [E, N])
            col = st.sb("col", [P, NT])
            plain = st.sb("plain", [P, 2, HALF])
            hid = st.pair("hid", [P, 8, N])
            ln = self.ln_buffers(st)
            f = self.ffn_sems(st, "ffn")
            s = st.sems_of("c_loaded", "loaded1", "loaded2", "split1", "split2", "b1_kept", "begun", "g_split", "logit",
                                                      "shifted", "exps", "chain", "shared", "sh_turned", "sh_kept", "bias_ready", "bias_added")
            with nc.Block() as block:
                @block.sync
                def _(sp):
                    sp.dma_start(raw1[:, :], a["L1_e1"][0]).then_inc(s["loaded1"], 16)
                    sp.dma_start(graw[:, :, :], a["L1_gate"]).then_inc(s["c_loaded"], 16)
                    sp.dma_start(gbias[:, :], a["L1_ffn_gate_b"].partition_broadcast(P)).then_inc(s["c_loaded"], 16)
                    sp.dma_start(temp[:, :], a["temperature"].partition_broadcast(P)).then_inc(s["c_loaded"], 16)
                    sp.dma_start(lt[:, :, :], a["lower"].partition_broadcast(P)).then_inc(s["c_loaded"], 16)
                    sp.dma_start(b2[:, :], a["L1_ffn_b2"]).then_inc(s["c_loaded"], 16)
                    sp.dma_start(raw2[:, :], a["L1_e2"][0]).then_inc(s["loaded2"], 16)
                    with sp.Fori(0, E - 1) as i:
                        sp.wait_ge(s["b1_kept"], i + 1)
                        sp.dma_start(raw1[:, :], a["L1_e1"][bass.ds(i + 1, 1)].rearrange("o p w -> (o p) w")).then_inc(s["loaded1"], 16)
                        sp.wait_ge(s["split2"], 2 * i + 2)
                        sp.dma_start(raw2[:, :], a["L1_e2"][bass.ds(i + 1, 1)].rearrange("o p w -> (o p) w")).then_inc(s["loaded2"], 16)

                @block.gpsimd
                def _(pool):
                    pool.wait_ge(s["c_loaded"], 80)
                    self.split_pool(pool, s["g_split"], graw[:, :, :], cut(gw, slice(None)), 0)

                    def first(e):
                        pool.wait_ge(s["loaded1"], 16 * e + 16)
                        pool.sem_inc(s["begun"], 1)
                        self.split_pool(pool, s["split1"], raw1[:, 0:W1], cut(w1, slice(None)), e)
                        nc.gpsimd.tensor_copy(b1[:, :], raw1[:, W1:W1 + 8]).then_inc(s["b1_kept"], 1)

                    def second(e):
                        pool.wait_ge(s["loaded2"], 16 * e + 16)
                        pool.sem_inc(s["begun"], 1)
                        self.split_pool(pool, s["split2"], raw2[:, :], tuple(x[:, :, :].rearrange("p a b -> p (a b)") for x in w2), e)

                    pool.wait_ge(s["split1"], 1)
                    nc.gpsimd.tensor_tensor(w1[1][:, :], raw1[:, 0:W1], w1[0][:, :].bitcast(F32), ALU.subtract).then_inc(s["split1"], 1)
                    nc.gpsimd.tensor_copy(b1[:, :], raw1[:, W1:W1 + 8]).then_inc(s["b1_kept"], 1)
                    second(0)
                    with pool.Fori(0, E - 1) as i:
                        pool.wait_ge(f["plain_done"], 16 * i + 16)
                        first(i + 1)
                        pool.wait_ge(f["y_ready"], NT * i + NT)
                        second(i + 1)

                @block.scalar
                def _(act):
                    self.ln_scalar_sqrt(act, ln)
                    self.split_scalar(act, ln, xT)
                    act.wait_ge(s["loaded1"], 16)
                    nc.scalar.activation(w1[0][:, :], raw1[:, 0:W1], ACT.Copy).then_inc(s["split1"], 1)
                    act.wait_ge(s["shifted"], 1)
                    nc.scalar.activation(logit[:, :, :], logit[:, :, :], ACT.Exp).then_inc(s["exps"], 1)
                    with act.Fori(0, E) as i:
                        act.wait_ge(s["b1_kept"], i + 1)
                        self.ffn_scalar(act, f, i, ACT.Gelu, plain, None, b1)
                    for g in range(2):
                        act.wait_ge(s["sh_turned"], g + 1)
                        n = min(512, N - 512 * g)
                        nc.scalar.activation(shareT[:, 512 * g:512 * g + n], ps[g][0:E, 0:n], ACT.Copy).then_inc(s["sh_kept"], 1)

                @block.vector
                def _(dve):
                    dve.sem_inc(f["y_used"], 1)
                    self.ln_vector(dve, ln, X, xn)
                    self.split_vector(dve, ln, xT)
                    c = Chain(dve, s["chain"])
                    dve.wait_ge(s["c_loaded"], 80)
                    dve.wait_ge(s["logit"], 1)
                    c.link(nc.vector.tensor_tensor(logit[:, :, :], ps[0][:, 0:NT * E].rearrange("p (t e) -> p t e", e=E),
                                                   gbias[:, :].unsqueeze(1).to_broadcast([P, NT, E]), ALU.add))
                    c.link(nc.vector.reciprocal(temp[:, :], temp[:, :]))
                    c.link(nc.vector.tensor_scalar(logit[:, :, :], logit[:, :, :], temp[:, 0:1], None, ALU.mult))
                    self.rank(dve, c, logit[:, :, :], lt, E, more, same, rank[:, :, :])
                    c.link(nc.vector.tensor_reduce(top[:, :], logit[:, :, :], AX, ALU.max))
                    nc.vector.tensor_tensor(logit[:, :, :], logit[:, :, :], top[:, :].unsqueeze(2).to_broadcast([P, NT, E]), ALU.subtract).then_inc(s["shifted"], 1)
                    dve.wait_ge(s["exps"], 1)
                    c.link(nc.vector.tensor_scalar(rank[:, :, :], rank[:, :, :], 2.0, None, ALU.is_lt))
                    c.link(nc.vector.tensor_tensor(share[:, :, :], rank[:, :, :], logit[:, :, :], ALU.mult))
                    c.link(nc.vector.tensor_reduce(top[:, :], share[:, :, :], AX, ALU.add))
                    c.link(nc.vector.reciprocal(top[:, :], top[:, :]))
                    nc.vector.tensor_tensor(share[:, :, :], share[:, :, :], top[:, :].unsqueeze(2).to_broadcast([P, NT, E]), ALU.mult).then_inc(s["shared"], 1)
                    dve.wait_ge(s["shared"], 1)
                    with dve.Fori(0, E) as i:
                        c.enter(i, 1)
                        dve.wait_ge(f["y_used"], NT * i + 1)
                        c.link(nc.vector.tensor_copy(col[:, :].unsqueeze(2), share[:, :, bass.ds(i, 1)]))
                        self.ffn_vector(dve, f, i, plain, None, hid)
                        for t in range(NT):
                            dve.wait_ge(f["y_ready"], NT * i + t + 1)
                            dve.wait_ge(f["y_used"], NT * i + 1)
                            nc.vector.scalar_tensor_tensor(out=X[:, t], in0=ps[4 + t % 4][:, 0:D], scalar=col[:, t:t + 1], in1=X[:, t],
                                                           op0=ALU.mult, op1=ALU.add).then_inc(f["y_used"], 1)
                        c.leave(E)
                    dve.wait_ge(f["y_used"], NT * E + 1)
                    for t in range(NT):
                        dve.wait_ge(s["bias_ready"], t + 1)
                        nc.vector.tensor_tensor(X[:, t], X[:, t], ps[2 + t % 4][:, 0:D], ALU.add).then_inc(s["bias_added"], 1)

                @block.tensor
                def _(pe):
                    self.turn_tensor(pe, ln, xn)
                    pe.wait_ge(s["g_split"], 2)
                    self.logits(pe, ln, xT, gw, E, s["logit"])
                    pe.wait_ge(s["chain"], 1)
                    with pe.Fori(0, E) as i:
                        pe.wait_ge(s["split1"], 2 * i + 2)
                        self.ffn_tensor(pe, f, i, xT, lambda n, k, ft: cut(w1, slice(None), slice(k * INNER + ft * P, k * INNER + (ft + 1) * P)),
                                        False, hid, w2, lambda: pe.wait_ge(s["split2"], 2 * i + 2))
                    pe.wait_ge(s["shared"], 1)
                    for t in range(NT):
                        last = nc.tensor.transpose(ps[t // 4][0:E, tile(t % 4)], share[:, t, :], self.ident[:, :])
                        if t in (3, NT - 1):
                            last.then_inc(s["sh_turned"], 1)
                    pe.wait_ge(s["sh_kept"], 2)
                    for t in range(NT):
                        if t in (2, 3):
                            pe.wait_ge(f["y_used"], NT * E + 1)
                        if t >= 4:
                            pe.wait_ge(s["bias_added"], t - 3)
                        nc.tensor.matmul(ps[2 + t % 4][:, 0:D], shareT[:, tile(t)], b2[:, :], start=True, stop=True).then_inc(s["bias_ready"], 1)


STOP = 6


def _pos_enc():
    position = np.arange(S, dtype=np.float32)[:, None]
    div = np.exp(np.arange(0, DH, 2, dtype=np.float32) * np.float32(-(np.log(10000.0) / DH)))
    pe = np.zeros((S, DH), np.float32)
    pe[:, 0::2] = np.sin(position * div)
    pe[:, 1::2] = np.cos(position * div)
    return np.ascontiguousarray(np.concatenate([pe.T, pe.T], 0))


def _ktiles(w):
    return w.reshape(-1, P, w.shape[-1]).transpose(1, 0, 2)


def kernel(**inputs):
    import concourse.bacc as bacc
    from concourse.bass_utils import run_bass_kernel_spmd

    i = {k: np.asarray(v) for k, v in inputs.items()}
    wqkv = i["L0_attn_W_qkv"].reshape(KT, P, 3, HP, P).transpose(3, 1, 0, 2, 4).reshape(HP, P, KT * 3 * P)
    bqkv = i["L0_attn_b_qkv"].reshape(3, HP, P)
    arrays = {
        "x": i["x"].reshape(N, D),
        "L0_qkv": np.concatenate([wqkv, bqkv.transpose(1, 2, 0)], 2),
        "L0_attn_b_out": i["L0_attn_b_out"],
        "L0_wo": _ktiles(i["L0_attn_W_out"]),
        "pos": _pos_enc(),
    }
    def gs(g, b):
        return np.stack([i[g].reshape(KT, P).T, i[b].reshape(KT, P).T], 1)

    experts = np.concatenate([
        np.stack([i["L0_ffn_sw_gate"].reshape(KT, P, 2, P).transpose(2, 1, 0, 3), i["L0_ffn_sw_up"].reshape(KT, P, 2, P).transpose(2, 1, 0, 3)], 3),
        np.stack([i["L0_ffn_w_gate"].reshape(16, KT, P, P).transpose(0, 2, 1, 3), i["L0_ffn_w_up"].reshape(16, KT, P, P).transpose(0, 2, 1, 3)], 3),
    ], 0).reshape(18, P, 4 * P)
    down = np.concatenate([i["L0_ffn_sw_down"].reshape(2, P, D), i["L0_ffn_w_down"]], 0)
    arrays.update({
        "ctx": i["ctx_1024"].reshape(B, CH, CP, D).transpose(0, 2, 1, 3),
        "mask": i["mask_BxSxS2_ff0"],
        "L0_ln1": gs("L0_xattn_ln1_g", "L0_xattn_ln1_b"),
        "L0_ln2": gs("L0_xattn_ln2_g", "L0_xattn_ln2_b"),
        "L1_cln": gs("L1_xattn_cln_g", "L1_xattn_cln_b"),
        "L1_ln": gs("L1_xattn_ln_g", "L1_xattn_ln_b"),
        "L0_wq": _ktiles(i["L0_xattn_wq"]), "L0_wk": _ktiles(i["L0_xattn_wk"]), "L0_wv": _ktiles(i["L0_xattn_wv"]),
        "L0_xwo": _ktiles(i["L0_xattn_wo"]).reshape(P, -1), "L0_w1": _ktiles(i["L0_xattn_w1"]).reshape(P, -1),
        "L0_w2": _ktiles(i["L0_xattn_w2"]).reshape(P, -1),
        "L0_b1": i["L0_xattn_b1"].reshape(8, P).T, "L0_xattn_bo": i["L0_xattn_bo"], "L0_xattn_b2": i["L0_xattn_b2"],
        "L1_wkv": _ktiles(np.concatenate([i["L1_xattn_Wkv"][:, :DH], i["L1_xattn_Wkv"]], 1)),
        "L0_gate": _ktiles(i["L0_ffn_gate_kernel"]), "L0_ffn_gate_bias": i["L0_ffn_gate_bias"],
        "L0_experts": np.concatenate([experts, down], 2),
        "lower": np.tril(np.ones((16, 16), np.float32), -1),
        "L1_wqv": _ktiles(np.concatenate([i["L1_attn_Wq"].T, i["L1_attn_Wv"].T], 1)),
        "L1_norm_w": np.stack([i["L1_attn_q_norm_w"].reshape(-1), i["L1_attn_v_norm_w"].reshape(-1)]),
        "own": np.repeat(np.where(np.arange(P)[:, None] // 16 == np.arange(8)[None, :], np.float32(1), np.float32(0))[:, :, None], S, 2),
        "causal": np.triu(np.ones((S, S), np.float32)),
        "L1_wq": _ktiles(i["L1_xattn_Wq"]),
        "L1_w1": _ktiles(i["L1_xattn_W1"]), "L1_w2": _ktiles(i["L1_xattn_W2"]).reshape(P, -1),
        "L1_wo": _ktiles(i["L1_xattn_Wout"]).reshape(P, -1),
        "L1_e1": np.concatenate([i["L1_ffn_W1"].reshape(8, KT, P, 1024).transpose(0, 2, 1, 3).reshape(8, P, -1),
                                 i["L1_ffn_b1"].reshape(8, 8, P).transpose(0, 2, 1)], 2),
        "L1_e2": i["L1_ffn_W2"].reshape(8, 8, P, D).transpose(0, 2, 1, 3).reshape(8, P, -1),
        "L1_gate": _ktiles(i["L1_ffn_gate_w"]), "L1_ffn_gate_b": i["L1_ffn_gate_b"], "L1_ffn_b2": i["L1_ffn_b2"],
        "temperature": i["L1_ffn_temperature"].reshape(1),
    })
    nc = bacc.Bacc("TRN2", target_bir_lowering=False, num_devices=1)
    arrays = {k: np.ascontiguousarray(v) for k, v in arrays.items()}
    aps = {k: nc.dram_tensor(k, v.shape, F32, kind="ExternalInput").ap() for k, v in arrays.items()}
    aps["spill"] = nc.dram_tensor("spill", (N, D), F32, kind="Internal").ap()
    aps["out"] = nc.dram_tensor("out", (N, D), F32, kind="ExternalOutput").ap()
    Kernel(nc, aps, STOP).build()
    r = run_bass_kernel_spmd(nc, [arrays], core_ids=[0])
    return r.results[0]["out"].reshape(B, S, D)
```
